# Optimizing a Trainium2 kernel written in Bass

```python
import numpy as np
import jax
import jax.numpy as jnp

def _softmax(x, axis=-1):
    return jax.nn.softmax(x, axis=axis)

def _gelu(x):
    return jax.nn.gelu(x, approximate=True)

def _silu(x):
    return jax.nn.silu(x)

def _sigmoid(x):
    return jax.nn.sigmoid(x)

def _layernorm(x, axis=-1, eps=1e-05):
    m = jnp.mean(x, axis=axis, keepdims=True)
    v = jnp.var(x, axis=axis, keepdims=True)
    return (x - m) / jnp.sqrt(v + eps)

def _scatter_add(tgt, idx, src, axis=0):
    return tgt.at[idx].add(src)

def _segment_sum(src, seg, n):
    return jax.ops.segment_sum(src, seg, n)
kernel_name = 'mk_flamingo_gated_d1_seqx_r4_9f9e9b'

def setup_inputs(seed: int=0):
    np.random.seed(seed)
    _w = jnp.asarray

    def _rec_inputs():
        import jax
        import jax.numpy as jnp
        _rk = jax.random.key(seed)
        x = -0.0002928 + 1 * jax.random.normal(jax.random.fold_in(_rk, 1), (4, 1024, 256), jnp.float32)
        _lenS = 1024 - jax.random.randint(jax.random.fold_in(_rk, 7), (4,), 0, max(1, 1024 // 4) + 1, jnp.int32)
        _lenS2 = 154 - jax.random.randint(jax.random.fold_in(_rk, 8), (4,), 0, max(1, 154 // 4) + 1, jnp.int32)
        _ctx_1024P = jax.random.normal(jax.random.fold_in(_rk, 11), (4, 16, 256), jnp.float32)
        _ctx_1024c = jax.random.dirichlet(jax.random.fold_in(_rk, 511), 0.3 * jnp.ones((16,), jnp.float32), (4, 154))
        _ctx_1024t = jnp.einsum('bsk,bkd->bsd', _ctx_1024c, _ctx_1024P)
        _ctx_1024t = _ctx_1024t * jax.lax.rsqrt(jnp.mean(jnp.square(_ctx_1024t)) + 1e-12) * 0.953939
        ctx_1024 = -1.39393e-06 + 0.999914 * (_ctx_1024t + 0.3 * jax.random.normal(jax.random.fold_in(_rk, 611), (4, 154, 256), jnp.float32))
        _g = jax.random.normal(jax.random.fold_in(_rk, 9001), (2, 1), jnp.float32)
        _g = jnp.sign(_g) * jnp.maximum(jnp.abs(_g), 1.0) + (_g == 0) * 1.0
        g_xattn = _g[0]
        g_ffn = _g[1]
        return (x, ctx_1024, g_xattn, g_ffn)
    x, ctx_1024, g_xattn, g_ffn = _rec_inputs()

    def _L0_xattn_setup():
        import jax, jax.numpy as jnp
        import numpy as np
        EMBED_DIM = 256
        NUM_HEADS = 16
        HEAD_DIM = EMBED_DIM // NUM_HEADS
        SCALE_BASE = EMBED_DIM

        def xpos_apply(x, downscale):
            L, D = (x.shape[1], x.shape[2])
            half = D // 2
            base = (jnp.arange(0, D, 2, dtype=jnp.float32) + 0.4 * D) / (1.4 * D)
            pos = jnp.arange(L, dtype=jnp.float32)
            scale = base[None, :] ** (pos[:, None] / SCALE_BASE)
            inv_freq = 1.0 / 10000.0 ** (jnp.arange(half, dtype=jnp.float32) / half)
            sinusoid = pos[:, None] * inv_freq[None, :]
            sin, cos = (jnp.sin(sinusoid), jnp.cos(sinusoid))
            if downscale:
                scale = 1.0 / scale
            sin_s = jnp.repeat(sin * scale, 2, axis=-1)
            cos_s = jnp.repeat(cos * scale, 2, axis=-1)
            x1, x2 = (x[..., ::2], x[..., 1::2])
            rot = jnp.stack([-x2, x1], axis=-1).reshape(x.shape)
            return x * cos_s + rot * sin_s
        key = jax.random.key(seed)
        ks = jax.random.split(key, 12)
        B, L, E = (2, 512, EMBED_DIM)
        s = 1.0 / np.sqrt(E)
        inp = {'query': jax.random.normal(ks[0], (B, L, E), jnp.float32), 'key': jax.random.normal(ks[1], (B, L, E), jnp.float32), 'value': jax.random.normal(ks[2], (B, L, E), jnp.float32), 'Wq': jax.random.normal(ks[3], (E, E), jnp.float32) * s, 'bq': jax.random.normal(ks[4], (E,), jnp.float32) * 0.01, 'Wk': jax.random.normal(ks[5], (E, E), jnp.float32) * s, 'bk': jax.random.normal(ks[6], (E,), jnp.float32) * 0.01, 'Wv': jax.random.normal(ks[7], (E, E), jnp.float32) * s, 'bv': jax.random.normal(ks[8], (E,), jnp.float32) * 0.01, 'Wo': jax.random.normal(ks[9], (E, E), jnp.float32) * s, 'bo': jax.random.normal(ks[10], (E,), jnp.float32) * 0.01}
        return inp
    _L0_xattn_all = _L0_xattn_setup()
    _L0_xattn_in = {k: v for k, v in _L0_xattn_all.items() if k in ('Wq', 'bq', 'Wk', 'bk', 'Wv', 'bv', 'Wo', 'bo')}
    del _L0_xattn_all

    def _L0_ffn_setup():
        import jax, jax.numpy as jnp
        import numpy as np
        B, S, D, H = (8, 256, 256, 1024)
        E, R = (3, 8)
        SCALING = 1.0 / R

        def _mole(x, W, b, A, Bm, Rw):
            gates = jax.nn.softmax(jnp.einsum('bsd,de->bse', x, Rw), axis=-1)
            base = jnp.einsum('bsd,dh->bsh', x, W) + b
            z = jnp.einsum('bsd,edr->ebsr', x, A)
            zg = z * jnp.transpose(gates, (2, 0, 1))[..., None]
            lora = jnp.einsum('ebsr,erh->bsh', zg, Bm)
            return base + SCALING * lora
        key = jax.random.key(seed)
        ks = jax.random.split(key, 12)
        s = lambda k, shape, scale: jax.random.normal(k, shape, dtype=jnp.float32) * scale
        return {'x': s(ks[0], (B, S, D), 1.0), 'W1': s(ks[1], (D, H), D ** (-0.5)), 'b1': jnp.zeros((H,), jnp.float32), 'A1': s(ks[2], (E, D, R), D ** (-0.5)), 'B1': s(ks[3], (E, R, H), 0.0) + s(ks[4], (E, R, H), R ** (-0.5)), 'R1': s(ks[5], (D, E), D ** (-0.5)), 'W2': s(ks[6], (H, D), H ** (-0.5)), 'b2': jnp.zeros((D,), jnp.float32), 'A2': s(ks[7], (E, H, R), H ** (-0.5)), 'B2': s(ks[8], (E, R, D), R ** (-0.5)), 'R2': s(ks[9], (H, E), H ** (-0.5))}
    _L0_ffn_all = _L0_ffn_setup()
    _L0_ffn_in = {k: v for k, v in _L0_ffn_all.items() if k in ('W1', 'b1', 'A1', 'B1', 'R1', 'W2', 'b2', 'A2', 'B2', 'R2')}
    del _L0_ffn_all
    return {'x': x, 'ctx_1024': ctx_1024, 'g_xattn': g_xattn, 'g_ffn': g_ffn, 'L0_xattn_Wq': _L0_xattn_in['Wq'], 'L0_xattn_bq': _L0_xattn_in['bq'], 'L0_xattn_Wk': _L0_xattn_in['Wk'], 'L0_xattn_bk': _L0_xattn_in['bk'], 'L0_xattn_Wv': _L0_xattn_in['Wv'], 'L0_xattn_bv': _L0_xattn_in['bv'], 'L0_xattn_Wo': _L0_xattn_in['Wo'], 'L0_xattn_bo': _L0_xattn_in['bo'], 'L0_ffn_W1': _L0_ffn_in['W1'], 'L0_ffn_b1': _L0_ffn_in['b1'], 'L0_ffn_A1': _L0_ffn_in['A1'], 'L0_ffn_B1': _L0_ffn_in['B1'], 'L0_ffn_R1': _L0_ffn_in['R1'], 'L0_ffn_W2': _L0_ffn_in['W2'], 'L0_ffn_b2': _L0_ffn_in['b2'], 'L0_ffn_A2': _L0_ffn_in['A2'], 'L0_ffn_B2': _L0_ffn_in['B2'], 'L0_ffn_R2': _L0_ffn_in['R2']}

def reference(x, ctx_1024, g_xattn, g_ffn, L0_xattn_Wq, L0_xattn_bq, L0_xattn_Wk, L0_xattn_bk, L0_xattn_Wv, L0_xattn_bv, L0_xattn_Wo, L0_xattn_bo, L0_ffn_W1, L0_ffn_b1, L0_ffn_A1, L0_ffn_B1, L0_ffn_R1, L0_ffn_W2, L0_ffn_b2, L0_ffn_A2, L0_ffn_B2, L0_ffn_R2):
    import jax
    import jax.numpy as jnp

    def _L0_xattn_ref(query, key, value, Wq, bq, Wk, bk, Wv, bv, Wo, bo):
        import jax, jax.numpy as jnp
        import numpy as np
        EMBED_DIM = 256
        NUM_HEADS = 16
        HEAD_DIM = EMBED_DIM // NUM_HEADS
        SCALE_BASE = EMBED_DIM

        def xpos_apply(x, downscale):
            L, D = (x.shape[1], x.shape[2])
            half = D // 2
            base = (jnp.arange(0, D, 2, dtype=jnp.float32) + 0.4 * D) / (1.4 * D)
            pos = jnp.arange(L, dtype=jnp.float32)
            scale = base[None, :] ** (pos[:, None] / SCALE_BASE)
            inv_freq = 1.0 / 10000.0 ** (jnp.arange(half, dtype=jnp.float32) / half)
            sinusoid = pos[:, None] * inv_freq[None, :]
            sin, cos = (jnp.sin(sinusoid), jnp.cos(sinusoid))
            if downscale:
                scale = 1.0 / scale
            sin_s = jnp.repeat(sin * scale, 2, axis=-1)
            cos_s = jnp.repeat(cos * scale, 2, axis=-1)
            x1, x2 = (x[..., ::2], x[..., 1::2])
            rot = jnp.stack([-x2, x1], axis=-1).reshape(x.shape)
            return x * cos_s + rot * sin_s
        B, T, E = query.shape
        S = key.shape[1]
        H, D = (NUM_HEADS, HEAD_DIM)
        scaling = D ** (-0.5)
        q = (query @ Wq.T + bq) * scaling
        k = key @ Wk.T + bk
        v = value @ Wv.T + bv

        def split_heads(x, L):
            return x.reshape(B, L, H, D).transpose(0, 2, 1, 3).reshape(B * H, L, D)
        q = split_heads(q, T)
        k = split_heads(k, S)
        v = split_heads(v, S)
        k = xpos_apply(k, downscale=True)
        q = xpos_apply(q, downscale=False)
        attn_weights = jnp.einsum('btd,bsd->bts', q, k)
        attn_weights = jax.nn.softmax(attn_weights.astype(jnp.float32), axis=-1).astype(q.dtype)
        attn = jnp.einsum('bts,bsd->btd', attn_weights, v)
        attn = attn.reshape(B, H, T, D).transpose(0, 2, 1, 3).reshape(B, T, E)
        return attn @ Wo.T + bo

    def _L0_ffn_ref(x, W1, b1, A1, B1, R1, W2, b2, A2, B2, R2):
        import jax, jax.numpy as jnp
        import numpy as np
        B, S, D, H = (8, 256, 256, 1024)
        E, R = (3, 8)
        SCALING = 1.0 / R

        def _mole(x, W, b, A, Bm, Rw):
            gates = jax.nn.softmax(jnp.einsum('bsd,de->bse', x, Rw), axis=-1)
            base = jnp.einsum('bsd,dh->bsh', x, W) + b
            z = jnp.einsum('bsd,edr->ebsr', x, A)
            zg = z * jnp.transpose(gates, (2, 0, 1))[..., None]
            lora = jnp.einsum('ebsr,erh->bsh', zg, Bm)
            return base + SCALING * lora
        h = _mole(x, W1, b1, A1, B1, R1)
        h = jax.nn.relu(h)
        return _mole(h, W2, b2, A2, B2, R2)
    x = x + jnp.tanh(g_xattn[0]) * _L0_xattn_ref(_layernorm(x, axis=-1), ctx_1024, ctx_1024, L0_xattn_Wq, L0_xattn_bq, L0_xattn_Wk, L0_xattn_bk, L0_xattn_Wv, L0_xattn_bv, L0_xattn_Wo, L0_xattn_bo)
    x = x + jnp.tanh(g_ffn[0]) * _L0_ffn_ref(_layernorm(x, axis=-1), L0_ffn_W1, L0_ffn_b1, L0_ffn_A1, L0_ffn_B1, L0_ffn_R1, L0_ffn_W2, L0_ffn_b2, L0_ffn_A2, L0_ffn_B2, L0_ffn_R2)
    return x

_drawn_inputs = setup_inputs


def setup_inputs(seed=0):
    import zlib

    import numpy as np

    out = dict(_drawn_inputs(seed))
    spreads = {'L0_ffn_b1': (0.0, 0.1), 'L0_ffn_b2': (0.0, 0.1)}
    factors = {'L0_xattn_bq': 64.0, 'L0_xattn_bk': 64.0, 'L0_xattn_bv': 8.0, 'L0_xattn_bo': 7.809}
    for name, (base, spread) in spreads.items():
        noise = np.random.default_rng([zlib.crc32(name.encode()), seed]).standard_normal(out[name].shape)
        drawn = base * np.exp(spread * noise) if base else spread * noise
        out[name] = jnp.asarray(drawn.astype(out[name].dtype))
    for name, factor in factors.items():
        out[name] = (out[name] * factor).astype(out[name].dtype)
    return out
```

```python
from contextlib import ExitStack

import numpy as np

import concourse.bass as bass
from concourse import mybir

F32 = mybir.dt.float32
F32R = mybir.dt.float32r
ACT = mybir.ActivationFunctionType
ALU = mybir.AluOpType
AX = mybir.AxisListType

B, T, E, S, H = 4, 1024, 256, 154, 16
D = E // H
HID, NE, R = 1024, 3, 8
P = 128
CH = 512
UB = T // CH
TT = CH // P
FT = E // P
HT = HID // P
NG = H // 2
NQ = H // 4
SR = S - P
ZC = 28
NL = NE * R
W2N = E + ZC
KS = 96
KA = KS + 2
LR = 96
EPS = 1e-5
DSEL = 16


class Count:

    def __init__(self, sem, per):
        self.sem, self.per = sem, per

    def at(self, n, k=None):
        return self.per * n + (self.per if k is None else k)


def build(nc, x, ctx_in, wq, wkv, wo, w1, w2, a1, lora, tables, out):
    with ExitStack() as stack:
        def sb(name, shape, dt=F32):
            return stack.enter_context(nc.sbuf_tensor(name, shape, dt))

        def count(name, per):
            return Count(stack.enter_context(nc.semaphore(name)), per)

        x_in = sb("x_in", [P, 2, TT, E])
        xn = sb("xn", [P, TT, E])
        xT_hi = sb("xT_hi", [P, FT, CH], F32R)
        xT_lo = sb("xT_lo", [P, FT, CH], F32R)
        split = sb("split", [P, TT * NG * KS], F32R)
        qs = split[:, :].rearrange("p (k g r) -> p k g r", k=TT, g=NG)
        ns = split[:, 0:NQ * 512].rearrange("p (g c r) -> p g c r", g=NQ, r=32)
        heads_t = sb("heads_t", [P, NQ, 16, 32])
        qT = sb("qT", [KA, NG, CH], F32R)
        max_t = sb("max_t", [P, TT, 2, NG], F32R)
        max_f = xT_lo[0:H, 0, :]
        probs = sb("probs", [P, 8, CH])
        probs_r = sb("probs_r", [P, NQ, CH])
        q_ev = probs[:, 0:2, :].rearrange("p a (k e) -> p (a k) e", e=E)
        q_rc = probs[:, 2:4, :].rearrange("p a (k e) -> p (a k) e", e=E)
        q_rs = probs[:, 4:6, :].rearrange("p a (k e) -> p (a k) e", e=E)
        ctxT = probs[:, 6, 0:2 * S].rearrange("p (f s) -> p f s", f=FT)
        k_ev = probs_r[:, 0, :].rearrange("p (a e) -> p a e", a=2)
        k_rc = probs_r[:, 1, :].rearrange("p (a e) -> p a e", a=2)
        k_rs = probs_r[:, 2, :].rearrange("p (a e) -> p a e", a=2)
        ctx_sb = probs_r[:, 3, :].rearrange("p (a e) -> p a e", a=2)
        x1 = sb("x1", [P, TT, E])
        zT = sb("zT", [LR, CH], F32R)
        h_hi = sb("h_hi", [P, HT, CH], F32R)
        h_lo = sb("h_lo", [P, HT, CH], F32R)
        oT = h_lo[:, 0:NQ, :]
        wq_hi, wq_lo = (sb(f"wq_{n}", [P, FT, E], F32R) for n in ("hi", "lo"))
        wkv_sb = sb("wkv_sb", [P, FT, 2 * E])
        wo_hi, wo_lo = (sb(f"wo_{n}", [P, NQ, E], F32R) for n in ("hi", "lo"))
        a1_hi, a1_lo = (sb(f"a1_{n}", [P, FT, ZC], F32R) for n in ("hi", "lo"))
        w1_hi, w1_lo = (sb(f"w1_{n}", [P, FT, HID], F32R) for n in ("hi", "lo"))
        w2_hi, w2_lo = (sb(f"w2_{n}", [P, HT, W2N], F32R) for n in ("hi", "lo"))
        lora_sb = sb("lora_sb", [LR, HID + E], F32R)
        km = sb("km", [KA, NG, 2, S], F32R)
        kr = sb("kr", [KA, NG, P], F32R)
        v_sb = sb("v_sb", [P, H, 32])
        vr_sb = sb("vr_sb", [P, NQ, P])
        ks = sb("ks", [P, 2, NG, KA], F32R)
        tab = sb("tab", [P, tables.shape[1]])
        ident = sb("ident", [P, P])
        ident_r = sb("ident_r", [P, P], F32R)
        ln_s = sb("ln_s", [P, 2, TT, 6])
        ln_m = sb("ln_m", [P, 2, TT, 2])
        ln_v = sb("ln_v", [P, 2, TT])
        ln_r = sb("ln_r", [P, 2, TT])
        half = sb("half", [P, TT])
        eps = sb("eps", [P, TT])
        pace = sb("pace", [P, 1])
        gate = sb("gate", [P, 2])
        den = sb("den", [P, NQ, 16])
        zc = sb("zc", [P, 1, TT, ZC])
        zmax = sb("zmax", [P, 1, TT])
        zsh = sb("zsh", [P, 1, TT, NE])
        zex = sb("zex", [P, 1, TT, NE])
        zsum = sb("zsum", [P, 1, TT])
        zrec = sb("zrec", [P, 1, TT])
        zw = sb("zw", [P, 1, TT, NE])
        zg = sb("zg", [P, 1, TT, NL])
        zs = sb("zs", [P, 1, TT, LR], F32R)

        o = 0

        def cols(n):
            nonlocal o
            o += n
            return tab[:, o - n:o]

        cos_q = cols(UB * TT * D).rearrange("p (u k d) -> p u k d", u=UB, k=TT)
        sin_q = cols(UB * TT * D).rearrange("p (u k d) -> p u k d", u=UB, k=TT)
        cos_k = cols(2 * D).rearrange("p (a d) -> p a d", a=2)
        sin_k = cols(2 * D).rearrange("p (a d) -> p a d", a=2)
        bq_b, bk_b, bv_b, bo_b = cols(E), cols(E), cols(E), cols(E)
        g_b, mask = cols(2), cols(2)

        psX = stack.enter_context(nc.psum_tensor("psX", [P, 4, CH], F32))
        psF = stack.enter_context(nc.psum_tensor("psF", [P, 3, CH], F32))
        psO = stack.enter_context(nc.psum_tensor("psO", [P, CH], F32))

        x_loaded = [count(f"x_loaded{u}", 16) for u in range(2)]
        ctx_loaded = count("ctx_loaded", 32)
        tab_loaded = count("tab_loaded", 16)
        wkv_loaded = count("wkv_loaded", 16)
        stage_loaded = count("stage_loaded", 16)
        stage_loaded2 = count("stage_loaded2", 16)
        stage_hi = count("stage_hi", 1)
        stage_lo = count("stage_lo", 1)
        const_p = count("const_p", 1)
        const_v = count("const_v", 1)
        gate_ready = count("gate_ready", 1)
        gbo_ready = count("gbo_ready", 1)
        ln1_stat, ln1_agg = count("ln1_stat", TT), count("ln1_agg", TT)
        ln1_eps, ln1_rstd, ln1_out = count("ln1_eps", 1), count("ln1_rstd", 1), count("ln1_out", TT)
        ln2_stat, ln2_agg = count("ln2_stat", TT), count("ln2_agg", TT)
        ln2_eps, ln2_rstd, ln2_out = count("ln2_eps", 1), count("ln2_rstd", 1), count("ln2_out", TT)
        xb_ready = count("xb_ready", 1)
        xT_ps, xT_hi_s, xT_lo_s = count("xT_ps", FT), count("xT_hi_s", FT), count("xT_lo_s", FT)
        x2T_ps, x2T_hi_s, x2T_lo_s = count("x2T_ps", FT), count("x2T_hi_s", FT), count("x2T_lo_s", FT)
        q_ps, q_evac = count("q_ps", 2), count("q_evac", 2)
        q_cos, q_sin, q_rot = count("q_cos", 1), count("q_sin", TT), count("q_rot", 1)
        q_hi, q_hi2, q_lo = count("q_hi", 1), count("q_hi2", 1), count("q_lo", 1)
        qT_ps, qT_a, qT_v = count("qT_ps", NG), count("qT_a", NG // 2), count("qT_v", NG // 2)
        max_ps, max_red = count("max_ps", TT * NG // 2), count("max_red", TT * NG // 2)
        maxT_ps, maxT_s, max_rows = count("maxT_ps", 1), count("maxT_s", 1), count("max_rows", 32)
        sc_ps, sc_exp = count("sc_ps", 10), count("sc_exp", 10)
        pv_ps, pv_t = count("pv_ps", NQ), count("pv_t", NQ)
        den_inv, o_norm = count("den_inv", 2), count("o_norm", 2)
        o_hi, o_lo, o_back = count("o_hi", 2), count("o_lo", 2), count("o_back", 2)
        oT_s = count("oT_s", 2)
        wo_ps, x1_s = count("wo_ps", 2), count("x1_s", 2)
        z1_ps, g1_v, g1_e = count("z1_ps", 1), count("g1_v", 9), count("g1_e", 1)
        z1T_ps, z1T_s = count("z1T_ps", 1), count("z1T_s", 1)
        w1_ps, w1_hi_s, w1_lo_s = count("w1_ps", HT), count("h_hi_s", HT), count("h_lo_s", HT)
        w2_ps = count("w2_ps", TT)
        g2_c, g2_v, g2_e = count("g2_c", TT), count("g2_v", 16), count("g2_e", 2)
        z2T_ps, z2T_s = count("z2T_ps", 2), count("z2T_s", 2)
        y_ps, y_out, stored = count("y_ps", TT), count("y_out", TT), count("stored", 16)
        ctxT_ps, ctxT_s = count("ctxT_ps", 1), count("ctxT_s", 1)
        kv_ps, kv_evac = count("kv_ps", 2), count("kv_evac", 2)
        v_evac = count("v_evac", 5)
        k_rot, k_split = count("k_rot", 4), count("k_split", 2)
        km_ps, km_v, km_a = count("km_ps", 3), count("km_v", 6), count("km_a", 2)

        x_d = x.rearrange("b (u p k) e -> b u p k e", u=UB, k=TT)
        out_d = out.rearrange("b (u p k) e -> b u p k e", u=UB, k=TT)

        st = heads_t[:, :, :, :].rearrange("p a b c -> p (a b c)")
        stl = x1[:, :, :].rearrange("p a b -> p (a b)")
        nwa = FT * E + NQ * E + FT * ZC

        block = stack.enter_context(nc.Block())

        @block.sync
        def _(sp):
            sp.dma_start(x_in[:, 0], x_d[0, 0]).then_inc(x_loaded[0].sem, 16)
            sp.dma_start(tab[:, :], tables).then_inc(tab_loaded.sem, 16)
            sp.dma_start(st[:, 0:FT * E], wq).then_inc(stage_loaded.sem, 16)
            sp.wait_ge(const_v.sem, 1)
            sp.dma_start(ctx_sb[:, 0, :], ctx_in[0, 0:P]).then_inc(ctx_loaded.sem, 16)
            sp.dma_start(ctx_sb[0:SR, 1, :], ctx_in[0, P:S]).then_inc(ctx_loaded.sem, 16)
            sp.dma_start(wkv_sb[:, :, :], wkv.rearrange("(f p) n -> p f n", p=P)).then_inc(wkv_loaded.sem, 16)
            sp.dma_start(x_in[:, 1], x_d[0, 1]).then_inc(x_loaded[1].sem, 16)
            sp.dma_start(stl[:, 0:NQ * E], wo).then_inc(stage_loaded2.sem, 16)
            sp.wait_ge(stage_lo.sem, 1)
            sp.dma_start(st[:, 0:FT * HID], w1).then_inc(stage_loaded.sem, 16)
            sp.wait_ge(stage_lo.sem, 2)
            sp.dma_start(stl[:, 0:W2N + FT * ZC], a1).then_inc(stage_loaded2.sem, 16)
            sp.wait_ge(stage_lo.sem, 3)
            sp.dma_start(st[:, 0:(HT - 1) * W2N], w2).then_inc(stage_loaded.sem, 16)
            def rows_of_maxima(c):
                sp.wait_ge(maxT_s.sem, maxT_s.at(c))
                for hh in range(2):
                    sp.dma_start(qT[KS + hh:KS + hh + 1, :, :].bitcast(F32),
                                 xT_lo[NG * hh:NG * hh + NG, 0, :].bitcast(F32)).then_inc(max_rows.sem, 16)

            def load(b, u):
                sp.dma_start(x_in[:, u], x_d[b, u]).then_inc(x_loaded[u].sem, 16)

            rows_of_maxima(0)
            sp.wait_ge(stage_lo.sem, 6)
            sp.dma_start(st[0:LR, 0:HID + E], lora).then_inc(stage_loaded.sem, 16)
            rows_of_maxima(1)
            load(1, 0)
            with sp.Fori(1, B - 1) as b:
                rows_of_maxima(2 * b)
                load(b, 1)
                rows_of_maxima(2 * b + 1)
                load(b + 1, 0)
            rows_of_maxima(2 * B - 2)
            load(B - 1, 1)
            rows_of_maxima(2 * B - 1)

        @block.gpsimd
        def _(pool):
            nc.gpsimd.memset(ident[:, :], 0.0).then_inc(const_p.sem, 1)
            pool.wait_ge(const_p.sem, 1)
            nc.gpsimd.affine_select(out=ident[:, :], in_=ident[:, :], compare_op=ALU.not_equal, fill=1.0,
                                    base=0, pattern=[[-1, P]], channel_multiplier=1).then_inc(const_p.sem, 1)
            nc.gpsimd.memset(half[:, :], -0.5).then_inc(const_p.sem, 1)
            nc.gpsimd.memset(eps[:, :], EPS)
            nc.gpsimd.memset(zs[:, :, :, :].bitcast(F32), 0.0).then_inc(const_p.sem, 1)
            pool.wait_ge(const_p.sem, 4)
            nc.gpsimd.memset(zs[:, :, :, NL:NL + 1].bitcast(F32), 1.0)
            nc.gpsimd.memset(zs[:, :, :, 64 + NL:65 + NL].bitcast(F32), 1.0).then_inc(const_p.sem, 1)

            def rstd(which, agg, eps_s, out_s, c):
                pool.wait_ge(agg.sem, agg.at(c))
                nc.gpsimd.tensor_tensor(ln_v[:, which, :], ln_m[:, which, :, 1], eps[:, :],
                                        ALU.add).then_inc(eps_s.sem, 1)
                pool.wait_ge(eps_s.sem, eps_s.at(c))
                nc.gpsimd.tensor_tensor(ln_r[:, which, :], ln_v[:, which, :], half[:, :],
                                        ALU.pow).then_inc(out_s.sem, 1)

            def residual_base(c, u):
                pool.wait_ge(ln1_out.sem, ln1_out.at(c))
                for k in range(TT):
                    ins = nc.gpsimd.tensor_tensor(x_in[:, u, k], x_in[:, u, k], bo_b, ALU.add)
                ins.then_inc(xb_ready.sem, 1)

            def step(c, u, first=False, last=False):
                if not first:
                    rstd(1, ln2_agg, ln2_eps, ln2_rstd, c - 1)
                pool.wait_ge(q_evac.sem, q_evac.at(c))
                nc.gpsimd.tensor_tensor(
                    q_rc.rearrange("p k (h d) -> p k h d", d=D), q_ev.rearrange("p k (h d) -> p k h d", d=D),
                    cos_q[:, u].unsqueeze(2).to_broadcast([P, TT, H, D]), ALU.mult).then_inc(q_cos.sem, 1)
                pool.wait_ge(q_hi.sem, q_hi.at(c))
                nc.gpsimd.tensor_tensor(
                    qs[:, :, :, 32:64].rearrange("p k g r -> p (k g) r"),
                    q_rc.rearrange("p k (g r) -> p (k g) r", r=32),
                    qs[:, :, :, 0:32].rearrange("p k g r -> p (k g) r").bitcast(F32),
                    ALU.subtract).then_inc(q_lo.sem, 1)
                if not last:
                    rstd(0, ln1_agg, ln1_eps, ln1_rstd, c + 1)
                    residual_base(c + 1, 1 - u)

            rstd(0, ln1_agg, ln1_eps, ln1_rstd, 0)
            pool.wait_ge(gbo_ready.sem, 1)
            residual_base(0, 0)
            step(0, 0, first=True)
            step(1, 1)
            with pool.Fori(1, B - 1) as b:
                step(2 * b, 0)
                step(2 * b + 1, 1)
            step(2 * B - 2, 0)
            step(2 * B - 1, 1, last=True)
            rstd(1, ln2_agg, ln2_eps, ln2_rstd, 2 * B - 1)

        @block.scalar
        def _(act):
            def copy(out_ap, in_ap, **kw):
                return nc.scalar.activation(out_ap, in_ap, ACT.Copy, **kw)

            def stage(src, hi):
                copy(hi, src).then_inc(stage_hi.sem, 1)

            def norm_hi(c, f2):
                act.wait_ge(o_norm.sem, o_norm.at(c, f2 + 1))
                copy(ns[:, 2 * f2:2 * f2 + 2, :, 0:D].rearrange("p g c d -> p (g c) d"),
                     heads_t[:, 2 * f2:2 * f2 + 2, :, 0:D].rearrange("p g c d -> p (g c) d")).then_inc(o_hi.sem, 1)

            def heads_back(c, f2):
                act.wait_ge(o_back.sem, o_back.at(c, f2 + 1))
                copy(oT[:, 2 * f2:2 * f2 + 2, :], heads_t[:, 2 * f2:2 * f2 + 2, :, :]
                     .rearrange("p g c r -> p g (c r)")).then_inc(oT_s.sem, 1)

            def store(b, u, c):
                act.wait_ge(y_out.sem, y_out.at(c))
                act.dma_start(out_d[b, u], x1[:, :, :]).then_inc(stored.sem, 16)

            def load_ctx(b, c):
                act.wait_ge(pv_ps.sem, pv_ps.at(c))
                act.dma_start(ctx_sb[:, 0, :], ctx_in[b, 0:P]).then_inc(ctx_loaded.sem, 16)
                act.dma_start(ctx_sb[0:SR, 1, :], ctx_in[b, P:S]).then_inc(ctx_loaded.sem, 16)

            def relu(d, m):
                act.wait_ge(w1_ps.sem, w1_ps.at(d, m + 1))
                nc.scalar.activation(h_hi[:, m, :], psF[:, m % 3, :], ACT.Relu).then_inc(w1_hi_s.sem, 1)

            def step(b, u, first=False, last=False):
                c = 2 * b + u
                d = c - 1
                for f in range(FT):
                    act.wait_ge(xT_ps.sem, xT_ps.at(c, f + 1))
                    copy(xT_hi[:, f, :], psX[:, f, :]).then_inc(xT_hi_s.sem, 1)
                if u == 0:
                    act.wait_ge(ctxT_ps.sem, ctxT_ps.at(b))
                    copy(ctxT, psO[:, 0:2 * S].rearrange("p (f s) -> p f s", f=FT)).then_inc(ctxT_s.sem, 1)
                if not first:
                    for f in range(FT):
                        act.wait_ge(x2T_ps.sem, x2T_ps.at(d, f + 1))
                        copy(xT_hi[:, f, :], psX[:, 2 + f, :]).then_inc(x2T_hi_s.sem, 1)
                act.wait_ge(q_rot.sem, q_rot.at(c))
                copy(split[:, :].rearrange("p (a r) -> p a r", r=KS)[:, :, 0:32],
                     q_rc.rearrange("p k (g r) -> p (k g) r", r=32)).then_inc(q_hi.sem, 1)
                copy(split[:, :].rearrange("p (a r) -> p a r", r=KS)[:, :, 64:96],
                     q_rc.rearrange("p k (g r) -> p (k g) r", r=32)).then_inc(q_hi2.sem, 1)
                if not first:
                    act.wait_ge(g1_v.sem, g1_v.at(d, 3))
                    nc.scalar.activation(zex[:, 0], zsh[:, 0], ACT.Exp).then_inc(g1_e.sem, 1)
                    act.wait_ge(z1T_ps.sem, z1T_ps.at(d))
                    copy(zT[:, :], psO[0:LR, :]).then_inc(z1T_s.sem, 1)
                    for m in range(3):
                        relu(d, m)
                if u == 0:
                    act.wait_ge(km_ps.sem, km_ps.at(b, 2))
                    for hh in range(2):
                        copy(km[:, 4:8, hh, 0:P], psX[0:KA, 1, :].rearrange("p (g s) -> p g s", g=4),
                             scale=mask[0:KA, hh:hh + 1]).then_inc(km_a.sem, 1)
                for g in range(0, NG, 2):
                    act.wait_ge(qT_ps.sem, qT_ps.at(c, g + 1))
                    copy(qT[0:KS, g, :], psX[0:KS, g % 4, :]).then_inc(qT_a.sem, 1)
                    if not first and 3 + g // 2 < HT:
                        relu(d, 3 + g // 2)
                if not first:
                    relu(d, 7)
                    for pr in range(2):
                        if pr == 1:
                            act.wait_ge(maxT_ps.sem, maxT_ps.at(c))
                            copy(max_f, psO[0:H, :], scale=-1.0).then_inc(maxT_s.sem, 1)
                        act.wait_ge(g2_v.sem, g2_v.at(d, 8 * pr + 2))
                        nc.scalar.activation(zex[:, 0, 2 * pr:2 * pr + 2], zsh[:, 0, 2 * pr:2 * pr + 2],
                                             ACT.Exp).then_inc(g2_e.sem, 1)
                        act.wait_ge(z2T_ps.sem, z2T_ps.at(d, pr + 1))
                        copy(zT[:, 256 * pr:256 * pr + 256], psO[0:LR, 0:256]).then_inc(z2T_s.sem, 1)
                else:
                    act.wait_ge(stage_loaded.sem, 32)
                    stage(st[:, 0:FT * HID], w1_hi[:, :, :].rearrange("p f n -> p (f n)"))
                    act.wait_ge(maxT_ps.sem, maxT_ps.at(c))
                    copy(max_f, psO[0:H, :], scale=-1.0).then_inc(maxT_s.sem, 1)
                exponentials(c, b, u, first, last)

            def stage_late(n):
                if n == 0:
                    act.wait_ge(stage_loaded2.sem, 32)
                    stage(stl[:, 0:W2N], w2_hi[:, HT - 1, :])
                    stage(stl[:, W2N:W2N + FT * ZC], a1_hi[:, :, :].rearrange("p f n -> p (f n)"))
                if n == 1:
                    act.wait_ge(stage_loaded.sem, 48)
                    stage(st[:, 0:(HT - 1) * W2N], w2_hi[:, 0:HT - 1, :].rearrange("p m n -> p (m n)"))
                if n == 2:
                    act.wait_ge(stage_loaded.sem, 64)
                    stage(st[0:LR, 0:HID + E], lora_sb[:, :])

            def exponentials(c, b, u, first, last):
                for i, (kind, n) in enumerate(SCORE_STEPS):
                    act.wait_ge(sc_ps.sem, sc_ps.at(c, i + 1))
                    if kind == "rest":
                        dst = probs_r[:, n:n + 2, :]
                    else:
                        dst = probs[:, n % 8:n % 8 + 2, :]
                        if n >= 8:
                            act.wait_ge(pv_ps.sem, pv_ps.at(c, n // 4 - 1))
                    nc.scalar.activation(dst, psX[:, 2 * (i % 2):2 * (i % 2) + 2, :], ACT.Exp).then_inc(sc_exp.sem, 1)
                    if first and i in (1, 3, 5):
                        stage_late(i // 2)
                if not first:
                    store(b if u else b - 1, 1 - u, c - 1)
                if u == 1 and not last:
                    load_ctx(b + 1, c)
                for f2 in range(2):
                    norm_hi(c, f2)
                    heads_back(c, f2)

            act.wait_ge(tab_loaded.sem, 16)
            nc.scalar.activation(gate[:, :], g_b, ACT.Tanh).then_inc(gate_ready.sem, 1)
            act.wait_ge(stage_loaded.sem, 16)
            stage(st[:, 0:FT * E], wq_hi[:, :, :].rearrange("p f n -> p (f n)"))
            act.wait_ge(stage_loaded2.sem, 16)
            stage(stl[:, 0:NQ * E], wo_hi[:, :, :].rearrange("p g n -> p (g n)"))
            step(0, 0, first=True)
            step(0, 1)
            with act.Fori(1, B - 1) as b:
                step(b, 0)
                step(b, 1)
            step(B - 1, 0)
            step(B - 1, 1, last=True)
            d = 2 * B - 1
            for f in range(FT):
                act.wait_ge(x2T_ps.sem, x2T_ps.at(d, f + 1))
                copy(xT_hi[:, f, :], psX[:, 2 + f, :]).then_inc(x2T_hi_s.sem, 1)
            act.wait_ge(g1_v.sem, g1_v.at(d, 3))
            nc.scalar.activation(zex[:, 0], zsh[:, 0], ACT.Exp).then_inc(g1_e.sem, 1)
            act.wait_ge(z1T_ps.sem, z1T_ps.at(d))
            copy(zT[:, :], psO[0:LR, :]).then_inc(z1T_s.sem, 1)
            for m in range(HT):
                relu(d, m)
            for pr in range(2):
                act.wait_ge(g2_v.sem, g2_v.at(d, 8 * pr + 2))
                nc.scalar.activation(zex[:, 0, 2 * pr:2 * pr + 2], zsh[:, 0, 2 * pr:2 * pr + 2],
                                     ACT.Exp).then_inc(g2_e.sem, 1)
                act.wait_ge(z2T_ps.sem, z2T_ps.at(d, pr + 1))
                copy(zT[:, 256 * pr:256 * pr + 256], psO[0:LR, 0:256]).then_inc(z2T_s.sem, 1)
            store(B - 1, 1, d)
            act.wait_ge(stored.sem, stored.at(d))

        @block.vector
        def _(dve):
            V = nc.vector

            def stage(src, hi, lo, n):
                dve.wait_ge(stage_hi.sem, n)
                V.tensor_tensor(lo, src, hi.bitcast(F32), ALU.subtract).then_inc(stage_lo.sem, 1)

            def statistics(which, src, c, stat, agg):
                for k in range(TT):
                    V.bn_stats(ln_s[:, which, k, :], src[:, k, :]).then_inc(stat.sem, 1)
                dve.wait_ge(stat.sem, stat.at(c))
                V.memset(pace[:, :], 0.0)
                for k in range(TT):
                    V.bn_aggr(ln_m[:, which, k, :], ln_s[:, which, k, :]).then_inc(agg.sem, 1)

            def normalise(which, src, c, rstd, done, free):
                dve.wait_ge(rstd.sem, rstd.at(c))
                if free is not None:
                    dve.wait_ge(*free)
                for k in range(TT):
                    V.tensor_scalar(xn[:, k, :], src[:, k, :], ln_m[:, which, k, 0:1], ln_r[:, which, k:k + 1],
                                    ALU.subtract, ALU.mult).then_inc(done.sem, 1)

            def ln1_stats(c, u, b):
                dve.wait_ge(x_loaded[u].sem, x_loaded[u].at(b))
                statistics(0, x_in[:, u], c, ln1_stat, ln1_agg)

            def ln1_norm(c, u, free):
                normalise(0, x_in[:, u], c, ln1_rstd, ln1_out, free)

            def gates(s, v, e, n, k0, k1, step0):
                nk = k1 - k0
                K = slice(k0, k1)
                i = step0

                def wait():
                    dve.wait_ge(v.sem, v.at(n, i))
                if step0 % 8:
                    wait()
                V.tensor_reduce(zmax[:, s, K], zc[:, s, K, NL:NL + NE], AX.X, ALU.max).then_inc(v.sem, 1)
                i += 1
                wait()
                V.tensor_tensor(zsh[:, s, K], zc[:, s, K, NL:NL + NE],
                                zmax[:, s, K].unsqueeze(2).to_broadcast([P, nk, NE]), ALU.subtract).then_inc(v.sem, 1)
                i += 1
                dve.wait_ge(e.sem, e.at(n, 1 if v is g1_v else k0 // 2 + 1))
                V.reduce_sum(zsum[:, s, K], zex[:, s, K], AX.X).then_inc(v.sem, 1)
                i += 1
                wait()
                V.reciprocal(zrec[:, s, K], zsum[:, s, K]).then_inc(v.sem, 1)
                i += 1
                wait()
                V.scalar_tensor_tensor(out=zw[:, s, K], in0=zex[:, s, K], scalar=1.0 / R,
                                       in1=zrec[:, s, K].unsqueeze(2).to_broadcast([P, nk, NE]),
                                       op0=ALU.mult, op1=ALU.mult).then_inc(v.sem, 1)
                i += 1
                wait()
                V.tensor_tensor(zg[:, s, K].rearrange("p k (e r) -> p (k e) r", r=R),
                                zc[:, s, K, 0:NL].rearrange("p k (e r) -> p k e r", r=R),
                                zw[:, s, K].unsqueeze(3).to_broadcast([P, nk, NE, R]),
                                ALU.mult).then_inc(v.sem, 1)
                i += 1
                wait()
                V.tensor_copy(zs[:, s, K, 0:NL], zg[:, s, K])
                V.tensor_copy(zs[:, s, K, 64:64 + NL], zg[:, s, K]).then_inc(v.sem, 1)
                i += 1
                wait()
                V.tensor_tensor(zs[:, s, K, 32:32 + NL], zg[:, s, K], zs[:, s, K, 0:NL].bitcast(F32),
                                ALU.subtract).then_inc(v.sem, 1)

            def residual(d, u, stored_before=True):
                if stored_before:
                    dve.wait_ge(stored.sem, stored.at(d - 1))
                for j in range(2):
                    dve.wait_ge(wo_ps.sem, wo_ps.at(d, j + 1))
                    if j == 0:
                        dve.wait_ge(xb_ready.sem, xb_ready.at(d))
                    V.scalar_tensor_tensor(out=x1[:, 2 * j:2 * j + 2, :],
                                           in0=psX[:, j, :].rearrange("p (k e) -> p k e", k=2),
                                           scalar=gate[:, 0:1], in1=x_in[:, u, 2 * j:2 * j + 2, :],
                                           op0=ALU.mult, op1=ALU.add).then_inc(x1_s.sem, 1)

            def xT_low(c, ps, hi_s, lo_s, bank):
                for f in range(FT):
                    dve.wait_ge(hi_s.sem, hi_s.at(c, f + 1))
                    V.tensor_tensor(xT_lo[:, f, :], psX[:, bank + f, :], xT_hi[:, f, :].bitcast(F32),
                                    ALU.subtract).then_inc(lo_s.sem, 1)

            def q_bias(c):
                for j in range(2):
                    dve.wait_ge(q_ps.sem, q_ps.at(c, j + 1))
                    V.tensor_tensor(q_ev[:, 2 * j:2 * j + 2, :], psX[:, 2 + j, :].rearrange("p (k e) -> p k e", k=2),
                                    bq_b.unsqueeze(1).to_broadcast([P, 2, E]), ALU.add).then_inc(q_evac.sem, 1)

            def q_sine(c, u):
                dve.wait_ge(q_evac.sem, q_evac.at(c))
                for k in range(TT):
                    V.tensor_tensor(q_rs[:, k, :].rearrange("p (h s d) -> p h s d", s=2, d=D // 2),
                                    q_ev[:, k, :].rearrange("p (h s d) -> p h s d", s=2, d=D // 2)[:, :, ::-1, :],
                                    sin_q[:, u, k, :].rearrange("p (s d) -> p s d", s=2).unsqueeze(1)
                                    .to_broadcast([P, H, 2, D // 2]), ALU.mult).then_inc(q_sin.sem, 1)

            def q_sum(c):
                dve.wait_ge(q_cos.sem, q_cos.at(c))
                dve.wait_ge(q_sin.sem, q_sin.at(c))
                V.tensor_tensor(q_rc, q_rc, q_rs, ALU.add).then_inc(q_rot.sem, 1)

            def keys_and_values(b):
                dve.wait_ge(kv_ps.sem, kv_ps.at(b, 1))
                V.tensor_tensor(k_ev[:, 0, :], psF[:, 1, 0:E], bk_b, ALU.add).then_inc(kv_evac.sem, 1)
                V.tensor_tensor(v_sb[:, :, 0:D], psF[:, 1, E:2 * E].rearrange("p (h d) -> p h d", d=D),
                                bv_b.rearrange("p (h d) -> p h d", d=D), ALU.add).then_inc(v_evac.sem, 1)
                dve.wait_ge(kv_ps.sem, kv_ps.at(b, 2))
                V.tensor_tensor(k_ev[0:SR, 1, :], psF[0:SR, 2, 0:E], bk_b[0:SR, :], ALU.add).then_inc(kv_evac.sem, 1)
                for j in range(4):
                    q = slice(32 * j, 32 * j + SR)
                    V.tensor_tensor(vr_sb[q, :, 32 * j:32 * j + D],
                                    psF[q, 2, E:2 * E].rearrange("p (g j d) -> p g j d", j=4, d=D)[:, :, j, :],
                                    bv_b[q, :].rearrange("p (g j d) -> p g j d", j=4, d=D)[:, :, j, :],
                                    ALU.add).then_inc(v_evac.sem, 1)
                dve.wait_ge(kv_evac.sem, kv_evac.at(b))
                V.tensor_tensor(k_rc.rearrange("p a (h d) -> p a h d", d=D), k_ev.rearrange("p a (h d) -> p a h d", d=D),
                                cos_k.unsqueeze(2).to_broadcast([P, 2, H, D]), ALU.mult).then_inc(k_rot.sem, 1)
                for a in range(2):
                    V.tensor_tensor(k_rs[:, a, :].rearrange("p (h s d) -> p h s d", s=2, d=D // 2),
                                    k_ev[:, a, :].rearrange("p (h s d) -> p h s d", s=2, d=D // 2)[:, :, ::-1, :],
                                    sin_k[:, a, :].rearrange("p (s d) -> p s d", s=2).unsqueeze(1)
                                    .to_broadcast([P, H, 2, D // 2]), ALU.mult).then_inc(k_rot.sem, 1)
                dve.wait_ge(k_rot.sem, k_rot.at(b, 3))
                V.tensor_tensor(k_rc, k_rc, k_rs, ALU.add).then_inc(k_rot.sem, 1)
                dve.wait_ge(k_rot.sem, k_rot.at(b, 4))
                kf = k_rc.rearrange("p a (g r) -> p (a g) r", r=32)
                kd = ks[:, :, :, :].rearrange("p a g r -> p (a g) r")
                V.tensor_copy(kd[:, :, 0:64].rearrange("p a (t r) -> p a t r", t=2),
                              kf.unsqueeze(2).to_broadcast([P, 2 * NG, 2, 32])).then_inc(k_split.sem, 1)
                dve.wait_ge(k_split.sem, k_split.at(b, 1))
                V.tensor_tensor(kd[:, :, 64:96], kf, kd[:, :, 0:32].bitcast(F32), ALU.subtract).then_inc(k_split.sem, 1)

            def key_operands(b):
                dve.wait_ge(km_ps.sem, km_ps.at(b, 1))
                for hh in range(2):
                    V.tensor_scalar(km[:, 0:4, hh, 0:P], psX[0:KA, 0, :].rearrange("p (g s) -> p g s", g=4),
                                    mask[0:KA, hh:hh + 1], None, ALU.mult).then_inc(km_v.sem, 1)
                dve.wait_ge(km_ps.sem, km_ps.at(b, 3))
                rest = psX[0:KA, 2, 0:NG * 32].rearrange("p (g s) -> p g s", g=NG)[:, :, 0:SR]
                for hh in range(2):
                    V.tensor_scalar(km[:, :, hh, P:S], rest, mask[0:KA, hh:hh + 1], None, ALU.mult).then_inc(km_v.sem, 1)
                for hh in range(2):
                    for a in range(2):
                        ins = V.tensor_scalar(
                            kr[:, a::2, 64 * a + 32 * hh:64 * a + 32 * hh + SR],
                            rest[:, a::2, :], mask[0:KA, hh:hh + 1], None, ALU.mult)
                    ins.then_inc(km_v.sem, 1)

            def q_transposed(c, g):
                dve.wait_ge(qT_ps.sem, qT_ps.at(c, g + 1))
                V.tensor_copy(qT[0:KS, g, :], psX[0:KS, g % 4, :]).then_inc(qT_v.sem, 1)

            def h_low(d, m):
                dve.wait_ge(w1_hi_s.sem, w1_hi_s.at(d, m + 1))
                V.scalar_tensor_tensor(out=h_lo[:, m, :], in0=psF[:, m % 3, :], scalar=0.0,
                                       in1=h_hi[:, m, :].bitcast(F32), op0=ALU.max,
                                       op1=ALU.subtract).then_inc(w1_lo_s.sem, 1)

            def reduce_max(c, i):
                k, gp = i // 4, i % 4
                dve.wait_ge(max_ps.sem, max_ps.at(c, i + 1))
                V.tensor_reduce(max_t[:, k, :, 2 * gp:2 * gp + 2].rearrange("p h g -> p g h"),
                                psX[:, 2 * (i % 2):2 * (i % 2) + 2, 0:2 * S].rearrange("p g (h s) -> p g h s", h=2),
                                AX.X, ALU.max).then_inc(max_red.sem, 1)

            def copy_z2(d, k):
                dve.wait_ge(w2_ps.sem, w2_ps.at(d, k + 1))
                V.tensor_copy(zc[:, 0, k, :], psF[:, F_OF_K[k], E:W2N]).then_inc(g2_c.sem, 1)

            def gates2(d, pr):
                dve.wait_ge(g2_c.sem, g2_c.at(d, 2 * pr + 2))
                gates(0, g2_v, g2_e, d, 2 * pr, 2 * pr + 2, 8 * pr)

            def finish(d, k):
                dve.wait_ge(y_ps.sem, y_ps.at(d, k + 1))
                V.scalar_tensor_tensor(out=x1[:, k, :], in0=psF[:, F_OF_K[k], 0:E], scalar=gate[:, 1:2],
                                       in1=x1[:, k, :], op0=ALU.mult, op1=ALU.add).then_inc(y_out.sem, 1)

            def head_blocks(c, g):
                dve.wait_ge(pv_ps.sem, pv_ps.at(c, g + 1))
                V.transpose(heads_t[:, g, :, :].rearrange("p c r -> p (c r)"), psO[:, :]).then_inc(pv_t.sem, 1)

            def head_norm(c, f2):
                G2 = slice(2 * f2, 2 * f2 + 2)
                hv = heads_t[:, G2, :, :].rearrange("p g c r -> p (g c) r")
                nv = ns[:, G2, :, :].rearrange("p g c r -> p (g c) r")
                dve.wait_ge(pv_t.sem, pv_t.at(c, 2 * f2 + 2))
                V.reciprocal(den[:, G2, :].rearrange("p g c -> p (g c)"), hv[:, :, DSEL]).then_inc(den_inv.sem, 1)
                dve.wait_ge(den_inv.sem, den_inv.at(c, f2 + 1))
                V.tensor_tensor(hv[:, :, 0:D], hv[:, :, 0:D],
                                den[:, G2, :].rearrange("p g c -> p (g c)").unsqueeze(2).to_broadcast([P, 32, D]),
                                ALU.mult).then_inc(o_norm.sem, 1)

            def head_back(c, f2):
                G2 = slice(2 * f2, 2 * f2 + 2)
                hv = heads_t[:, G2, :, :].rearrange("p g c r -> p (g c) r")
                nv = ns[:, G2, :, :].rearrange("p g c r -> p (g c) r")
                dve.wait_ge(o_hi.sem, o_hi.at(c, f2 + 1))
                V.tensor_tensor(nv[:, :, D:32], hv[:, :, 0:D], nv[:, :, 0:D].bitcast(F32),
                                ALU.subtract).then_inc(o_lo.sem, 1)
                dve.wait_ge(o_lo.sem, o_lo.at(c, f2 + 1))
                V.transpose(heads_t[:, G2, :, :].rearrange("p g c r -> p g (c r)"),
                            ns[:, G2, :, :].rearrange("p g c r -> p g (c r)").bitcast(F32)).then_inc(o_back.sem, 1)

            def gates1(d):
                dve.wait_ge(z1_ps.sem, z1_ps.at(d))
                V.tensor_copy(zc[:, 0], psO[:, 0:TT * ZC].rearrange("p (k z) -> p k z", z=ZC)).then_inc(g1_v.sem, 1)
                gates(0, g1_v, g1_e, d, 0, TT, 1)

            def step(b, u, first=False, second=False, last=False):
                c = 2 * b + u
                d = c - 1
                xT_low(c, xT_ps, xT_hi_s, xT_lo_s, 0)
                q_bias(c)
                if not first:
                    residual(d, 1 - u, not second)
                    ln2_stats(d)
                q_sine(c, u)
                if not first:
                    ln2_norm(d, c)
                q_sum(c)
                if not first:
                    xT_low(d, x2T_ps, x2T_hi_s, x2T_lo_s, 2)
                if u == 0:
                    keys_and_values(b)
                if not first:
                    gates1(d)
                    for m in range(3):
                        h_low(d, m)
                if u == 0:
                    key_operands(b)
                for g in range(1, NG, 2):
                    q_transposed(c, g)
                    if not first:
                        h_low(d, 3 + g // 2)
                if not first:
                    h_low(d, 7)
                else:
                    stage(st[:, 0:FT * HID], w1_hi[:, :, :].rearrange("p f n -> p (f n)"),
                          w1_lo[:, :, :].rearrange("p f n -> p (f n)"), 3)
                for i in range(16):
                    reduce_max(c, i)
                    if not first:
                        if i == 4:
                            copy_z2(d, 0)
                        if i == 8:
                            copy_z2(d, 1)
                            gates2(d, 0)
                        if i == 12:
                            copy_z2(d, 2)
                            finish(d, 0)
                            finish(d, 1)
                if not first:
                    copy_z2(d, 3)
                    gates2(d, 1)
                    finish(d, 2)
                    finish(d, 3)
                if first:
                    stage(stl[:, 0:W2N], w2_hi[:, HT - 1, :], w2_lo[:, HT - 1, :], 4)
                    stage(stl[:, W2N:W2N + FT * ZC], a1_hi[:, :, :].rearrange("p f n -> p (f n)"),
                          a1_lo[:, :, :].rearrange("p f n -> p (f n)"), 5)
                    stage(st[:, 0:(HT - 1) * W2N], w2_hi[:, 0:HT - 1, :].rearrange("p m n -> p (m n)"),
                          w2_lo[:, 0:HT - 1, :].rearrange("p m n -> p (m n)"), 6)
                    dve.wait_ge(stage_hi.sem, 7)
                    V.tensor_tensor(lora_sb[64:LR, :], st[64:LR, 0:HID + E], lora_sb[64:LR, :].bitcast(F32),
                                    ALU.subtract).then_inc(stage_lo.sem, 1)
                    dve.wait_ge(stage_lo.sem, 7)
                if not last:
                    if u == 0:
                        ln1_stats(c + 1, 1, b)
                    else:
                        ln1_stats(c + 1, 0, b + 1)
                for g in range(2):
                    head_blocks(c, g)
                head_norm(c, 0)
                if not last:
                    ln1_norm(c + 1, 1 - u, (x2T_ps.sem, x2T_ps.at(d)) if not first else (xT_ps.sem, xT_ps.at(c)))
                head_blocks(c, 2)
                head_back(c, 0)
                head_blocks(c, 3)
                head_norm(c, 1)
                head_back(c, 1)

            def ln2_stats(d):
                dve.wait_ge(x1_s.sem, x1_s.at(d))
                statistics(1, x1, d, ln2_stat, ln2_agg)

            def ln2_norm(d, c):
                normalise(1, x1, d, ln2_rstd, ln2_out,
                          (xT_ps.sem, xT_ps.at(c)) if c is not None else None)

            V.memset(probs_r[:, :, :], 0.0).then_inc(const_v.sem, 1)
            V.memset(kr[:, :, :].bitcast(F32), 0.0).then_inc(const_v.sem, 1)
            V.memset(v_sb[:, :, :], 0.0).then_inc(const_v.sem, 1)
            V.memset(vr_sb[:, :, :], 0.0).then_inc(const_v.sem, 1)
            V.memset(ks[:, :, :, KS:KA].bitcast(F32), 1.0).then_inc(const_v.sem, 1)
            ln1_stats(0, 0, 0)
            dve.wait_ge(const_v.sem, 5)
            V.memset(v_sb[:, :, DSEL:DSEL + 1], 1.0)
            for j in range(4):
                V.memset(vr_sb[32 * j:32 * j + SR, :, 32 * j + DSEL:32 * j + DSEL + 1], 1.0)
            dve.wait_ge(const_p.sem, 2)
            V.tensor_copy(ident_r[:, :], ident[:, :]).then_inc(const_v.sem, 1)
            ln1_norm(0, 0, None)
            dve.wait_ge(gate_ready.sem, 1)
            V.tensor_scalar(bo_b, bo_b, gate[:, 0:1], None, ALU.mult).then_inc(gbo_ready.sem, 1)
            stage(st[:, 0:FT * E], wq_hi[:, :, :].rearrange("p f n -> p (f n)"),
                  wq_lo[:, :, :].rearrange("p f n -> p (f n)"), 1)
            stage(stl[:, 0:NQ * E], wo_hi[:, :, :].rearrange("p g n -> p (g n)"),
                  wo_lo[:, :, :].rearrange("p g n -> p (g n)"), 2)
            step(0, 0, first=True)
            step(0, 1, second=True)
            with dve.Fori(1, B - 1) as b:
                step(b, 0)
                step(b, 1)
            step(B - 1, 0)
            step(B - 1, 1, last=True)
            d = 2 * B - 1
            residual(d, 1)
            ln2_stats(d)
            ln2_norm(d, None)
            xT_low(d, x2T_ps, x2T_hi_s, x2T_lo_s, 2)
            gates1(d)
            for m in range(HT):
                h_low(d, m)
            copy_z2(d, 0)
            copy_z2(d, 1)
            gates2(d, 0)
            copy_z2(d, 2)
            finish(d, 0)
            finish(d, 1)
            copy_z2(d, 3)
            gates2(d, 1)
            finish(d, 2)
            finish(d, 3)

        @block.tensor
        def _(pe):
            mm = nc.tensor.matmul

            def tokens(k):
                return slice(P * k, P * k + P)

            def transpose_x(c, bank, src_s, ps):
                pe.wait_ge(src_s.sem, src_s.at(c))
                for f in range(FT):
                    for k in range(TT):
                        ins = nc.tensor.transpose(psX[:, bank + f, tokens(k)], xn[:, k, P * f:P * f + P], ident[:, :])
                    ins.then_inc(ps.sem, 1)

            def ctx_transposed(b, c, first):
                pe.wait_ge(ctx_loaded.sem, ctx_loaded.at(b))
                if not first:
                    pe.wait_ge(pv_t.sem, pv_t.at(c - 1))
                for f in range(FT):
                    nc.tensor.transpose(psO[:, S * f:S * f + P], ctx_sb[:, 0, P * f:P * f + P], ident[:, :])
                    ins = nc.tensor.transpose(psO[:, S * f + P:S * f + S], ctx_sb[0:SR, 1, P * f:P * f + P],
                                              ident[0:SR, 0:SR])
                ins.then_inc(ctxT_ps.sem, 1)

            def project_q(c, first):
                pe.wait_ge(xT_hi_s.sem, xT_hi_s.at(c))
                pe.wait_ge(xT_lo_s.sem, xT_lo_s.at(c))
                if first:
                    pe.wait_ge(stage_lo.sem, 1)
                else:
                    pe.wait_ge(sc_exp.sem, sc_exp.at(c - 1))
                for k in range(TT):
                    o_ps = psX[:, 2 + k // 2, E * (k % 2):E * (k % 2) + E]
                    n = 0
                    for a, w in ((xT_hi, wq_hi), (xT_lo, wq_hi), (xT_hi, wq_lo)):
                        for f in range(FT):
                            ins = mm(o_ps, a[:, f, tokens(k)], w[:, f, :], start=n == 0, stop=n == 5)
                            n += 1
                    if k % 2:
                        ins.then_inc(q_ps.sem, 1)

            def project_out(d, c):
                pe.wait_ge(oT_s.sem, oT_s.at(d))
                if c is not None:
                    pe.wait_ge(xT_lo_s.sem, xT_lo_s.at(c))
                for k in range(TT):
                    o_ps = psX[:, k // 2, E * (k % 2):E * (k % 2) + E]
                    n = 0
                    for w in (wo_hi, wo_lo):
                        for g in range(NQ):
                            ins = mm(o_ps, oT[:, g, tokens(k)], w[:, g, :], start=n == 0, stop=n == 7)
                            n += 1
                    if k % 2:
                        ins.then_inc(wo_ps.sem, 1)

            def project_kv(b, c, first):
                pe.wait_ge(ctxT_s.sem, ctxT_s.at(b))
                if first:
                    pe.wait_ge(wkv_loaded.sem, 16)
                else:
                    pe.wait_ge(y_out.sem, y_out.at(c - 2))
                for f in range(FT):
                    ins = mm(psF[:, 1, :], ctxT[:, f, 0:P], wkv_sb[:, f, :], start=f == 0, stop=f == FT - 1)
                ins.then_inc(kv_ps.sem, 1)
                for f in range(FT):
                    mm(psF[0:SR, 2, :], ctxT[:, f, P:S], wkv_sb[:, f, :], start=f == 0, stop=f == FT - 1)
                for f in range(FT):
                    for j in range(1, 4):
                        ins = mm(psF[32 * j:32 * j + SR, 2, E:2 * E], ctxT[:, f, P:S], wkv_sb[:, f, E:2 * E],
                                 start=f == 0, stop=f == FT - 1)
                ins.then_inc(kv_ps.sem, 1)

            def router1(d, c):
                pe.wait_ge(x2T_hi_s.sem, x2T_hi_s.at(d))
                pe.wait_ge(x2T_lo_s.sem, x2T_lo_s.at(d))
                if c == 1:
                    pe.wait_ge(stage_lo.sem, 7)
                pe.wait_ge(pv_t.sem, pv_t.at(d))
                for k in range(TT):
                    n = 0
                    for a, w in ((xT_hi, a1_hi), (xT_lo, a1_hi), (xT_hi, a1_lo)):
                        for f in range(FT):
                            ins = mm(psO[:, ZC * k:ZC * k + ZC], a[:, f, tokens(k)], w[:, f, :], start=n == 0, stop=n == 5)
                            n += 1
                ins.then_inc(z1_ps.sem, 1)

            def lora1_operand(d):
                pe.wait_ge(g1_v.sem, g1_v.at(d))
                for k in range(TT):
                    ins = nc.tensor.transpose(psO[0:LR, tokens(k)].bitcast(F32R), zs[:, 0, k, :], ident_r[:, :])
                ins.then_inc(z1T_ps.sem, 1)

            def hidden_main(d, m, kv_b=None, second=False):
                if m == 0:
                    if not second:
                        pe.wait_ge(y_out.sem, y_out.at(d - 1))
                elif m < 3:
                    if kv_b is not None:
                        pe.wait_ge(kv_evac.sem, kv_evac.at(kv_b, m))
                        pe.wait_ge(v_evac.sem, v_evac.at(kv_b, 1 if m == 1 else 5))
                else:
                    pe.wait_ge(w1_lo_s.sem, w1_lo_s.at(d, m - 2))
                n = 0
                for a, w in ((xT_hi, w1_hi), (xT_lo, w1_hi), (xT_hi, w1_lo)):
                    for f in range(FT):
                        mm(psF[:, m % 3, :], w[:, f, P * m:P * m + P], a[:, f, :], start=n == 0, stop=False)
                        n += 1

            def hidden_lora(d, m):
                if m == 0:
                    pe.wait_ge(z1T_s.sem, z1T_s.at(d))
                mm(psF[:, m % 3, :], lora_sb[:, P * m:P * m + P], zT[:, :], start=False, stop=True).then_inc(w1_ps.sem, 1)

            def key_transposes(b):
                pe.wait_ge(k_split.sem, k_split.at(b))
                for g in range(NG):
                    ins = nc.tensor.transpose(psX[0:KA, g // 4, tokens(g % 4)].bitcast(F32R), ks[:, 0, g, :], ident_r[:, :])
                    if g % 4 == 3:
                        ins.then_inc(km_ps.sem, 1)
                for g in range(NG):
                    ins = nc.tensor.transpose(psX[0:KA, 2, 32 * g:32 * g + SR].bitcast(F32R), ks[0:SR, 1, g, :],
                                              ident_r[0:SR, 0:SR])
                ins.then_inc(km_ps.sem, 1)

            def q_transposes(c, g, u, b, first):
                if g == 0:
                    pe.wait_ge(q_lo.sem, q_lo.at(c))
                    pe.wait_ge(q_hi2.sem, q_hi2.at(c))
                    if u == 0:
                        pe.wait_ge(km_v.sem, km_v.at(b))
                        pe.wait_ge(km_a.sem, km_a.at(b))
                elif g >= 4 and g % 2 == 0:
                    pe.wait_ge(qT_a.sem, qT_a.at(c, g // 2 - 1))
                elif g >= 4:
                    pe.wait_ge(qT_v.sem, qT_v.at(c, g // 2 - 1))
                for k in range(TT):
                    ins = nc.tensor.transpose(psX[0:KS, g % 4, tokens(k)].bitcast(F32R), qs[:, k, g, :], ident_r[:, :])
                ins.then_inc(qT_ps.sem, 1)

            def max_scores(c, i):
                k, gp = i // 4, i % 4
                if i == 0:
                    pe.wait_ge(qT_a.sem, qT_a.at(c, 3))
                    pe.wait_ge(qT_v.sem, qT_v.at(c, 3))
                elif i == 1:
                    pe.wait_ge(qT_a.sem, qT_a.at(c))
                    pe.wait_ge(qT_v.sem, qT_v.at(c))
                else:
                    pe.wait_ge(max_red.sem, max_red.at(c, i - 1))
                for j in range(2):
                    g = 2 * gp + j
                    ins = mm(psX[:, 2 * (i % 2) + j, 0:2 * S], qT[0:KS, g, tokens(k)],
                             km[0:KS, g, :, :].rearrange("p h s -> p (h s)"), start=True, stop=True)
                ins.then_inc(max_ps.sem, 1)

            def out_part(d, k, part):
                if part == 0:
                    if k == 0:
                        pe.wait_ge(w1_hi_s.sem, w1_hi_s.at(d))
                        pe.wait_ge(w1_lo_s.sem, w1_lo_s.at(d))
                    if k == 3:
                        pe.wait_ge(y_out.sem, y_out.at(d, 1))
                bank = F_OF_K[k]
                for m in range(2 * part, 2 * part + 2):
                    for i, (a, w) in enumerate(((h_hi, w2_hi), (h_lo, w2_hi), (h_hi, w2_lo))):
                        ins = mm(psF[:, bank, 0:W2N], a[:, m, tokens(k)], w[:, m, :],
                                 start=m == 0 and i == 0, stop=m == HT - 1 and i == 2)
                if part == 3:
                    ins.then_inc(w2_ps.sem, 1)

            def lora2_operand(d, pr):
                pe.wait_ge(g2_v.sem, g2_v.at(d, 8 * pr + 8))
                if pr == 0:
                    pe.wait_ge(z1T_s.sem, z1T_s.at(d))
                for j in range(2):
                    ins = nc.tensor.transpose(psO[0:LR, tokens(j)].bitcast(F32R), zs[:, 0, 2 * pr + j, :], ident_r[:, :])
                ins.then_inc(z2T_ps.sem, 1)

            def out_lora(d, pr):
                pe.wait_ge(z2T_s.sem, z2T_s.at(d, pr + 1))
                for k in (2 * pr, 2 * pr + 1):
                    mm(psF[:, F_OF_K[k], 0:E], zT[:, tokens(k)], lora_sb[:, HID:HID + E], start=False, stop=True,
                       skip_group_check=True).then_inc(y_ps.sem, 1)

            def max_transposed(c, first):
                pe.wait_ge(max_red.sem, max_red.at(c))
                if not first:
                    pe.wait_ge(z2T_s.sem, z2T_s.at(c - 1, 1))
                for k in range(TT):
                    ins = nc.tensor.transpose(psO[0:H, tokens(k)].bitcast(F32R),
                                              max_t[:, k, :, :].rearrange("p h g -> p (h g)"), ident_r[:, :])
                ins.then_inc(maxT_ps.sem, 1)

            def scores(c, i):
                if i == 0:
                    pe.wait_ge(max_rows.sem, max_rows.at(c))
                if i >= 2:
                    pe.wait_ge(sc_exp.sem, sc_exp.at(c, i - 1))
                kind, n = SCORE_STEPS[i]
                for j in range(2):
                    o_ps = psX[:, 2 * (i % 2) + j, :]
                    if kind == "rest":
                        g = 2 * (n + j)
                        mm(o_ps, kr[:, g, :], qT[:, g, :], start=True, stop=False)
                        ins = mm(o_ps, kr[:, g + 1, :], qT[:, g + 1, :], start=False, stop=True)
                    else:
                        ins = mm(o_ps, km[:, n // 2, j, 0:P], qT[:, n // 2, :], start=True, stop=True)
                ins.then_inc(sc_ps.sem, 1)

            def values(c, g, first):
                pe.wait_ge(sc_exp.sem, sc_exp.at(c, PV_AFTER[g]))
                if g == 0:
                    if first:
                        pe.wait_ge(maxT_s.sem, maxT_s.at(c))
                        pe.wait_ge(const_v.sem, 6)
                    else:
                        pe.wait_ge(z2T_s.sem, z2T_s.at(c - 1))
                        pe.wait_ge(maxT_s.sem, maxT_s.at(c))
                else:
                    pe.wait_ge(pv_t.sem, pv_t.at(c, g))
                mm(psO[:, :], vr_sb[:, g, :], probs_r[:, g, :], start=True, stop=False)
                for j in range(4):
                    h = 4 * g + j
                    ins = mm(psO[32 * j:32 * j + 32, :], v_sb[:, h, :], probs[:, h % 8, :], start=False, stop=True)
                ins.then_inc(pv_ps.sem, 1)

            def step(b, u, first=False, second=False):
                c = 2 * b + u
                d = c - 1
                if first:
                    pe.wait_ge(const_p.sem, 4)
                    pe.wait_ge(const_v.sem, 6)
                else:
                    pe.wait_ge(sc_exp.sem, sc_exp.at(d, 9))
                transpose_x(c, 0, ln1_out, xT_ps)
                if u == 0:
                    ctx_transposed(b, c, first)
                project_q(c, first)
                if not first:
                    project_out(d, c)
                if u == 0:
                    project_kv(b, c, first)
                if not first:
                    pe.wait_ge(q_evac.sem, q_evac.at(c))
                    transpose_x(d, 2, ln2_out, x2T_ps)
                    router1(d, 1 if second else None)
                    kv_b = b if u == 0 else None
                    hidden_main(d, 0, kv_b, second)
                    hidden_main(d, 1, kv_b, second)
                    lora1_operand(d)
                    hidden_lora(d, 0)
                    hidden_lora(d, 1)
                    hidden_main(d, 2, kv_b, second)
                    hidden_lora(d, 2)
                    pe.wait_ge(x1_s.sem, x1_s.at(d))
                if u == 0:
                    key_transposes(b)
                for g in range(NG):
                    q_transposes(c, g, u, b, first)
                    if not first and g % 2:
                        m = 3 + g // 2
                        hidden_main(d, m, kv_b, second)
                        hidden_lora(d, m)
                if not first:
                    hidden_main(d, 7, kv_b, second)
                    hidden_lora(d, 7)
                for i in range(16):
                    max_scores(c, i)
                    if not first and 1 <= i < 13:
                        out_part(d, (i - 1) // 4, (i - 1) % 4)
                    if not first and i == 12:
                        lora2_operand(d, 0)
                        out_lora(d, 0)
                max_transposed(c, first)
                if not first:
                    for part in range(4):
                        out_part(d, 3, part)
                for i in range(10):
                    scores(c, i)
                    if i == 1 and not first:
                        pe.wait_ge(maxT_s.sem, maxT_s.at(c))
                        lora2_operand(d, 1)
                        out_lora(d, 1)
                    if i in PV_SLOT:
                        values(c, PV_SLOT[i], first)
                values(c, 3, first)

            step(0, 0, first=True)
            step(0, 1, second=True)
            with pe.Fori(1, B) as b:
                step(b, 0)
                step(b, 1)
            d = 2 * B - 1
            project_out(d, None)
            transpose_x(d, 2, ln2_out, x2T_ps)
            router1(d, None)
            hidden_main(d, 0)
            hidden_main(d, 1)
            lora1_operand(d)
            hidden_lora(d, 0)
            hidden_lora(d, 1)
            for m in range(2, HT):
                hidden_main(d, m)
                hidden_lora(d, m)
            for k in range(TT):
                for part in range(4):
                    out_part(d, k, part)
                if k == 2:
                    lora2_operand(d, 0)
                    out_lora(d, 0)
            pe.wait_ge(z2T_s.sem, z2T_s.at(d, 1))
            lora2_operand(d, 1)
            out_lora(d, 1)


SCORE_STEPS = [("rest", 0), ("main", 0), ("main", 2), ("main", 4), ("main", 6),
               ("rest", 2), ("main", 8), ("main", 10), ("main", 12), ("main", 14)]
PV_AFTER = [3, 5, 8, 10]
PV_SLOT = {4: 0, 6: 1, 9: 2}
F_OF_K = [2, 0, 1, 2]


def position_tables():
    f = np.float32
    base = (np.arange(0, D, 2, dtype=f) + f(0.4 * D)) / f(1.4 * D)
    inv = (f(1.0) / f(10000.0) ** (np.arange(D // 2, dtype=f) / f(D // 2))).astype(f)

    def cs(pos, down):
        pos = pos.astype(f)
        scale = (base[None, :] ** (pos[:, None] / f(E))).astype(f)
        if down:
            scale = (f(1.0) / scale).astype(f)
        ang = pos[:, None] * inv[None, :]
        c, s = np.cos(ang).astype(f) * scale, np.sin(ang).astype(f) * scale
        return np.concatenate([c, c], 1), np.concatenate([-s, s], 1)

    u, p, k = np.meshgrid(np.arange(UB), np.arange(P), np.arange(TT), indexing="ij")
    pos = (CH * u + TT * p + k).transpose(1, 0, 2).reshape(-1)
    cq, sq = (t.reshape(P, -1) * f(D ** -0.5) for t in cs(pos, False))
    pos = (np.arange(P)[:, None] + P * np.arange(2)[None, :]).reshape(-1)
    ck, sk = (t.reshape(P, -1) for t in cs(pos, True))
    r = np.arange(P)
    head = np.where(r < KS, (r % 32) // D, r - KS)
    mask = np.stack([(head == 0), (head == 1)], 1).astype(f)
    return np.concatenate([cq, sq, ck, sk], 1).astype(f), mask


def kernel(**inputs):
    import numpy as _np
    import concourse.bacc as _bacc
    from concourse.bass_utils import run_bass_kernel_spmd as _run

    i = {n: _np.asarray(a) for n, a in inputs.items()}
    perm = _np.arange(E).reshape(H, D // 2, 2).transpose(0, 2, 1).reshape(-1)
    wq = i["L0_xattn_Wq"].T[:, perm].reshape(FT, P, E).transpose(1, 0, 2).reshape(P, -1)
    wkv = _np.concatenate([i["L0_xattn_Wk"].T[:, perm], i["L0_xattn_Wv"].T], 1)
    wo = i["L0_xattn_Wo"].T.reshape(NQ, 4, 1, D, E)
    wo = _np.broadcast_to(wo, (NQ, 4, 2, D, E)).reshape(NQ, P, E).transpose(1, 0, 2).reshape(P, -1)
    w1 = i["L0_ffn_W1"].reshape(FT, P, HID).transpose(1, 0, 2).reshape(P, -1)

    def lora_router(a, r):
        n = a.shape[1]
        return _np.concatenate([a.transpose(1, 0, 2).reshape(n, NL), r, _np.zeros((n, 1), r.dtype)], 1)

    a1 = lora_router(i["L0_ffn_A1"], i["L0_ffn_R1"]).reshape(FT, P, ZC).transpose(1, 0, 2).reshape(P, -1)
    w2 = _np.concatenate([i["L0_ffn_W2"], lora_router(i["L0_ffn_A2"], i["L0_ffn_R2"])], 1)
    w2 = w2.reshape(HT, P, W2N).transpose(1, 0, 2)
    a1 = _np.concatenate([w2[:, HT - 1, :], a1], 1)
    w2 = w2[:, 0:HT - 1, :].reshape(P, -1)
    lora = _np.zeros((LR, HID + E), _np.float32)
    lo = _np.concatenate([i["L0_ffn_B1"].reshape(NL, HID), i["L0_ffn_B2"].reshape(NL, E)], 1)
    bias = _np.concatenate([i["L0_ffn_b1"], i["L0_ffn_b2"]])
    for r in (0, 32, 64):
        lora[r:r + NL] = lo
    for r in (0, 64):
        lora[r + NL] = bias
    pos, mask = position_tables()
    rows = _np.concatenate([i["L0_xattn_bq"][perm], i["L0_xattn_bk"][perm], i["L0_xattn_bv"], i["L0_xattn_bo"],
                            i["g_xattn"], i["g_ffn"]])
    tables = _np.concatenate([pos, _np.broadcast_to(rows, (P, rows.size)), mask], 1)

    arrays = {"x": i["x"], "ctx": i["ctx_1024"], "wq": wq, "wkv": wkv, "wo": wo, "w1": w1, "w2": w2, "a1": a1,
              "lora": lora, "tables": tables}
    arrays = {f"in_{n}_dram": _np.ascontiguousarray(a) for n, a in arrays.items()}
    nc = _bacc.Bacc("TRN2", target_bir_lowering=False, num_devices=1)
    args = [nc.dram_tensor(n, a.shape, mybir.dt.from_np(a.dtype), kind="ExternalInput").ap()
            for n, a in arrays.items()]
    args.append(nc.dram_tensor("out_0_dram", (B, T, E), F32, kind="ExternalOutput").ap())
    build(nc, *args)
    r = _run(nc, [arrays], core_ids=[0])
    return r.results[0]["out_0_dram"]
```

```python
from contextlib import ExitStack

import numpy as np

import concourse.bass as bass
from concourse import mybir

F32 = mybir.dt.float32
F32R = mybir.dt.float32r
ACT = mybir.ActivationFunctionType
ALU = mybir.AluOpType
AX = mybir.AxisListType

B, T, E, S, H = 4, 1024, 256, 154, 16
D = E // H
HID, NE, R = 1024, 3, 8
P = 128
CH = 512
UB = T // CH
TT = CH // P
FT = E // P
HT = HID // P
NG = H // 2
NQ = H // 4
SR = S - P
ZC = 28
NL = NE * R
W2N = E + ZC
KS = 96
KA = KS + 2
LR = 96
EPS = 1e-5
DSEL = 16


class Count:

    def __init__(self, sem, per):
        self.sem, self.per = sem, per

    def at(self, n, k=None):
        return self.per * n + (self.per if k is None else k)


def build(nc, x, ctx_in, wq, wkv, wo, w1, w2, a1, lora, tables, out):
    with ExitStack() as stack:
        def sb(name, shape, dt=F32):
            return stack.enter_context(nc.sbuf_tensor(name, shape, dt))

        def count(name, per):
            return Count(stack.enter_context(nc.semaphore(name)), per)

        x_ln = sb("x_ln", [P, TT, E])
        x1 = sb("x1", [P, 2, TT, E])
        xn = sb("xn", [P, TT, E])
        xT_hi = sb("xT_hi", [P, FT, CH], F32R)
        xT_lo = sb("xT_lo", [P, FT, CH], F32R)
        split = sb("split", [P, TT * NG * KS], F32R)
        qs = split[:, :].rearrange("p (k g r) -> p k g r", k=TT, g=NG)
        ns = split[:, 0:NQ * 512].rearrange("p (g c r) -> p g c r", g=NQ, r=32)
        oT = split[:, 0:NQ * 512].rearrange("p (g t) -> p g t", g=NQ)
        heads_t = sb("heads_t", [P, NQ, 16, 32])
        qT = sb("qT", [KA, NG, CH], F32R)
        max_t = sb("max_t", [P, TT, 2, NG], F32R)
        max_f = split[0:H, NQ * 512:NQ * 512 + CH]
        probs = sb("probs", [P, 8, CH])
        probs_r = sb("probs_r", [P, NQ, CH])
        q_ev = probs[:, 0:2, :].rearrange("p a (k e) -> p (a k) e", e=E)
        q_rc = probs[:, 2:4, :].rearrange("p a (k e) -> p (a k) e", e=E)
        q_rs = probs[:, 4:6, :].rearrange("p a (k e) -> p (a k) e", e=E)
        zT = sb("zT", [LR, CH], F32R)
        h_hi = sb("h_hi", [P, HT, CH], F32R)
        h_lo = sb("h_lo", [P, HT, CH], F32R)
        wq_hi, wq_lo = (sb(f"wq_{n}", [P, FT, E], F32R) for n in ("hi", "lo"))
        wkv_sb = sb("wkv_sb", [P, FT, 2 * E])
        wo_hi, wo_lo = (sb(f"wo_{n}", [P, NQ, E], F32R) for n in ("hi", "lo"))
        a1_hi, a1_lo = (sb(f"a1_{n}", [P, FT, ZC], F32R) for n in ("hi", "lo"))
        w1_hi, w1_lo = (sb(f"w1_{n}", [P, FT, HID], F32R) for n in ("hi", "lo"))
        w2_hi, w2_lo = (sb(f"w2_{n}", [P, HT, W2N], F32R) for n in ("hi", "lo"))
        lora_sb = sb("lora_sb", [LR, HID + E], F32R)
        km = sb("km", [KA, NG, 2, S], F32R)
        kr = sb("kr", [KA, NG, P], F32R)
        v_sb = sb("v_sb", [P, H, 32])
        vr_sb = sb("vr_sb", [P, NQ, P])
        ks = sb("ks", [P, 2, NG, KA], F32R)
        ctx_sb, k_rc, k_ev, k_rs = x_ln[:, 0:2, :], x_ln[:, 0:2, :], x_ln[:, 2:4, :], xn[:, 0:2, :]
        ctxT = sb("ctxT", [P, FT, S])
        tab = sb("tab", [P, tables.shape[1]])
        ident_r = sb("ident_r", [P, P], F32R)
        ln_s = sb("ln_s", [P, 2, TT, 6])
        ln_m = sb("ln_m", [P, 2, TT, 2])
        ln_v = sb("ln_v", [P, 2, TT])
        ln_r = sb("ln_r", [P, 2, TT])
        ln_n = sb("ln_n", [P, 2, TT])
        ln_b = sb("ln_b", [P, 2, TT])
        half = sb("half", [P, TT])
        eps = sb("eps", [P, TT])
        pace = sb("pace", [P, 1])
        gate = sb("gate", [P, 2])
        den = sb("den", [P, NQ, 16])
        zc = sb("zc", [P, 1, TT, ZC])
        zmax = sb("zmax", [P, 1, TT])
        zsh = sb("zsh", [P, 1, TT, NE])
        zex = sb("zex", [P, 1, TT, NE])
        zsum = sb("zsum", [P, 1, TT])
        zrec = sb("zrec", [P, 1, TT])
        zw = sb("zw", [P, 1, TT, NE])
        zg = sb("zg", [P, 1, TT, NL])
        zs = sb("zs", [P, 1, TT, LR], F32R)

        o = 0

        def cols(n):
            nonlocal o
            o += n
            return tab[:, o - n:o]

        cos_q = cols(UB * TT * D).rearrange("p (u k d) -> p u k d", u=UB, k=TT)
        sin_q = cols(UB * TT * D).rearrange("p (u k d) -> p u k d", u=UB, k=TT)
        cos_k = cols(2 * D).rearrange("p (a d) -> p a d", a=2)
        sin_k = cols(2 * D).rearrange("p (a d) -> p a d", a=2)
        bq_b, bk_b, bv_b, bo_b = cols(E), cols(E), cols(E), cols(E)
        g_b, mask = cols(2), cols(2)

        psX = stack.enter_context(nc.psum_tensor("psX", [P, 4, CH], F32))
        psF = stack.enter_context(nc.psum_tensor("psF", [P, 3, CH], F32))
        psO = stack.enter_context(nc.psum_tensor("psO", [P, CH], F32))

        def pv_bank(g):
            return psF[:, g // 2, :] if g % 2 else psO[:, :]

        x_loaded = count("x_loaded", 16)
        x1_loaded = [count(f"x1_loaded{u}", 16) for u in range(2)]
        ctx_loaded = count("ctx_loaded", 32)
        tab_loaded = count("tab_loaded", 16)
        wkv_loaded = count("wkv_loaded", 16)
        w_loaded = {n: count(f"{n}_loaded", 16) for n in ("wq", "wo", "w1", "a1", "w2a", "w2b", "lora1", "lora2")}
        w_hi = {n: count(f"{n}_hi", 1) for n in w_loaded}
        w_lo = {n: count(f"{n}_lo", 1) for n in w_loaded}
        const_p = count("const_p", 1)
        const_v = count("const_v", 1)
        gate_ready = count("gate_ready", 1)
        gbo_ready = count("gbo_ready", 1)
        ln1_stat, ln1_agg = count("ln1_stat", TT), count("ln1_agg", TT)
        ln1_eps, ln1_rstd, ln1_out = count("ln1_eps", 1), count("ln1_rstd", 2), count("ln1_out", TT)
        ln2_stat, ln2_agg = count("ln2_stat", TT), count("ln2_agg", TT)
        ln2_eps, ln2_rstd, ln2_out = count("ln2_eps", 1), count("ln2_rstd", 2), count("ln2_out", TT)
        xb_ready = count("xb_ready", 1)
        xT_ps, xT_hi_s, xT_lo_s = count("xT_ps", FT), count("xT_hi_s", FT), count("xT_lo_s", FT)
        x2T_ps, x2T_hi_s, x2T_lo_s = count("x2T_ps", FT), count("x2T_hi_s", FT), count("x2T_lo_s", FT)
        q_ps, q_evac = count("q_ps", 2), count("q_evac", 2)
        q_cos, q_sin, q_rot = count("q_cos", 1), count("q_sin", TT), count("q_rot", 1)
        q_hi, q_hi2, q_lo = count("q_hi", 1), count("q_hi2", 1), count("q_lo", 1)
        qT_ps, qT_a, qT_v = count("qT_ps", NG), count("qT_a", NG // 2), count("qT_v", NG // 2)
        max_ps, max_red = count("max_ps", TT * NG // 2), count("max_red", TT * NG // 2)
        maxT_ps, maxT_s, max_rows = count("maxT_ps", 1), count("maxT_s", 1), count("max_rows", 32)
        sc_ps, sc_exp = count("sc_ps", 10), count("sc_exp", 10)
        pv_ps, pv_t = count("pv_ps", NQ), count("pv_t", NQ)
        den_inv, o_norm = count("den_inv", 2), count("o_norm", 2)
        o_hi, o_lo, o_back = count("o_hi", 2), count("o_lo", 2), count("o_back", 2)
        oT_s = count("oT_s", 2)
        wo_ps, x1_s = count("wo_ps", 2), count("x1_s", 2)
        z1_ps, g1_v, g1_e = count("z1_ps", 1), count("g1_v", 9), count("g1_e", 1)
        z1T_ps, z1T_s = count("z1T_ps", 1), count("z1T_s", 1)
        w1_ps, w1_hi_s, w1_lo_s = count("w1_ps", HT), count("h_hi_s", HT), count("h_lo_s", HT)
        w2_ps = count("w2_ps", TT)
        g2_c, g2_v, g2_e = count("g2_c", TT), count("g2_v", 16), count("g2_e", 2)
        z2T_ps, z2T_s = count("z2T_ps", 2), count("z2T_s", 2)
        y_ps, y_out, stored = count("y_ps", TT), count("y_out", TT), count("stored", 16)
        ctxT_ps, ctxT_s = count("ctxT_ps", 1), count("ctxT_s", 1)
        k_ps, k_evac = count("k_ps", 1), count("k_evac", 2)
        v_ps, v_evac = count("v_ps", 1), count("v_evac", 5)
        k_rot, k_split = count("k_rot", 4), count("k_split", 2)
        km_ps, km_v, km_a = count("km_ps", 3), count("km_v", 4), count("km_a", 4)

        x_d = x.rearrange("b (u p k) e -> b u p k e", u=UB, k=TT)
        out_d = out.rearrange("b (u p k) e -> b u p k e", u=UB, k=TT)

        q6, q7 = probs[:, 6, :], probs[:, 7, :]
        flat_h = heads_t[:, :, :, :].rearrange("p a b c -> p (a b c)")
        x1_0, x1_1 = (x1[:, u, :, :].rearrange("p k e -> p (k e)") for u in range(UB))
        n_w2 = (HT - 1) * W2N
        staged = {"wq": q6, "wo": x1_1, "w1": flat_h, "a1": q7[:, 0:FT * ZC], "w2a": flat_h[:, 0:n_w2],
                  "w2b": q6[:, 0:W2N], "lora1": x1_0[0:LR, :], "lora2": q7[0:LR, 256:256 + E]}
        ident_0 = q7[:, 128:256]
        ctx_0 = probs_r[:, 3, :].rearrange("p (a e) -> p a e", a=2)
        halves = {n: [t[:, :, :].rearrange("p a b -> p (a b)") for t in pair] for n, pair in
                  {"w1": (w1_hi, w1_lo), "wo": (wo_hi, wo_lo), "a1": (a1_hi, a1_lo), "w2": (w2_hi, w2_lo),
                   "wq": (wq_hi, wq_lo)}.items()}
        halves["w2a"], halves["w2b"] = ([t[:, 0:n_w2] for t in halves["w2"]], [t[:, n_w2:] for t in halves["w2"]])
        halves["lora1"], halves["lora2"] = ([t, t[64:LR, :]] for t in (lora_sb[:, 0:HID], lora_sb[:, HID:HID + E]))

        def low_args(n):
            hi, lo = halves[n]
            if n in ("lora1", "lora2"):
                return dict(out=lo, in0=staged[n][64:LR, :], in1=hi[64:LR, :].bitcast(F32), op=ALU.subtract)
            return dict(out=lo, in0=staged[n], in1=hi.bitcast(F32), op=ALU.subtract)

        block = stack.enter_context(nc.Block())

        @block.sync
        def _(sp):
            sp.dma_start(x_ln[:, :, :], x_d[0, 0]).then_inc(x_loaded.sem, 16)
            def stage(n, src):
                sp.dma_start(staged[n], src).then_inc(w_loaded[n].sem, 16)

            stage("wq", wq)
            sp.dma_start(tab[:, :], tables).then_inc(tab_loaded.sem, 16)
            sp.dma_start(ctx_0[:, 0, :], ctx_in[0, 0:P]).then_inc(ctx_loaded.sem, 16)
            sp.dma_start(ctx_0[0:SR, 1, :], ctx_in[0, P:S]).then_inc(ctx_loaded.sem, 16)
            stage("w1", w1)
            sp.dma_start(wkv_sb[:, :, :], wkv.rearrange("(f p) n -> p f n", p=P)).then_inc(wkv_loaded.sem, 16)
            stage("wo", wo)
            stage("a1", a1)
            stage("lora1", lora[:, 0:HID])
            stage("lora2", lora[:, HID:HID + E])
            sp.wait_ge(w_lo["w1"].sem, 1)
            stage("w2a", w2[:, 0:n_w2])
            sp.wait_ge(w_lo["wq"].sem, 1)
            stage("w2b", w2[:, n_w2:n_w2 + W2N])

            def rows_of_maxima(c):
                sp.wait_ge(maxT_s.sem, maxT_s.at(c))
                for hh in range(2):
                    sp.dma_start(qT[KS + hh:KS + hh + 1, :, :].bitcast(F32),
                                 split[NG * hh:NG * hh + NG, NQ * 512:NQ * 512 + CH].bitcast(F32)).then_inc(max_rows.sem, 16)

            rows_of_maxima(0)
            rows_of_maxima(1)
            with sp.Fori(1, B) as b:
                rows_of_maxima(2 * b)
                rows_of_maxima(2 * b + 1)

        @block.gpsimd
        def _(pool):
            nc.gpsimd.memset(ident_0, 0.0).then_inc(const_p.sem, 1)
            pool.wait_ge(const_p.sem, 1)
            nc.gpsimd.affine_select(out=ident_0, in_=ident_0, compare_op=ALU.not_equal, fill=1.0,
                                    base=0, pattern=[[-1, P]], channel_multiplier=1).then_inc(const_p.sem, 1)
            nc.gpsimd.memset(half[:, :], -0.5).then_inc(const_p.sem, 1)
            nc.gpsimd.memset(eps[:, :], EPS)
            nc.gpsimd.memset(zs[:, :, :, :].bitcast(F32), 0.0).then_inc(const_p.sem, 1)
            pool.wait_ge(const_p.sem, 4)
            nc.gpsimd.memset(zs[:, :, :, NL:NL + 1].bitcast(F32), 1.0)
            nc.gpsimd.memset(zs[:, :, :, 64 + NL:65 + NL].bitcast(F32), 1.0).then_inc(const_p.sem, 1)

            def rstd(which, agg, eps_s, out_s, c):
                pool.wait_ge(agg.sem, agg.at(c))
                nc.gpsimd.tensor_tensor(ln_v[:, which, :], ln_m[:, which, :, 1], eps[:, :], ALU.add)
                nc.gpsimd.tensor_scalar(ln_n[:, which, :], ln_m[:, which, :, 0], -1.0, None,
                                        ALU.mult).then_inc(eps_s.sem, 1)
                pool.wait_ge(eps_s.sem, eps_s.at(c))
                nc.gpsimd.tensor_tensor(ln_r[:, which, :], ln_v[:, which, :], half[:, :],
                                        ALU.pow).then_inc(out_s.sem, 1)
                pool.wait_ge(out_s.sem, out_s.at(c, 1))
                nc.gpsimd.tensor_tensor(ln_b[:, which, :], ln_n[:, which, :], ln_r[:, which, :],
                                        ALU.mult).then_inc(out_s.sem, 1)

            def residual_base(b, u):
                pool.wait_ge(x1_loaded[u].sem, x1_loaded[u].at(b))
                for k in range(TT):
                    ins = nc.gpsimd.tensor_tensor(x1[:, u, k], x1[:, u, k], bo_b, ALU.add)
                ins.then_inc(xb_ready.sem, 1)

            def stage_low(n):
                pool.wait_ge(w_hi[n].sem, 1)
                nc.gpsimd.tensor_tensor(**low_args(n)).then_inc(w_lo[n].sem, 1)

            def step(b, u, first=False, last=False):
                c = 2 * b + u
                pool.wait_ge(q_evac.sem, q_evac.at(c))
                nc.gpsimd.tensor_tensor(
                    q_rc.rearrange("p k (h d) -> p k h d", d=D), q_ev.rearrange("p k (h d) -> p k h d", d=D),
                    cos_q[:, u].unsqueeze(2).to_broadcast([P, TT, H, D]), ALU.mult).then_inc(q_cos.sem, 1)
                pool.wait_ge(q_hi.sem, q_hi.at(c))
                nc.gpsimd.tensor_tensor(
                    qs[:, :, :, 32:64].rearrange("p k g r -> p (k g) r"),
                    q_rc.rearrange("p k (g r) -> p (k g) r", r=32),
                    qs[:, :, :, 0:32].rearrange("p k g r -> p (k g) r").bitcast(F32),
                    ALU.subtract).then_inc(q_lo.sem, 1)
                if not first:
                    rstd(1, ln2_agg, ln2_eps, ln2_rstd, c - 1)
                if not last:
                    rstd(0, ln1_agg, ln1_eps, ln1_rstd, c + 1)
                if first:
                    stage_low("w2a")
                    stage_low("w2b")
                residual_base(b, u)

            rstd(0, ln1_agg, ln1_eps, ln1_rstd, 0)
            stage_low("w1")
            pool.wait_ge(gbo_ready.sem, 1)
            step(0, 0, first=True)
            step(0, 1)
            with pool.Fori(1, B - 1) as b:
                step(b, 0)
                step(b, 1)
            step(B - 1, 0)
            step(B - 1, 1, last=True)
            rstd(1, ln2_agg, ln2_eps, ln2_rstd, 2 * B - 1)

        @block.scalar
        def _(act):
            def copy(out_ap, in_ap, **kw):
                return nc.scalar.activation(out_ap, in_ap, ACT.Copy, **kw)

            def stage_high(n):
                act.wait_ge(w_loaded[n].sem, 16)
                copy(halves[n][0], staged[n]).then_inc(w_hi[n].sem, 1)

            def norm_hi(c, f2):
                act.wait_ge(o_norm.sem, o_norm.at(c, f2 + 1))
                copy(ns[:, 2 * f2:2 * f2 + 2, :, 0:D].rearrange("p g c d -> p (g c) d"),
                     heads_t[:, 2 * f2:2 * f2 + 2, :, 0:D].rearrange("p g c d -> p (g c) d")).then_inc(o_hi.sem, 1)

            def heads_back(c, f2):
                act.wait_ge(o_back.sem, o_back.at(c, f2 + 1))
                copy(oT[:, 2 * f2:2 * f2 + 2, :], heads_t[:, 2 * f2:2 * f2 + 2, :, :]
                     .rearrange("p g c r -> p g (c r)")).then_inc(oT_s.sem, 1)

            def store(b, u, e):
                act.wait_ge(y_out.sem, y_out.at(e))
                act.dma_start(out_d[b, u], x1[:, u]).then_inc(stored.sem, 16)

            def load(b, u, c):
                act.wait_ge(ln1_out.sem, ln1_out.at(c - 1))
                if u:
                    act.wait_ge(k_split.sem, k_split.at(b))
                act.dma_start(x_ln[:, :, :], x_d[b, u]).then_inc(x_loaded.sem, 16)

            def reload(b, u, c, full):
                if full:
                    act.wait_ge(stored.sem, stored.at(c - 2))
                else:
                    n = "wo" if u else "lora1"
                    act.wait_ge(w_lo[n].sem, 1)
                act.dma_start(x1[:, u], x_d[b, u]).then_inc(x1_loaded[u].sem, 16)

            def load_ctx(b, c):
                act.wait_ge(ln1_out.sem, ln1_out.at(c + 1))
                act.dma_start(ctx_sb[:, 0, :], ctx_in[b, 0:P]).then_inc(ctx_loaded.sem, 16)
                act.dma_start(ctx_sb[0:SR, 1, :], ctx_in[b, P:S]).then_inc(ctx_loaded.sem, 16)

            def xT_high(n, ps, hi_s, banks):
                for f in range(FT):
                    act.wait_ge(ps.sem, ps.at(n, f + 1))
                    copy(xT_hi[:, f, :], banks[:, f, :]).then_inc(hi_s.sem, 1)

            def ctx_copy(b):
                act.wait_ge(ctxT_ps.sem, ctxT_ps.at(b))
                copy(ctxT[:, :, :], psF[:, 2, 0:2 * S].rearrange("p (f s) -> p f s", f=FT)).then_inc(ctxT_s.sem, 1)

            def normalise(which, src, c, rstd, done, free):
                act.wait_ge(rstd.sem, rstd.at(c))
                if free is not None:
                    act.wait_ge(free[0].sem, free[0].at(free[1]))
                for k in range(TT):
                    nc.scalar.activation(xn[:, k, :], src[:, k, :], ACT.Identity, bias=ln_b[:, which, k:k + 1],
                                         scale=ln_r[:, which, k:k + 1]).then_inc(done.sem, 1)

            def key_operands(b):
                act.wait_ge(km_ps.sem, km_ps.at(b, 2))
                for hh in range(2):
                    copy(km[:, 4:8, hh, 0:P], psX[0:KA, 3, :].rearrange("p (g s) -> p g s", g=4),
                         scale=mask[0:KA, hh:hh + 1]).then_inc(km_a.sem, 1)
                act.wait_ge(km_ps.sem, km_ps.at(b, 3))
                rest = psO[0:KA, 0:NG * 32].rearrange("p (g s) -> p g s", g=NG)[:, :, 0:SR]
                for hh in range(2):
                    for a in range(2):
                        ins = copy(kr[:, a::2, 64 * a + 32 * hh:64 * a + 32 * hh + SR], rest[:, a::2, :],
                                   scale=mask[0:KA, hh:hh + 1])
                    ins.then_inc(km_a.sem, 1)

            def relu(d, m):
                act.wait_ge(w1_ps.sem, w1_ps.at(d, m + 1))
                nc.scalar.activation(h_hi[:, m, :], psF[:, (m + 1) % 3, :], ACT.Relu).then_inc(w1_hi_s.sem, 1)

            def gate2_exp(e, pr):
                act.wait_ge(g2_v.sem, g2_v.at(e, 8 * pr + 2))
                nc.scalar.activation(zex[:, 0, 2 * pr:2 * pr + 2], zsh[:, 0, 2 * pr:2 * pr + 2],
                                     ACT.Exp).then_inc(g2_e.sem, 1)

            def gate2_copy(e, pr):
                act.wait_ge(z2T_ps.sem, z2T_ps.at(e, pr + 1))
                copy(zT[:, 256 * pr:256 * pr + 256], psO[0:LR, 0:256]).then_inc(z2T_s.sem, 1)

            def gate1_exp(d):
                act.wait_ge(g1_v.sem, g1_v.at(d, 3))
                nc.scalar.activation(zex[:, 0], zsh[:, 0], ACT.Exp).then_inc(g1_e.sem, 1)

            def gate1_copy(d):
                act.wait_ge(z1T_ps.sem, z1T_ps.at(d))
                copy(zT[:, :], psO[0:LR, :]).then_inc(z1T_s.sem, 1)

            def step(b, u, first=False, second=False, last=False):
                c = 2 * b + u
                d, e = c - 1, c - 2
                full = not first and not second
                if full and not last:
                    load(b + u, 1 - u, c + 1)
                if first:
                    load(0, 1, 1)
                if u == 0:
                    key_operands(b)
                act.wait_ge(q_rot.sem, q_rot.at(c))
                if not first:
                    act.wait_ge(wo_ps.sem, wo_ps.at(d))
                for lo, done in ((0, q_hi), (64, q_hi2)):
                    copy(split[:, :].rearrange("p (a r) -> p a r", r=KS)[:, :, lo:lo + 32],
                         q_rc.rearrange("p k (g r) -> p (k g) r", r=32)).then_inc(done.sem, 1)
                if full:
                    gate2_exp(e, 0)
                if not first:
                    normalise(1, x1[:, 1 - u], d, ln2_rstd, ln2_out, (xT_ps, c))
                if full:
                    gate2_copy(e, 0)
                if not first:
                    xT_high(d, x2T_ps, x2T_hi_s, psX[:, 2:4, :])
                if full:
                    gate2_exp(e, 1)
                for g in range(0, NG, 2):
                    act.wait_ge(qT_ps.sem, qT_ps.at(c, g + 1))
                    copy(qT[0:KS, g, :], psX[0:KS, g % 4, :]).then_inc(qT_a.sem, 1)
                if full:
                    gate2_copy(e, 1)
                if not first:
                    gate1_exp(d)
                    gate1_copy(d)
                    for m in range(7):
                        relu(d, m)
                        if full and m == 3:
                            store(b - 1, u, e)
                        if m == 5 and not last:
                            normalise(0, x_ln, c + 1, ln1_rstd, ln1_out, (x2T_ps, d))
                else:
                    for n in ("wo", "a1", "lora1", "lora2", "w2a", "w2b"):
                        stage_high(n)
                    normalise(0, x_ln, c + 1, ln1_rstd, ln1_out, (xT_ps, c))
                act.wait_ge(maxT_ps.sem, maxT_ps.at(c))
                copy(max_f, psO[0:H, :], scale=-1.0).then_inc(maxT_s.sem, 1)
                if not first:
                    relu(d, 7)
                reload(b, u, c, full)
                if u == 1 and not last:
                    load_ctx(b + 1, c)
                if first:
                    for n in ("a1", "w2b", "lora2"):
                        act.wait_ge(w_lo[n].sem, 1)
                for i, (kind, n) in enumerate(SCORE_STEPS):
                    act.wait_ge(sc_ps.sem, sc_ps.at(c, i + 1))
                    if kind == "rest":
                        dst = probs_r[:, n:n + 2, :]
                    else:
                        dst = probs[:, n % 8:n % 8 + 2, :]
                        if n >= 8:
                            act.wait_ge(pv_ps.sem, pv_ps.at(c, n // 4 - 1))
                    nc.scalar.activation(dst, psX[:, 2 * (i % 2):2 * (i % 2) + 2, :], ACT.Exp).then_inc(sc_exp.sem, 1)
                    if i == 1 and not last:
                        xT_high(c + 1, xT_ps, xT_hi_s, psF)
                    if i == 3 and not last and u == 1:
                        ctx_copy(b + 1)
                for f2 in range(2):
                    norm_hi(c, f2)
                    heads_back(c, f2)

            stage_high("wq")
            normalise(0, x_ln, 0, ln1_rstd, ln1_out, None)
            xT_high(0, xT_ps, xT_hi_s, psF)
            act.wait_ge(tab_loaded.sem, 16)
            nc.scalar.activation(gate[:, :], g_b, ACT.Tanh).then_inc(gate_ready.sem, 1)
            ctx_copy(0)
            stage_high("w1")
            step(0, 0, first=True)
            load(1, 0, 2)
            step(0, 1, second=True)
            with act.Fori(1, B - 1) as b:
                step(b, 0)
                step(b, 1)
            step(B - 1, 0)
            step(B - 1, 1, last=True)
            d = 2 * B - 1
            gate2_exp(d - 1, 0)
            normalise(1, x1[:, 1], d, ln2_rstd, ln2_out, None)
            gate2_copy(d - 1, 0)
            xT_high(d, x2T_ps, x2T_hi_s, psX[:, 2:4, :])
            gate2_exp(d - 1, 1)
            gate2_copy(d - 1, 1)
            gate1_exp(d)
            gate1_copy(d)
            for m in range(HT):
                relu(d, m)
            store(B - 1, 0, d - 1)
            for pr in range(2):
                gate2_exp(d, pr)
                gate2_copy(d, pr)
            store(B - 1, 1, d)
            act.wait_ge(stored.sem, stored.at(d))

        @block.vector
        def _(dve):
            V = nc.vector

            def statistics(which, src, c, stat, agg):
                for k in range(TT):
                    V.bn_stats(ln_s[:, which, k, :], src[:, k, :]).then_inc(stat.sem, 1)
                dve.wait_ge(stat.sem, stat.at(c))
                V.memset(pace[:, :], 0.0)
                for k in range(TT):
                    V.bn_aggr(ln_m[:, which, k, :], ln_s[:, which, k, :]).then_inc(agg.sem, 1)

            def ln1_stats(c):
                dve.wait_ge(x_loaded.sem, x_loaded.at(c))
                statistics(0, x_ln, c, ln1_stat, ln1_agg)

            def gates(s, v, e, n, k0, k1, step0, meanwhile=None):
                nk = k1 - k0
                K = slice(k0, k1)
                i = step0

                def wait():
                    dve.wait_ge(v.sem, v.at(n, i))
                if step0 % 8:
                    wait()
                V.tensor_reduce(zmax[:, s, K], zc[:, s, K, NL:NL + NE], AX.X, ALU.max).then_inc(v.sem, 1)
                i += 1
                wait()
                V.tensor_tensor(zsh[:, s, K], zc[:, s, K, NL:NL + NE],
                                zmax[:, s, K].unsqueeze(2).to_broadcast([P, nk, NE]), ALU.subtract).then_inc(v.sem, 1)
                i += 1
                if meanwhile is not None:
                    meanwhile()
                dve.wait_ge(e.sem, e.at(n, 1 if v is g1_v else k0 // 2 + 1))
                V.reduce_sum(zsum[:, s, K], zex[:, s, K], AX.X).then_inc(v.sem, 1)
                i += 1
                wait()
                V.reciprocal(zrec[:, s, K], zsum[:, s, K]).then_inc(v.sem, 1)
                i += 1
                wait()
                V.scalar_tensor_tensor(out=zw[:, s, K], in0=zex[:, s, K], scalar=1.0 / R,
                                       in1=zrec[:, s, K].unsqueeze(2).to_broadcast([P, nk, NE]),
                                       op0=ALU.mult, op1=ALU.mult).then_inc(v.sem, 1)
                i += 1
                wait()
                V.tensor_tensor(zg[:, s, K].rearrange("p k (e r) -> p (k e) r", r=R),
                                zc[:, s, K, 0:NL].rearrange("p k (e r) -> p k e r", r=R),
                                zw[:, s, K].unsqueeze(3).to_broadcast([P, nk, NE, R]),
                                ALU.mult).then_inc(v.sem, 1)
                i += 1
                wait()
                V.tensor_copy(zs[:, s, K, 0:NL], zg[:, s, K])
                V.tensor_copy(zs[:, s, K, 64:64 + NL], zg[:, s, K]).then_inc(v.sem, 1)
                i += 1
                wait()
                V.tensor_tensor(zs[:, s, K, 32:32 + NL], zg[:, s, K], zs[:, s, K, 0:NL].bitcast(F32),
                                ALU.subtract).then_inc(v.sem, 1)

            def residual(d, u):
                for j in range(2):
                    dve.wait_ge(wo_ps.sem, wo_ps.at(d, j + 1))
                    if j == 0:
                        dve.wait_ge(xb_ready.sem, xb_ready.at(d))
                    V.scalar_tensor_tensor(out=x1[:, u, 2 * j:2 * j + 2, :],
                                           in0=psX[:, j, :].rearrange("p (k e) -> p k e", k=2),
                                           scalar=gate[:, 0:1], in1=x1[:, u, 2 * j:2 * j + 2, :],
                                           op0=ALU.mult, op1=ALU.add).then_inc(x1_s.sem, 1)

            def xT_low(c, hi_s, lo_s, banks):
                for f in range(FT):
                    dve.wait_ge(hi_s.sem, hi_s.at(c, f + 1))
                    V.tensor_tensor(xT_lo[:, f, :], banks[:, f, :], xT_hi[:, f, :].bitcast(F32),
                                    ALU.subtract).then_inc(lo_s.sem, 1)

            def q_bias(c):
                for j in range(2):
                    dve.wait_ge(q_ps.sem, q_ps.at(c, j + 1))
                    V.tensor_tensor(q_ev[:, 2 * j:2 * j + 2, :], psX[:, j, :].rearrange("p (k e) -> p k e", k=2),
                                    bq_b.unsqueeze(1).to_broadcast([P, 2, E]), ALU.add).then_inc(q_evac.sem, 1)

            def q_sine(c, u):
                dve.wait_ge(q_evac.sem, q_evac.at(c))
                for k in range(TT):
                    V.tensor_tensor(q_rs[:, k, :].rearrange("p (h s d) -> p h s d", s=2, d=D // 2),
                                    q_ev[:, k, :].rearrange("p (h s d) -> p h s d", s=2, d=D // 2)[:, :, ::-1, :],
                                    sin_q[:, u, k, :].rearrange("p (s d) -> p s d", s=2).unsqueeze(1)
                                    .to_broadcast([P, H, 2, D // 2]), ALU.mult).then_inc(q_sin.sem, 1)

            def q_sum(c):
                dve.wait_ge(q_cos.sem, q_cos.at(c))
                dve.wait_ge(q_sin.sem, q_sin.at(c))
                V.tensor_tensor(q_rc, q_rc, q_rs, ALU.add).then_inc(q_rot.sem, 1)

            def values_bias(b):
                dve.wait_ge(v_ps.sem, v_ps.at(b))
                V.tensor_tensor(v_sb[:, :, 0:D], psF[:, 2, 0:E].rearrange("p (h d) -> p h d", d=D),
                                bv_b.rearrange("p (h d) -> p h d", d=D), ALU.add).then_inc(v_evac.sem, 1)
                for j in range(4):
                    q = slice(32 * j, 32 * j + SR)
                    V.tensor_tensor(vr_sb[q, :, 32 * j:32 * j + D],
                                    psF[q, 2, E:2 * E].rearrange("p (g j d) -> p g j d", j=4, d=D)[:, :, j, :],
                                    bv_b[q, :].rearrange("p (g j d) -> p g j d", j=4, d=D)[:, :, j, :],
                                    ALU.add).then_inc(v_evac.sem, 1)

            def rotate_keys(b):
                dve.wait_ge(k_ps.sem, k_ps.at(b))
                V.tensor_tensor(k_ev[:, 0, :], psF[:, 2, 0:E], bk_b, ALU.add).then_inc(k_evac.sem, 1)
                V.tensor_tensor(k_ev[0:SR, 1, :], psF[0:SR, 2, E:2 * E], bk_b[0:SR, :], ALU.add).then_inc(k_evac.sem, 1)
                dve.wait_ge(k_evac.sem, k_evac.at(b))
                V.tensor_tensor(k_rc.rearrange("p a (h d) -> p a h d", d=D), k_ev.rearrange("p a (h d) -> p a h d", d=D),
                                cos_k.unsqueeze(2).to_broadcast([P, 2, H, D]), ALU.mult).then_inc(k_rot.sem, 1)
                for a in range(2):
                    V.tensor_tensor(k_rs[:, a, :].rearrange("p (h s d) -> p h s d", s=2, d=D // 2),
                                    k_ev[:, a, :].rearrange("p (h s d) -> p h s d", s=2, d=D // 2)[:, :, ::-1, :],
                                    sin_k[:, a, :].rearrange("p (s d) -> p s d", s=2).unsqueeze(1)
                                    .to_broadcast([P, H, 2, D // 2]), ALU.mult).then_inc(k_rot.sem, 1)
                dve.wait_ge(k_rot.sem, k_rot.at(b, 3))
                V.tensor_tensor(k_rc, k_rc, k_rs, ALU.add).then_inc(k_rot.sem, 1)
                dve.wait_ge(k_rot.sem, k_rot.at(b, 4))
                kf = k_rc.rearrange("p a (g r) -> p (a g) r", r=32)
                kd = ks[:, :, :, :].rearrange("p a g r -> p (a g) r")
                V.tensor_copy(kd[:, :, 0:64].rearrange("p a (t r) -> p a t r", t=2),
                              kf.unsqueeze(2).to_broadcast([P, 2 * NG, 2, 32])).then_inc(k_split.sem, 1)
                dve.wait_ge(k_split.sem, k_split.at(b, 1))
                V.tensor_tensor(kd[:, :, 64:96], kf, kd[:, :, 0:32].bitcast(F32), ALU.subtract).then_inc(k_split.sem, 1)

            def key_operands(b):
                dve.wait_ge(km_ps.sem, km_ps.at(b, 1))
                for hh in range(2):
                    V.tensor_scalar(km[:, 0:4, hh, 0:P], psX[0:KA, 2, :].rearrange("p (g s) -> p g s", g=4),
                                    mask[0:KA, hh:hh + 1], None, ALU.mult).then_inc(km_v.sem, 1)
                dve.wait_ge(km_a.sem, km_a.at(b))
                rest = psO[0:KA, 0:NG * 32].rearrange("p (g s) -> p g s", g=NG)[:, :, 0:SR]
                for hh in range(2):
                    V.tensor_scalar(km[:, :, hh, P:S], rest, mask[0:KA, hh:hh + 1], None, ALU.mult).then_inc(km_v.sem, 1)

            def q_transposed(c, g):
                dve.wait_ge(qT_ps.sem, qT_ps.at(c, g + 1))
                V.tensor_copy(qT[0:KS, g, :], psX[0:KS, g % 4, :]).then_inc(qT_v.sem, 1)

            def h_low(d, m):
                dve.wait_ge(w1_hi_s.sem, w1_hi_s.at(d, m + 1))
                V.scalar_tensor_tensor(out=h_lo[:, m, :], in0=psF[:, (m + 1) % 3, :], scalar=0.0,
                                       in1=h_hi[:, m, :].bitcast(F32), op0=ALU.max,
                                       op1=ALU.subtract).then_inc(w1_lo_s.sem, 1)

            def reduce_max(c, i):
                k, gp = i // 4, i % 4
                dve.wait_ge(max_ps.sem, max_ps.at(c, i + 1))
                V.tensor_reduce(max_t[:, k, :, 2 * gp:2 * gp + 2].rearrange("p h g -> p g h"),
                                psX[:, 2 * (i % 2):2 * (i % 2) + 2, 0:2 * S].rearrange("p g (h s) -> p g h s", h=2),
                                AX.X, ALU.max).then_inc(max_red.sem, 1)

            def copy_z2(d, k):
                dve.wait_ge(w2_ps.sem, w2_ps.at(d, k + 1))
                V.tensor_copy(zc[:, 0, k, :], psF[:, F_OF_K[k], E:W2N]).then_inc(g2_c.sem, 1)

            def gates2(d, pr):
                dve.wait_ge(g2_c.sem, g2_c.at(d, 2 * pr + 2))
                gates(0, g2_v, g2_e, d, 2 * pr, 2 * pr + 2, 8 * pr)

            def finish(d, u, k):
                dve.wait_ge(y_ps.sem, y_ps.at(d, k + 1))
                V.scalar_tensor_tensor(out=x1[:, u, k, :], in0=psF[:, F_OF_K[k], 0:E], scalar=gate[:, 1:2],
                                       in1=x1[:, u, k, :], op0=ALU.mult, op1=ALU.add).then_inc(y_out.sem, 1)

            def head_blocks(c, g):
                dve.wait_ge(pv_ps.sem, pv_ps.at(c, g + 1))
                V.transpose(heads_t[:, g, :, :].rearrange("p c r -> p (c r)"), pv_bank(g)).then_inc(pv_t.sem, 1)

            def head_norm(c, f2):
                G2 = slice(2 * f2, 2 * f2 + 2)
                hv = heads_t[:, G2, :, :].rearrange("p g c r -> p (g c) r")
                nv = ns[:, G2, :, :].rearrange("p g c r -> p (g c) r")
                dve.wait_ge(pv_t.sem, pv_t.at(c, 2 * f2 + 2))
                V.reciprocal(den[:, G2, :].rearrange("p g c -> p (g c)"), hv[:, :, DSEL]).then_inc(den_inv.sem, 1)
                dve.wait_ge(den_inv.sem, den_inv.at(c, f2 + 1))
                V.tensor_tensor(hv[:, :, 0:D], hv[:, :, 0:D],
                                den[:, G2, :].rearrange("p g c -> p (g c)").unsqueeze(2).to_broadcast([P, 32, D]),
                                ALU.mult).then_inc(o_norm.sem, 1)

            def head_back(c, f2):
                G2 = slice(2 * f2, 2 * f2 + 2)
                hv = heads_t[:, G2, :, :].rearrange("p g c r -> p (g c) r")
                nv = ns[:, G2, :, :].rearrange("p g c r -> p (g c) r")
                dve.wait_ge(o_hi.sem, o_hi.at(c, f2 + 1))
                V.tensor_tensor(nv[:, :, D:32], hv[:, :, 0:D], nv[:, :, 0:D].bitcast(F32),
                                ALU.subtract).then_inc(o_lo.sem, 1)
                dve.wait_ge(o_lo.sem, o_lo.at(c, f2 + 1))
                V.transpose(heads_t[:, G2, :, :].rearrange("p g c r -> p g (c r)"),
                            ns[:, G2, :, :].rearrange("p g c r -> p g (c r)").bitcast(F32)).then_inc(o_back.sem, 1)

            def gates1(d, meanwhile=None):
                dve.wait_ge(z1_ps.sem, z1_ps.at(d))
                V.tensor_copy(zc[:, 0], psO[:, 0:TT * ZC].rearrange("p (k z) -> p k z", z=ZC)).then_inc(g1_v.sem, 1)
                gates(0, g1_v, g1_e, d, 0, TT, 1, meanwhile)

            def ln2_stats(d, u):
                dve.wait_ge(x1_s.sem, x1_s.at(d))
                statistics(1, x1[:, u], d, ln2_stat, ln2_agg)

            def step(b, u, first=False, second=False, last=False):
                c = 2 * b + u
                d, e = c - 1, c - 2
                full = not first and not second
                if not first:
                    head_blocks(d, 3)
                    head_norm(d, 1)
                q_bias(c)
                if not first:
                    head_back(d, 1)
                q_sine(c, u)
                q_sum(c)
                if first:
                    rotate_keys(b)
                if u == 0:
                    values_bias(b)
                    key_operands(b)
                if full:
                    copy_z2(e, 0)
                if not first:
                    residual(d, 1 - u)
                    ln2_stats(d, 1 - u)
                if full:
                    copy_z2(e, 1)
                    gates2(e, 0)
                    finish(e, u, 0)
                    finish(e, u, 1)
                    copy_z2(e, 2)
                if not first:
                    xT_low(d, x2T_hi_s, x2T_lo_s, psX[:, 2:4, :])
                if full:
                    copy_z2(e, 3)
                    gates2(e, 1)
                for g in range(1, NG, 2):
                    q_transposed(c, g)
                if first:
                    for n in ("wo", "a1", "lora1", "lora2"):
                        dve.wait_ge(w_hi[n].sem, 1)
                        V.tensor_tensor(**low_args(n)).then_inc(w_lo[n].sem, 1)
                if full:
                    finish(e, u, 2)
                    finish(e, u, 3)
                if not last:
                    ln1_stats(c + 1)
                if not first:
                    gates1(d, meanwhile=lambda: reduce_max(c, 0))
                for i in range(0 if first else 1, 16):
                    reduce_max(c, i)
                    if not first:
                        if i in (4, 5):
                            h_low(d, i - 4)
                        if i >= 6 and i % 2 == 0:
                            h_low(d, i // 2 - 1)
                if not first:
                    h_low(d, 7)
                if not last:
                    xT_low(c + 1, xT_hi_s, xT_lo_s, psF)
                if first:
                    dve.wait_ge(w_lo["w2a"].sem, 1)
                head_blocks(c, 0)
                head_blocks(c, 1)
                head_norm(c, 0)
                if u == 1 and not last:
                    rotate_keys(b + 1)
                head_blocks(c, 2)
                head_back(c, 0)

            dve.wait_ge(const_p.sem, 5)
            V.tensor_copy(ident_r[:, :], ident_0).then_inc(const_v.sem, 1)
            ln1_stats(0)
            V.memset(ks[:, :, :, KS:KA].bitcast(F32), 1.0).then_inc(const_v.sem, 1)
            dve.wait_ge(w_hi["wq"].sem, 1)
            V.tensor_tensor(**low_args("wq")).then_inc(w_lo["wq"].sem, 1)
            xT_low(0, xT_hi_s, xT_lo_s, psF)
            V.memset(kr[:, :, :].bitcast(F32), 0.0).then_inc(const_v.sem, 1)
            V.memset(v_sb[:, :, :], 0.0).then_inc(const_v.sem, 1)
            V.memset(vr_sb[:, :, :], 0.0).then_inc(const_v.sem, 1)
            dve.wait_ge(const_v.sem, 5)
            V.memset(v_sb[:, :, DSEL:DSEL + 1], 1.0)
            for j in range(4):
                ins = V.memset(vr_sb[32 * j:32 * j + SR, :, 32 * j + DSEL:32 * j + DSEL + 1], 1.0)
            ins.then_inc(const_v.sem, 1)
            dve.wait_ge(gate_ready.sem, 1)
            V.tensor_scalar(bo_b, bo_b, gate[:, 0:1], None, ALU.mult).then_inc(gbo_ready.sem, 1)
            step(0, 0, first=True)
            step(0, 1, second=True)
            with dve.Fori(1, B - 1) as b:
                step(b, 0)
                step(b, 1)
            step(B - 1, 0)
            step(B - 1, 1, last=True)
            d, e = LAST, LAST - 1
            head_blocks(d, 3)
            head_norm(d, 1)
            head_back(d, 1)
            copy_z2(e, 0)
            residual(d, 1)
            ln2_stats(d, 1)
            copy_z2(e, 1)
            gates2(e, 0)
            finish(e, 0, 0)
            finish(e, 0, 1)
            copy_z2(e, 2)
            xT_low(d, x2T_hi_s, x2T_lo_s, psX[:, 2:4, :])
            copy_z2(e, 3)
            gates2(e, 1)
            finish(e, 0, 2)
            finish(e, 0, 3)
            gates1(d)
            for m in range(HT):
                h_low(d, m)
            copy_z2(d, 0)
            copy_z2(d, 1)
            gates2(d, 0)
            copy_z2(d, 2)
            finish(d, 1, 0)
            finish(d, 1, 1)
            copy_z2(d, 3)
            gates2(d, 1)
            finish(d, 1, 2)
            finish(d, 1, 3)

        @block.tensor
        def _(pe):
            mm = nc.tensor.matmul
            ident = ident_r[:, :].bitcast(F32)

            def tokens(k):
                return slice(P * k, P * k + P)

            def transpose_x(c, banks, src_s, ps):
                pe.wait_ge(src_s.sem, src_s.at(c))
                for f in range(FT):
                    for k in range(TT):
                        ins = nc.tensor.transpose(banks[:, f, tokens(k)], xn[:, k, P * f:P * f + P], ident)
                    ins.then_inc(ps.sem, 1)

            def ctx_transposed(b, src):
                pe.wait_ge(ctx_loaded.sem, ctx_loaded.at(b))
                if src is ctx_sb:
                    pe.wait_ge(w1_lo_s.sem, w1_lo_s.at(2 * b - 2))
                for f in range(FT):
                    nc.tensor.transpose(psF[:, 2, S * f:S * f + P], src[:, 0, P * f:P * f + P], ident)
                    ins = nc.tensor.transpose(psF[:, 2, S * f + P:S * f + S], src[0:SR, 1, P * f:P * f + P],
                                              ident[0:SR, 0:SR])
                ins.then_inc(ctxT_ps.sem, 1)

            def project_q(c, first):
                pe.wait_ge(xT_hi_s.sem, xT_hi_s.at(c))
                pe.wait_ge(xT_lo_s.sem, xT_lo_s.at(c))
                if first:
                    pe.wait_ge(w_lo["wq"].sem, 1)
                for k in range(TT):
                    o_ps = psX[:, k // 2, E * (k % 2):E * (k % 2) + E]
                    n = 0
                    for a, w in ((xT_hi, wq_hi), (xT_lo, wq_hi), (xT_hi, wq_lo)):
                        for f in range(FT):
                            ins = mm(o_ps, a[:, f, tokens(k)], w[:, f, :], start=n == 0, stop=n == 5)
                            n += 1
                    if k % 2:
                        ins.then_inc(q_ps.sem, 1)

            def project_out(d, c, second):
                if c is not None:
                    pe.wait_ge(q_evac.sem, q_evac.at(c))
                if second:
                    pe.wait_ge(w_lo["wo"].sem, 1)
                pe.wait_ge(oT_s.sem, oT_s.at(d))
                for k in range(TT):
                    o_ps = psX[:, k // 2, E * (k % 2):E * (k % 2) + E]
                    n = 0
                    for w in (wo_hi, wo_lo):
                        for g in range(NQ):
                            ins = mm(o_ps, oT[:, g, tokens(k)], w[:, g, :], start=n == 0, stop=n == 7)
                            n += 1
                    if k % 2:
                        ins.then_inc(wo_ps.sem, 1)

            def project_k(b):
                pe.wait_ge(ctxT_s.sem, ctxT_s.at(b))
                for o, n, rows in ((0, P, slice(0, P)), (E, SR, slice(P, S))):
                    for f in range(FT):
                        ins = mm(psF[0:n, 2, o:o + E], ctxT[:, f, rows], wkv_sb[:, f, 0:E], start=f == 0, stop=f == FT - 1)
                ins.then_inc(k_ps.sem, 1)

            def project_v(b):
                pe.wait_ge(k_evac.sem, k_evac.at(b))
                for f in range(FT):
                    mm(psF[:, 2, 0:E], ctxT[:, f, 0:P], wkv_sb[:, f, E:2 * E], start=f == 0, stop=f == FT - 1)
                for f in range(FT):
                    for j in range(4):
                        ins = mm(psF[32 * j:32 * j + SR, 2, E:2 * E], ctxT[:, f, P:S], wkv_sb[:, f, E:2 * E],
                                 start=f == 0, stop=f == FT - 1)
                ins.then_inc(v_ps.sem, 1)

            def router1(d, second=False):
                pe.wait_ge(x2T_hi_s.sem, x2T_hi_s.at(d))
                pe.wait_ge(x2T_lo_s.sem, x2T_lo_s.at(d))
                if second:
                    for n in ("w1", "w2a", "w2b", "a1", "lora1", "lora2"):
                        pe.wait_ge(w_lo[n].sem, 1)
                    pe.wait_ge(pv_t.sem, pv_t.at(d))
                for k in range(TT):
                    n = 0
                    for a, w in ((xT_hi, a1_hi), (xT_lo, a1_hi), (xT_hi, a1_lo)):
                        for f in range(FT):
                            ins = mm(psO[:, ZC * k:ZC * k + ZC], a[:, f, tokens(k)], w[:, f, :], start=n == 0, stop=n == 5)
                            n += 1
                ins.then_inc(z1_ps.sem, 1)

            def lora1_operand(d):
                pe.wait_ge(g1_v.sem, g1_v.at(d))
                for k in range(TT):
                    ins = nc.tensor.transpose(psO[0:LR, tokens(k)].bitcast(F32R), zs[:, 0, k, :], ident_r[:, :])
                ins.then_inc(z1T_ps.sem, 1)

            def hidden_main(d, m, second=False, parts=(0, 1)):
                if parts[0] == 0:
                    if m >= 3:
                        pe.wait_ge(w1_lo_s.sem, w1_lo_s.at(d, m - 2))
                    elif not second:
                        pe.wait_ge(y_out.sem, y_out.at(d - 1, m + 2))
                ops = [(a, w, f) for a, w in ((xT_hi, w1_hi), (xT_lo, w1_hi), (xT_hi, w1_lo)) for f in range(FT)]
                for n in range(3 * parts[0], 3 * parts[-1] + 3):
                    a, w, f = ops[n]
                    mm(psF[:, (m + 1) % 3, :], w[:, f, P * m:P * m + P], a[:, f, :], start=n == 0, stop=False)

            def hidden_lora(d, m):
                if m == 0:
                    pe.wait_ge(z1T_s.sem, z1T_s.at(d))
                mm(psF[:, (m + 1) % 3, :], lora_sb[:, P * m:P * m + P], zT[:, :], start=False, stop=True).then_inc(w1_ps.sem, 1)

            def key_transposes(b):
                pe.wait_ge(k_split.sem, k_split.at(b))
                for g in range(NG):
                    ins = nc.tensor.transpose(psX[0:KA, 2 + g // 4, tokens(g % 4)].bitcast(F32R), ks[:, 0, g, :], ident_r[:, :])
                    if g % 4 == 3:
                        ins.then_inc(km_ps.sem, 1)
                for g in range(NG):
                    ins = nc.tensor.transpose(psO[0:KA, 32 * g:32 * g + SR].bitcast(F32R), ks[0:SR, 1, g, :],
                                              ident_r[0:SR, 0:SR])
                ins.then_inc(km_ps.sem, 1)

            def q_transposes(c, g, u, b, first):
                if g == 0:
                    pe.wait_ge(q_lo.sem, q_lo.at(c))
                    pe.wait_ge(q_hi2.sem, q_hi2.at(c))
                elif g >= 4 and g % 2 == 0:
                    pe.wait_ge(qT_a.sem, qT_a.at(c, g // 2 - 1))
                elif g >= 4:
                    pe.wait_ge(qT_v.sem, qT_v.at(c, g // 2 - 1))
                for k in range(TT):
                    ins = nc.tensor.transpose(psX[0:KS, g % 4, tokens(k)].bitcast(F32R), qs[:, k, g, :], ident_r[:, :])
                ins.then_inc(qT_ps.sem, 1)

            def max_scores(c, i):
                k, gp = i // 4, i % 4
                if i == 0:
                    pe.wait_ge(qT_a.sem, qT_a.at(c, 3))
                    pe.wait_ge(qT_v.sem, qT_v.at(c, 3))
                elif i == 1:
                    pe.wait_ge(qT_a.sem, qT_a.at(c))
                    pe.wait_ge(qT_v.sem, qT_v.at(c))
                else:
                    pe.wait_ge(max_red.sem, max_red.at(c, i - 1))
                for j in range(2):
                    g = 2 * gp + j
                    ins = mm(psX[:, 2 * (i % 2) + j, 0:2 * S], qT[0:KS, g, tokens(k)],
                             km[0:KS, g, :, :].rearrange("p h s -> p (h s)"), start=True, stop=True)
                ins.then_inc(max_ps.sem, 1)

            def out_tile(d, k):
                if k == 0:
                    pe.wait_ge(w1_hi_s.sem, w1_hi_s.at(d))
                    pe.wait_ge(w1_lo_s.sem, w1_lo_s.at(d))
                if k == 3:
                    pe.wait_ge(y_out.sem, y_out.at(d, 1))
                n = 0
                for m in range(HT):
                    for a, w in ((h_hi, w2_hi), (h_lo, w2_hi), (h_hi, w2_lo)):
                        ins = mm(psF[:, F_OF_K[k], 0:W2N], a[:, m, tokens(k)], w[:, m, :], start=n == 0, stop=n == 23)
                        n += 1
                ins.then_inc(w2_ps.sem, 1)

            def lora2_operand(d, pr):
                pe.wait_ge(g2_v.sem, g2_v.at(d, 8 * pr + 8))
                if pr == 1:
                    pe.wait_ge(z2T_s.sem, z2T_s.at(d, 1))
                for j in range(2):
                    ins = nc.tensor.transpose(psO[0:LR, tokens(j)].bitcast(F32R), zs[:, 0, 2 * pr + j, :], ident_r[:, :])
                ins.then_inc(z2T_ps.sem, 1)

            def out_lora(d, pr):
                pe.wait_ge(z2T_s.sem, z2T_s.at(d, pr + 1))
                for k in (2 * pr, 2 * pr + 1):
                    mm(psF[:, F_OF_K[k], 0:E], zT[:, tokens(k)], lora_sb[:, HID:HID + E], start=False, stop=True,
                       skip_group_check=True).then_inc(y_ps.sem, 1)

            def max_transposed(c, first):
                pe.wait_ge(max_red.sem, max_red.at(c))
                if not first:
                    pe.wait_ge(z1T_s.sem, z1T_s.at(c - 1))
                for k in range(TT):
                    ins = nc.tensor.transpose(psO[0:H, tokens(k)].bitcast(F32R),
                                              max_t[:, k, :, :].rearrange("p h g -> p (h g)"), ident_r[:, :])
                ins.then_inc(maxT_ps.sem, 1)

            def scores(c, i):
                if i == 0:
                    pe.wait_ge(max_rows.sem, max_rows.at(c))
                if i >= 2:
                    pe.wait_ge(sc_exp.sem, sc_exp.at(c, i - 1))
                kind, n = SCORE_STEPS[i]
                for j in range(2):
                    o_ps = psX[:, 2 * (i % 2) + j, :]
                    if kind == "rest":
                        g = 2 * (n + j)
                        mm(o_ps, kr[:, g, :], qT[:, g, :], start=True, stop=False)
                        ins = mm(o_ps, kr[:, g + 1, :], qT[:, g + 1, :], start=False, stop=True)
                    else:
                        ins = mm(o_ps, km[:, n // 2, j, 0:P], qT[:, n // 2, :], start=True, stop=True)
                ins.then_inc(sc_ps.sem, 1)

            def values(c, g, first, last):
                pe.wait_ge(sc_exp.sem, sc_exp.at(c, PV_AFTER[g]))
                if g == 0:
                    pe.wait_ge(maxT_s.sem, maxT_s.at(c))
                    if first:
                        pe.wait_ge(const_v.sem, 6)
                if g == 2:
                    pe.wait_ge(pv_t.sem, pv_t.at(c, 1))
                if g % 2 and not last:
                    pe.wait_ge(xT_lo_s.sem, xT_lo_s.at(c + 1, g // 2 + 1))
                mm(pv_bank(g), vr_sb[:, g, :], probs_r[:, g, :], start=True, stop=False)
                for j in range(4):
                    h = 4 * g + j
                    ins = mm(pv_bank(g)[32 * j:32 * j + 32, :], v_sb[:, h, :], probs[:, h % 8, :], start=False, stop=True)
                ins.then_inc(pv_ps.sem, 1)

            def step(b, u, first=False, second=False, last=False):
                c = 2 * b + u
                d, e = c - 1, c - 2
                full = not first and not second
                project_q(c, first)
                if first:
                    pe.wait_ge(wkv_loaded.sem, 16)
                    project_k(b)
                if u == 0:
                    if not first:
                        pe.wait_ge(pv_t.sem, pv_t.at(d, 3))
                    key_transposes(b)
                    project_v(b)
                if full:
                    pe.wait_ge(pv_t.sem, pv_t.at(d, 3))
                    out_tile(e, 0)
                if not first:
                    project_out(d, c, second)
                if full:
                    pe.wait_ge(pv_t.sem, pv_t.at(d))
                    out_tile(e, 1)
                    if u == 0:
                        pe.wait_ge(v_evac.sem, v_evac.at(b))
                    out_tile(e, 2)
                if u == 0:
                    pe.wait_ge(km_v.sem, km_v.at(b))
                    pe.wait_ge(km_a.sem, km_a.at(b))
                if full:
                    lora2_operand(e, 0)
                    out_lora(e, 0)
                if not first:
                    transpose_x(d, psX[:, 2:4, :], ln2_out, x2T_ps)
                if full:
                    out_tile(e, 3)
                if first:
                    pe.wait_ge(q_evac.sem, q_evac.at(c))
                else:
                    pe.wait_ge(x1_s.sem, x1_s.at(d))
                    pe.wait_ge(x2T_hi_s.sem, x2T_hi_s.at(d))
                    pe.wait_ge(x2T_lo_s.sem, x2T_lo_s.at(d))
                for g in range(NG):
                    q_transposes(c, g, u, b, first)
                if full:
                    lora2_operand(e, 1)
                    out_lora(e, 1)
                    pe.wait_ge(z2T_s.sem, z2T_s.at(e))
                if not first:
                    router1(d, second)
                for i in range(16):
                    max_scores(c, i)
                    if not first and i < 14:
                        hidden_main(d, i // 2, second, (i % 2,))
                        if i == 3:
                            lora1_operand(d)
                            hidden_lora(d, 0)
                            hidden_lora(d, 1)
                        if i >= 5 and i % 2:
                            hidden_lora(d, i // 2)
                max_transposed(c, first)
                if not first:
                    hidden_main(d, 7)
                    hidden_lora(d, 7)
                if not last:
                    if not first:
                        pe.wait_ge(w1_lo_s.sem, w1_lo_s.at(d, 7))
                    transpose_x(c + 1, psF, ln1_out, xT_ps)
                for i in range(10):
                    scores(c, i)
                    if i == 1 and u == 1 and not last:
                        ctx_transposed(b + 1, ctx_sb)
                    if i == 6 and u == 1 and not last:
                        project_k(b + 1)
                    if i in PV_SLOT:
                        values(c, PV_SLOT[i], first, last)
                values(c, 3, first, last)

            pe.wait_ge(const_v.sem, 1)
            transpose_x(0, psF, ln1_out, xT_ps)
            ctx_transposed(0, ctx_0)
            step(0, 0, first=True)
            step(0, 1, second=True)
            with pe.Fori(1, B - 1) as b:
                step(b, 0)
                step(b, 1)
            step(B - 1, 0)
            step(B - 1, 1, last=True)
            d, e = LAST, LAST - 1
            pe.wait_ge(pv_t.sem, pv_t.at(d, 3))
            out_tile(e, 0)
            project_out(d, None, False)
            pe.wait_ge(pv_t.sem, pv_t.at(d))
            out_tile(e, 1)
            out_tile(e, 2)
            lora2_operand(e, 0)
            out_lora(e, 0)
            transpose_x(d, psX[:, 2:4, :], ln2_out, x2T_ps)
            out_tile(e, 3)
            lora2_operand(e, 1)
            out_lora(e, 1)
            router1(d)
            hidden_main(d, 0)
            hidden_main(d, 1)
            lora1_operand(d)
            hidden_lora(d, 0)
            hidden_lora(d, 1)
            for m in range(2, HT):
                hidden_main(d, m)
                hidden_lora(d, m)
            for k in range(TT):
                out_tile(d, k)
                if k == 2:
                    lora2_operand(d, 0)
                    out_lora(d, 0)
            lora2_operand(d, 1)
            out_lora(d, 1)


SCORE_STEPS = [("rest", 0), ("main", 0), ("main", 2), ("main", 4), ("main", 6),
               ("rest", 2), ("main", 8), ("main", 10), ("main", 12), ("main", 14)]
PV_AFTER = [3, 5, 8, 10]
PV_SLOT = {3: 0, 5: 1, 8: 2}
LAST = B * UB - 1
F_OF_K = [0, 1, 2, 0]


def position_tables():
    f = np.float32
    base = (np.arange(0, D, 2, dtype=f) + f(0.4 * D)) / f(1.4 * D)
    inv = (f(1.0) / f(10000.0) ** (np.arange(D // 2, dtype=f) / f(D // 2))).astype(f)

    def cs(pos, down):
        pos = pos.astype(f)
        scale = (base[None, :] ** (pos[:, None] / f(E))).astype(f)
        if down:
            scale = (f(1.0) / scale).astype(f)
        ang = pos[:, None] * inv[None, :]
        c, s = np.cos(ang).astype(f) * scale, np.sin(ang).astype(f) * scale
        return np.concatenate([c, c], 1), np.concatenate([-s, s], 1)

    u, p, k = np.meshgrid(np.arange(UB), np.arange(P), np.arange(TT), indexing="ij")
    pos = (CH * u + TT * p + k).transpose(1, 0, 2).reshape(-1)
    cq, sq = (t.reshape(P, -1) * f(D ** -0.5) for t in cs(pos, False))
    pos = (np.arange(P)[:, None] + P * np.arange(2)[None, :]).reshape(-1)
    ck, sk = (t.reshape(P, -1) for t in cs(pos, True))
    r = np.arange(P)
    head = np.where(r < KS, (r % 32) // D, r - KS)
    mask = np.stack([(head == 0), (head == 1)], 1).astype(f)
    return np.concatenate([cq, sq, ck, sk], 1).astype(f), mask


def kernel(**inputs):
    import numpy as _np
    import concourse.bacc as _bacc
    from concourse.bass_utils import run_bass_kernel_spmd as _run

    i = {n: _np.asarray(a) for n, a in inputs.items()}
    perm = _np.arange(E).reshape(H, D // 2, 2).transpose(0, 2, 1).reshape(-1)
    wq = i["L0_xattn_Wq"].T[:, perm].reshape(FT, P, E).transpose(1, 0, 2).reshape(P, -1)
    wkv = _np.concatenate([i["L0_xattn_Wk"].T[:, perm], i["L0_xattn_Wv"].T], 1)
    wo = i["L0_xattn_Wo"].T.reshape(NQ, 4, 1, D, E)
    wo = _np.broadcast_to(wo, (NQ, 4, 2, D, E)).reshape(NQ, P, E).transpose(1, 0, 2).reshape(P, -1)
    w1 = i["L0_ffn_W1"].reshape(FT, P, HID).transpose(1, 0, 2).reshape(P, -1)

    def lora_router(a, r):
        n = a.shape[1]
        return _np.concatenate([a.transpose(1, 0, 2).reshape(n, NL), r, _np.zeros((n, 1), r.dtype)], 1)

    a1 = lora_router(i["L0_ffn_A1"], i["L0_ffn_R1"]).reshape(FT, P, ZC).transpose(1, 0, 2).reshape(P, -1)
    w2 = _np.concatenate([i["L0_ffn_W2"], lora_router(i["L0_ffn_A2"], i["L0_ffn_R2"])], 1)
    w2 = w2.reshape(HT, P, W2N).transpose(1, 0, 2).reshape(P, -1)
    lora = _np.zeros((LR, HID + E), _np.float32)
    lo = _np.concatenate([i["L0_ffn_B1"].reshape(NL, HID), i["L0_ffn_B2"].reshape(NL, E)], 1)
    bias = _np.concatenate([i["L0_ffn_b1"], i["L0_ffn_b2"]])
    for r in (0, 32, 64):
        lora[r:r + NL] = lo
    for r in (0, 64):
        lora[r + NL] = bias
    pos, mask = position_tables()
    rows = _np.concatenate([i["L0_xattn_bq"][perm], i["L0_xattn_bk"][perm], i["L0_xattn_bv"], i["L0_xattn_bo"],
                            i["g_xattn"], i["g_ffn"]])
    tables = _np.concatenate([pos, _np.broadcast_to(rows, (P, rows.size)), mask], 1)

    arrays = {"x": i["x"], "ctx": i["ctx_1024"], "wq": wq, "wkv": wkv, "wo": wo, "w1": w1, "w2": w2, "a1": a1,
              "lora": lora, "tables": tables}
    arrays = {f"in_{n}_dram": _np.ascontiguousarray(a) for n, a in arrays.items()}
    nc = _bacc.Bacc("TRN2", target_bir_lowering=False, num_devices=1)
    args = [nc.dram_tensor(n, a.shape, mybir.dt.from_np(a.dtype), kind="ExternalInput").ap()
            for n, a in arrays.items()]
    args.append(nc.dram_tensor("out_0_dram", (B, T, E), F32, kind="ExternalOutput").ap())
    build(nc, *args)
    r = _run(nc, [arrays], core_ids=[0])
    return r.results[0]["out_0_dram"]
```

```python
from contextlib import ExitStack

import numpy as np

import concourse.bass as bass
from concourse import mybir

F32 = mybir.dt.float32
F32R = mybir.dt.float32r
ACT = mybir.ActivationFunctionType
ALU = mybir.AluOpType
AX = mybir.AxisListType

B, T, E, S, H = 4, 1024, 256, 154, 16
D = E // H
HID, NE, R = 1024, 3, 8
P = 128
CH = 512
UB = T // CH
TT = CH // P
FT = E // P
HT = HID // P
NG = H // 2
NQ = H // 4
SR = S - P
ZC = 28
NL = NE * R
W2N = E + ZC
KS = 96
KA = KS + 2
LR = 96
EPS = 1e-5
DSEL = 16


class Count:

    def __init__(self, sem, per):
        self.sem, self.per = sem, per

    def at(self, n, k=None):
        return self.per * n + (self.per if k is None else k)


def build(nc, x, ctx_in, wq, wkv, wo, w1, w2, a1, lora, tables, out):
    with ExitStack() as stack:
        def sb(name, shape, dt=F32):
            return stack.enter_context(nc.sbuf_tensor(name, shape, dt))

        def count(name, per):
            return Count(stack.enter_context(nc.semaphore(name)), per)

        x_ln = sb("x_ln", [P, TT, E])
        x1 = sb("x1", [P, 2, TT, E])
        xn = sb("xn", [P, TT, E])
        xT_hi = sb("xT_hi", [P, FT, CH], F32R)
        xT_lo = sb("xT_lo", [P, FT, CH], F32R)
        split = sb("split", [P, TT * NG * KS], F32R)
        qs = split[:, :].rearrange("p (k g r) -> p k g r", k=TT, g=NG)
        ns = split[:, 0:NQ * 512].rearrange("p (g c r) -> p g c r", g=NQ, r=32)
        oT = split[:, 0:NQ * 512].rearrange("p (g t) -> p g t", g=NQ)
        heads_t = sb("heads_t", [P, NQ, 16, 32])
        qT = sb("qT", [KA, NG, CH], F32R)
        max_t = sb("max_t", [P, TT, 2, H // 2], F32R)
        max_f = split[0:H // 2, NQ * 512:].rearrange("p (f t) -> p f t", f=2)
        probs = sb("probs", [P, 8, CH])
        probs_r = sb("probs_r", [P, NQ, CH])
        q_ev = probs[:, 0:2, :].rearrange("p a (k e) -> p (a k) e", e=E)
        q_rc = probs[:, 2:4, :].rearrange("p a (k e) -> p (a k) e", e=E)
        q_rs = probs[:, 4:6, :].rearrange("p a (k e) -> p (a k) e", e=E)
        zT = sb("zT", [LR, CH], F32R)
        h_hi = sb("h_hi", [P, HT, CH], F32R)
        h_lo = sb("h_lo", [P, HT, CH], F32R)
        wq_hi, wq_lo = (sb(f"wq_{n}", [P, FT, E], F32R) for n in ("hi", "lo"))
        wkv_sb = sb("wkv_sb", [P, FT, 2 * E])
        wo_hi, wo_lo = (sb(f"wo_{n}", [P, NQ, E], F32R) for n in ("hi", "lo"))
        a1_sb = sb("a1_sb", [P, FT, 32])
        w1_hi, w1_lo = (sb(f"w1_{n}", [P, FT, HID], F32R) for n in ("hi", "lo"))
        w2_hi, w2_lo = (sb(f"w2_{n}", [P, HT, W2N], F32R) for n in ("hi", "lo"))
        lora_sb = sb("lora_sb", [LR, HID + E], F32R)
        km = sb("km", [KA, NG, 2, S], F32R)
        kr = sb("kr", [KA, NG, P], F32R)
        v_sb = sb("v_sb", [P, H, 32])
        vr_sb = sb("vr_sb", [P, NQ, P])
        ks = sb("ks", [P, 2, NG, KA], F32R)
        ctx_sb, k_rc, k_ev, k_rs = x_ln[:, 0:2, :], x_ln[:, 0:2, :], x_ln[:, 2:4, :], xn[:, 0:2, :]
        ctxT = sb("ctxT", [P, FT, S])
        tab = sb("tab", [P, tables.shape[1]])
        ident_r = sb("ident_r", [P, P], F32R)
        ln_s = sb("ln_s", [P, 2, TT, 6])
        ln_m = sb("ln_m", [P, 2, TT, 2])
        ln_v = sb("ln_v", [P, 2, TT])
        ln_r = sb("ln_r", [P, 2, TT])
        ln_n = sb("ln_n", [P, 2, TT])
        ln_b = sb("ln_b", [P, 2, TT])
        half = sb("half", [P, TT])
        eps = sb("eps", [P, TT])
        pace = sb("pace", [P, 1])
        gate = sb("gate", [P, 2])
        den = sb("den", [P, NQ, 16])
        zc = sb("zc", [P, TT, 32])
        zmax = sb("zmax", [P, TT])
        zsh = sb("zsh", [P, TT, NE])
        zex = sb("zex", [P, TT, NE])
        zsum = sb("zsum", [P, TT])
        zrec = sb("zrec", [P, TT])
        zw = sb("zw", [P, TT, NE])
        zg = sb("zg", [P, TT, NL])
        zs = sb("zs", [P, TT, LR], F32R)

        o = 0

        def cols(n):
            nonlocal o
            o += n
            return tab[:, o - n:o]

        cos_q = cols(UB * TT * D).rearrange("p (u k d) -> p u k d", u=UB, k=TT)
        sin_q = cols(UB * TT * D).rearrange("p (u k d) -> p u k d", u=UB, k=TT)
        cos_k = cols(2 * D).rearrange("p (a d) -> p a d", a=2)
        sin_k = cols(2 * D).rearrange("p (a d) -> p a d", a=2)
        bq_b, bk_b, bv_b, bo_b = cols(E), cols(E), cols(E), cols(E)
        g_b, mask = cols(2), cols(2)

        psX = stack.enter_context(nc.psum_tensor("psX", [P, 4, CH], F32))
        psF = stack.enter_context(nc.psum_tensor("psF", [P, 3, CH], F32))
        psO = stack.enter_context(nc.psum_tensor("psO", [P, CH], F32))

        def pv_bank(g):
            return psF[:, g // 2, :] if g % 2 else psO[:, :]

        x_loaded = count("x_loaded", 16)
        x1_loaded = [count(f"x1_loaded{u}", 16) for u in range(2)]
        ctx_loaded = count("ctx_loaded", 32)
        tab_loaded = count("tab_loaded", 16)
        wkv_loaded = count("wkv_loaded", 16)
        w_loaded = {n: count(f"{n}_loaded", 16) for n in ("wq", "wo", "w1", "w2a", "w2b", "lora1", "lora2")}
        a1_loaded = count("a1_loaded", 16)
        w_hi = {n: count(f"{n}_hi", 1) for n in w_loaded}
        w_lo = {n: count(f"{n}_lo", 1) for n in w_loaded}
        const_p = count("const_p", 1)
        const_v = count("const_v", 1)
        gate_ready = count("gate_ready", 1)
        gbo_ready = count("gbo_ready", 1)
        ln1_stat, ln1_agg = count("ln1_stat", TT), count("ln1_agg", TT)
        ln1_eps, ln1_rstd, ln1_out = count("ln1_eps", 1), count("ln1_rstd", 2), count("ln1_out", TT)
        ln2_stat, ln2_agg = count("ln2_stat", TT), count("ln2_agg", TT)
        ln2_eps, ln2_rstd, ln2_out = count("ln2_eps", 1), count("ln2_rstd", 2), count("ln2_out", TT)
        xb_ready = count("xb_ready", 1)
        xT_ps, xT_lo_s = count("xT_ps", FT), count("xT_lo_s", FT)
        xT_hi_a, xT_hi_v = count("xT_hi_a", 1), count("xT_hi_v", 1)
        x2T_ps, x2T_hi_s, x2T_lo_s = count("x2T_ps", FT), count("x2T_hi_s", FT), count("x2T_lo_s", FT)
        q_ps, q_evac = count("q_ps", 2), count("q_evac", 2)
        q_cos, q_sin, q_rot = count("q_cos", 1), count("q_sin", TT), count("q_rot", 1)
        q_hi, q_hi2, q_lo = count("q_hi", 1), count("q_hi2", 1), count("q_lo", 1)
        qT_ps, qT_a, qT_v = count("qT_ps", NG), count("qT_a", NG // 2), count("qT_v", NG // 2)
        max_ps, max_red = count("max_ps", TT * NG // 2), count("max_red", TT * NG // 2)
        maxT_ps = count("maxT_ps", 2)
        maxT_s, max_rows = ([count(f"{n}{f}", per) for f in range(2)] for n, per in (("maxT_s", 1), ("max_rows", 32)))
        sc_ps, sc_exp = count("sc_ps", 10), count("sc_exp", 10)
        pv_ps, pv_t = count("pv_ps", NQ), count("pv_t", NQ)
        den_inv, o_norm = count("den_inv", 2), count("o_norm", 2)
        o_hi, o_lo, o_back = count("o_hi", 2), count("o_lo", 2), count("o_back", 2)
        oT_s = count("oT_s", 2)
        wo_ps, x1_s = count("wo_ps", 2), count("x1_s", 2)
        z1_ps, g1_v, g1_e = count("z1_ps", 1), count("g1_v", 9), count("g1_e", 1)
        z1T_ps, z1T_s = count("z1T_ps", 1), count("z1T_s", 1)
        w1_ps, w1_hi_s, w1_lo_s = count("w1_ps", HT), count("h_hi_s", HT), count("h_lo_s", HT)
        w2_ps = count("w2_ps", TT)
        g2_c, g2_v, g2_e = count("g2_c", TT), count("g2_v", 16), count("g2_e", 2)
        z2T_ps, z2T_s = count("z2T_ps", 2), count("z2T_s", 2)
        y_ps, y_out, stored = count("y_ps", TT), count("y_out", TT), count("stored", 16)
        ctxT_ps, ctxT_s = count("ctxT_ps", 1), count("ctxT_s", 1)
        k_ps, k_evac = count("k_ps", 1), count("k_evac", 2)
        v_ps, v_evac = count("v_ps", 1), count("v_evac", 5)
        k_rot, k_split = count("k_rot", 4), count("k_split", 2)
        km_ps, km_v, km_a = count("km_ps", 3), count("km_v", 4), count("km_a", 4)

        x_d = x.rearrange("b (u p k) e -> b u p k e", u=UB, k=TT)
        out_d = out.rearrange("b (u p k) e -> b u p k e", u=UB, k=TT)

        q6, q7 = probs[:, 6, :], probs[:, 7, :]
        flat_h = heads_t[:, :, :, :].rearrange("p a b c -> p (a b c)")
        x1_0, x1_1 = (x1[:, u, :, :].rearrange("p k e -> p (k e)") for u in range(UB))
        n_w2 = (HT - 1) * W2N
        staged = {"wq": q6, "wo": x1_1, "w1": flat_h, "w2a": flat_h[:, 0:n_w2],
                  "w2b": q6[:, 0:W2N], "lora1": x1_0[0:LR, :], "lora2": q7[0:LR, 256:256 + E]}
        ident_0 = q7[:, 128:256]
        ctx_0 = probs_r[:, 3, :].rearrange("p (a e) -> p a e", a=2)
        halves = {n: [t[:, :, :].rearrange("p a b -> p (a b)") for t in pair] for n, pair in
                  {"w1": (w1_hi, w1_lo), "wo": (wo_hi, wo_lo), "w2": (w2_hi, w2_lo),
                   "wq": (wq_hi, wq_lo)}.items()}
        halves["w2a"], halves["w2b"] = ([t[:, 0:n_w2] for t in halves["w2"]], [t[:, n_w2:] for t in halves["w2"]])
        halves["lora1"], halves["lora2"] = ([t, t[64:LR, :]] for t in (lora_sb[:, 0:HID], lora_sb[:, HID:HID + E]))

        def low_args(n):
            hi, lo = halves[n]
            if n in ("lora1", "lora2"):
                return dict(out=lo, in0=staged[n][64:LR, :], in1=hi[64:LR, :].bitcast(F32), op=ALU.subtract)
            return dict(out=lo, in0=staged[n], in1=hi.bitcast(F32), op=ALU.subtract)

        block = stack.enter_context(nc.Block())

        @block.sync
        def _(sp):
            sp.dma_start(x_ln[:, :, :], x_d[0, 0]).then_inc(x_loaded.sem, 16)

            def stage(n, src):
                sp.dma_start(staged[n], src).then_inc(w_loaded[n].sem, 16)

            stage("wq", wq)
            sp.dma_start(tab[:, :], tables).then_inc(tab_loaded.sem, 16)
            sp.dma_start(ctx_0[:, 0, :], ctx_in[0, 0:P]).then_inc(ctx_loaded.sem, 16)
            sp.dma_start(ctx_0[0:SR, 1, :], ctx_in[0, P:S]).then_inc(ctx_loaded.sem, 16)
            stage("w1", w1)
            sp.dma_start(wkv_sb[:, :, :], wkv.rearrange("(f p) n -> p f n", p=P)).then_inc(wkv_loaded.sem, 16)
            stage("wo", wo)
            sp.dma_start(a1_sb[:, :, :], a1.rearrange("p (f z) -> p f z", f=FT)).then_inc(a1_loaded.sem, 16)
            stage("lora1", lora[:, 0:HID])
            stage("lora2", lora[:, HID:HID + E])
            sp.wait_ge(w_lo["w1"].sem, 1)
            stage("w2a", w2[:, 0:n_w2])
            sp.wait_ge(w_lo["wq"].sem, 1)
            stage("w2b", w2[:, n_w2:n_w2 + W2N])

            def rows_of_maxima(c):
                for f in range(2):
                    sp.wait_ge(maxT_s[f].sem, maxT_s[f].at(c))
                    for hh in range(2):
                        sp.dma_start(qT[KS + hh:KS + hh + 1, 4 * f:4 * f + 4, :].bitcast(F32),
                                     max_f[4 * hh:4 * hh + 4, f, :].bitcast(F32)).then_inc(max_rows[f].sem, 16)

            rows_of_maxima(0)
            rows_of_maxima(1)
            with sp.Fori(1, B) as b:
                rows_of_maxima(2 * b)
                rows_of_maxima(2 * b + 1)

        @block.gpsimd
        def _(pool):
            nc.gpsimd.memset(ident_0, 0.0).then_inc(const_p.sem, 1)
            pool.wait_ge(const_p.sem, 1)
            nc.gpsimd.affine_select(out=ident_0, in_=ident_0, compare_op=ALU.not_equal, fill=1.0,
                                    base=0, pattern=[[-1, P]], channel_multiplier=1).then_inc(const_p.sem, 1)
            nc.gpsimd.memset(half[:, :], -0.5).then_inc(const_p.sem, 1)
            nc.gpsimd.memset(eps[:, :], EPS)
            nc.gpsimd.memset(zs[:, :, :].bitcast(F32), 0.0).then_inc(const_p.sem, 1)
            pool.wait_ge(const_p.sem, 4)
            nc.gpsimd.memset(zs[:, :, NL:NL + 1].bitcast(F32), 1.0)
            nc.gpsimd.memset(zs[:, :, 64 + NL:65 + NL].bitcast(F32), 1.0).then_inc(const_p.sem, 1)

            def rstd(which, agg, eps_s, out_s, c):
                pool.wait_ge(agg.sem, agg.at(c))
                nc.gpsimd.tensor_tensor(ln_v[:, which, :], ln_m[:, which, :, 1], eps[:, :], ALU.add)
                nc.gpsimd.tensor_scalar(ln_n[:, which, :], ln_m[:, which, :, 0], -1.0, None,
                                        ALU.mult).then_inc(eps_s.sem, 1)
                pool.wait_ge(eps_s.sem, eps_s.at(c))
                nc.gpsimd.tensor_tensor(ln_r[:, which, :], ln_v[:, which, :], half[:, :],
                                        ALU.pow).then_inc(out_s.sem, 1)
                pool.wait_ge(out_s.sem, out_s.at(c, 1))
                nc.gpsimd.tensor_tensor(ln_b[:, which, :], ln_n[:, which, :], ln_r[:, which, :],
                                        ALU.mult).then_inc(out_s.sem, 1)

            def residual_base(b, u):
                pool.wait_ge(x1_loaded[u].sem, x1_loaded[u].at(b))
                for k in range(TT):
                    ins = nc.gpsimd.tensor_tensor(x1[:, u, k], x1[:, u, k], bo_b, ALU.add)
                ins.then_inc(xb_ready.sem, 1)

            def stage_low(n):
                pool.wait_ge(w_hi[n].sem, 1)
                nc.gpsimd.tensor_tensor(**low_args(n)).then_inc(w_lo[n].sem, 1)

            def step(b, u, first=False, last=False):
                c = 2 * b + u
                pool.wait_ge(q_evac.sem, q_evac.at(c))
                nc.gpsimd.tensor_tensor(
                    q_rc.rearrange("p k (h d) -> p k h d", d=D), q_ev.rearrange("p k (h d) -> p k h d", d=D),
                    cos_q[:, u].unsqueeze(2).to_broadcast([P, TT, H, D]), ALU.mult).then_inc(q_cos.sem, 1)
                if not first:
                    rstd(1, ln2_agg, ln2_eps, ln2_rstd, c - 1)
                if first:
                    for n in ("wo", "lora1", "lora2"):
                        stage_low(n)
                        pool.wait_ge(w_lo[n].sem, 1)
                if not last:
                    rstd(0, ln1_agg, ln1_eps, ln1_rstd, c + 1)
                if first:
                    stage_low("w2a")
                    stage_low("w2b")
                residual_base(b, u)

            rstd(0, ln1_agg, ln1_eps, ln1_rstd, 0)
            stage_low("w1")
            pool.wait_ge(gbo_ready.sem, 1)
            step(0, 0, first=True)
            step(0, 1)
            with pool.Fori(1, B - 1) as b:
                step(b, 0)
                step(b, 1)
            step(B - 1, 0)
            step(B - 1, 1, last=True)
            rstd(1, ln2_agg, ln2_eps, ln2_rstd, 2 * B - 1)

        @block.scalar
        def _(act):
            def copy(out_ap, in_ap, **kw):
                return nc.scalar.activation(out_ap, in_ap, ACT.Copy, **kw)

            def stage_high(n):
                act.wait_ge(w_loaded[n].sem, 16)
                copy(halves[n][0], staged[n]).then_inc(w_hi[n].sem, 1)

            def norm_hi(c, f2):
                act.wait_ge(o_norm.sem, o_norm.at(c, f2 + 1))
                copy(ns[:, 2 * f2:2 * f2 + 2, :, 0:D].rearrange("p g c d -> p (g c) d"),
                     heads_t[:, 2 * f2:2 * f2 + 2, :, 0:D].rearrange("p g c d -> p (g c) d")).then_inc(o_hi.sem, 1)

            def heads_back(c, f2):
                act.wait_ge(o_back.sem, o_back.at(c, f2 + 1))
                copy(oT[:, 2 * f2:2 * f2 + 2, :], heads_t[:, 2 * f2:2 * f2 + 2, :, :]
                     .rearrange("p g c r -> p g (c r)")).then_inc(oT_s.sem, 1)

            def store(b, u, e):
                act.wait_ge(y_out.sem, y_out.at(e))
                act.dma_start(out_d[b, u], x1[:, u]).then_inc(stored.sem, 16)

            def load(b, u, c):
                act.wait_ge(ln1_out.sem, ln1_out.at(c - 1))
                if u:
                    act.wait_ge(k_split.sem, k_split.at(b))
                act.dma_start(x_ln[:, :, :], x_d[b, u]).then_inc(x_loaded.sem, 16)

            def reload(b, u, c, full):
                if full:
                    act.wait_ge(stored.sem, stored.at(c - 2))
                else:
                    n = "wo" if u else "lora1"
                    act.wait_ge(w_lo[n].sem, 1)
                act.dma_start(x1[:, u], x_d[b, u]).then_inc(x1_loaded[u].sem, 16)

            def load_ctx(b, c):
                act.wait_ge(ln1_out.sem, ln1_out.at(c + 1))
                act.dma_start(ctx_sb[:, 0, :], ctx_in[b, 0:P]).then_inc(ctx_loaded.sem, 16)
                act.dma_start(ctx_sb[0:SR, 1, :], ctx_in[b, P:S]).then_inc(ctx_loaded.sem, 16)

            def xT_high(c):
                act.wait_ge(xT_ps.sem, xT_ps.at(c, 1))
                copy(xT_hi[:, 0, :], psF[:, 0, :]).then_inc(xT_hi_a.sem, 1)

            def x2T_high(d):
                for f in range(FT):
                    act.wait_ge(x2T_ps.sem, x2T_ps.at(d, f + 1))
                    copy(xT_hi[:, f, :], psX[:, 2 + f, :]).then_inc(x2T_hi_s.sem, 1)

            def ctx_copy(b):
                act.wait_ge(ctxT_ps.sem, ctxT_ps.at(b))
                copy(ctxT[:, :, :], psF[:, 2, 0:2 * S].rearrange("p (f s) -> p f s", f=FT)).then_inc(ctxT_s.sem, 1)

            def normalise(which, src, c, rstd, done, free):
                act.wait_ge(rstd.sem, rstd.at(c))
                if free is not None:
                    act.wait_ge(free[0].sem, free[0].at(free[1]))
                for k in range(TT):
                    nc.scalar.activation(xn[:, k, :], src[:, k, :], ACT.Identity, bias=ln_b[:, which, k:k + 1],
                                         scale=ln_r[:, which, k:k + 1]).then_inc(done.sem, 1)

            def key_operands(b):
                act.wait_ge(km_ps.sem, km_ps.at(b, 2))
                for hh in range(2):
                    copy(km[:, 4:8, hh, 0:P], psX[0:KA, 3, :].rearrange("p (g s) -> p g s", g=4),
                         scale=mask[0:KA, hh:hh + 1]).then_inc(km_a.sem, 1)
                act.wait_ge(km_ps.sem, km_ps.at(b, 3))
                rest = psO[0:KA, 0:NG * 32].rearrange("p (g s) -> p g s", g=NG)[:, :, 0:SR]
                for hh in range(2):
                    for a in range(2):
                        ins = copy(kr[:, a::2, 64 * a + 32 * hh:64 * a + 32 * hh + SR], rest[:, a::2, :],
                                   scale=mask[0:KA, hh:hh + 1])
                    ins.then_inc(km_a.sem, 1)

            def relu(d, m):
                act.wait_ge(w1_ps.sem, w1_ps.at(d, m + 1))
                nc.scalar.activation(h_hi[:, m, :], psF[:, (m + 1) % 3, :], ACT.Relu).then_inc(w1_hi_s.sem, 1)

            def maxima_copy(c):
                act.wait_ge(maxT_ps.sem, maxT_ps.at(c, 1))
                copy(max_f[:, 0, :], psO[0:H // 2, :], scale=-1.0).then_inc(maxT_s[0].sem, 1)

            def gate2_exp(e, pr):
                act.wait_ge(g2_v.sem, g2_v.at(e, 8 * pr + 2))
                nc.scalar.activation(zex[:, 2 * pr:2 * pr + 2], zsh[:, 2 * pr:2 * pr + 2],
                                     ACT.Exp).then_inc(g2_e.sem, 1)

            def gate2_copy(e, pr):
                act.wait_ge(z2T_ps.sem, z2T_ps.at(e, pr + 1))
                copy(zT[:, 256 * pr:256 * pr + 256], psO[0:LR, 0:256]).then_inc(z2T_s.sem, 1)

            def gate1_exp(d):
                act.wait_ge(g1_v.sem, g1_v.at(d, 3))
                nc.scalar.activation(zex[:, :, :], zsh[:, :, :], ACT.Exp).then_inc(g1_e.sem, 1)

            def gate1_copy(d):
                act.wait_ge(z1T_ps.sem, z1T_ps.at(d))
                copy(zT[:, :], psO[0:LR, :]).then_inc(z1T_s.sem, 1)

            def step(b, u, first=False, second=False, last=False):
                c = 2 * b + u
                d, e = c - 1, c - 2
                full = not first and not second
                if full and not last:
                    load(b + u, 1 - u, c + 1)
                if first:
                    load(0, 1, 1)
                if u == 0:
                    key_operands(b)
                if full:
                    gate2_exp(e, 0)
                if full:
                    gate2_copy(e, 0)
                act.wait_ge(q_rot.sem, q_rot.at(c))
                if not first:
                    act.wait_ge(wo_ps.sem, wo_ps.at(d))
                for lo, done in ((0, q_hi), (64, q_hi2)):
                    copy(split[:, :].rearrange("p (a r) -> p a r", r=KS)[:, :, lo:lo + 32],
                         q_rc.rearrange("p k (g r) -> p (k g) r", r=32)).then_inc(done.sem, 1)
                if not first:
                    normalise(1, x1[:, 1 - u], d, ln2_rstd, ln2_out, (xT_ps, c))
                if full:
                    gate2_exp(e, 1)
                if not first:
                    x2T_high(d)
                for g in range(0, NG, 2):
                    act.wait_ge(qT_ps.sem, qT_ps.at(c, g + 1))
                    copy(qT[0:KS, g, :], psX[0:KS, g % 4, :]).then_inc(qT_a.sem, 1)
                    if full and g == 0:
                        gate2_copy(e, 1)
                    if not first and g == 0:
                        gate1_exp(d)
                if not first:
                    gate1_copy(d)
                    for m in range(HT):
                        relu(d, m)
                        if m == 3:
                            maxima_copy(c)
                            if full:
                                store(b - 1, u, e)
                        if m == 5 and not last:
                            normalise(0, x_ln, c + 1, ln1_rstd, ln1_out, (x2T_ps, d))
                else:
                    for n in ("wo", "lora1", "lora2", "w2a", "w2b"):
                        stage_high(n)
                    normalise(0, x_ln, c + 1, ln1_rstd, ln1_out, (xT_ps, c))
                    maxima_copy(c)
                reload(b, u, c, full)
                if u == 1 and not last:
                    load_ctx(b + 1, c)
                if first:
                    for n in ("w2b", "lora2"):
                        act.wait_ge(w_lo[n].sem, 1)
                for i, (kind, n) in enumerate(SCORE_STEPS):
                    act.wait_ge(sc_ps.sem, sc_ps.at(c, i + 1))
                    if kind == "rest":
                        dst = probs_r[:, n:n + 2, :]
                    else:
                        dst = probs[:, n % 8:n % 8 + 2, :]
                        if n >= 8:
                            act.wait_ge(pv_ps.sem, pv_ps.at(c, n // 4 - 1))
                    nc.scalar.activation(dst, psX[:, 2 * (i % 2):2 * (i % 2) + 2, :], ACT.Exp).then_inc(sc_exp.sem, 1)
                    if i == 2 and not last:
                        xT_high(c + 1)
                    if i == 4 and not last and u == 1:
                        ctx_copy(b + 1)
                for f2 in range(2):
                    norm_hi(c, f2)
                    heads_back(c, f2)

            stage_high("wq")
            normalise(0, x_ln, 0, ln1_rstd, ln1_out, None)
            xT_high(0)
            act.wait_ge(tab_loaded.sem, 16)
            nc.scalar.activation(gate[:, :], g_b, ACT.Tanh).then_inc(gate_ready.sem, 1)
            ctx_copy(0)
            stage_high("w1")
            step(0, 0, first=True)
            load(1, 0, 2)
            step(0, 1, second=True)
            with act.Fori(1, B - 1) as b:
                step(b, 0)
                step(b, 1)
            step(B - 1, 0)
            step(B - 1, 1, last=True)
            d = 2 * B - 1
            gate2_exp(d - 1, 0)
            gate2_copy(d - 1, 0)
            normalise(1, x1[:, 1], d, ln2_rstd, ln2_out, None)
            gate2_exp(d - 1, 1)
            x2T_high(d)
            gate2_copy(d - 1, 1)
            gate1_exp(d)
            gate1_copy(d)
            for m in range(HT):
                relu(d, m)
            store(B - 1, 0, d - 1)
            for pr in range(2):
                gate2_exp(d, pr)
                gate2_copy(d, pr)
            for pr in range(2):
                act.wait_ge(y_out.sem, y_out.at(d, 2 * pr + 2))
                act.dma_start(out_d[B - 1, 1][:, 2 * pr:2 * pr + 2], x1[:, 1, 2 * pr:2 * pr + 2]).then_inc(stored.sem, 16)
            act.wait_ge(stored.sem, stored.at(d) + 16)

        @block.vector
        def _(dve):
            V = nc.vector

            def statistics(which, src, c, stat, agg):
                for k in range(TT):
                    V.bn_stats(ln_s[:, which, k, :], src[:, k, :]).then_inc(stat.sem, 1)
                dve.wait_ge(stat.sem, stat.at(c))
                V.memset(pace[:, :], 0.0)
                for k in range(TT):
                    V.bn_aggr(ln_m[:, which, k, :], ln_s[:, which, k, :]).then_inc(agg.sem, 1)

            def ln1_stats(c):
                dve.wait_ge(x_loaded.sem, x_loaded.at(c))
                statistics(0, x_ln, c, ln1_stat, ln1_agg)

            def gates_shift(v, n, i, K):
                nk = K.stop - K.start
                V.tensor_reduce(zmax[:, K], zc[:, K, NL:NL + NE], AX.X, ALU.max).then_inc(v.sem, 1)
                dve.wait_ge(v.sem, v.at(n, i + 1))
                V.tensor_tensor(zsh[:, K], zc[:, K, NL:NL + NE],
                                zmax[:, K].unsqueeze(2).to_broadcast([P, nk, NE]), ALU.subtract).then_inc(v.sem, 1)

            def gates_weigh(v, e, n, i, K, e_done):
                nk = K.stop - K.start
                dve.wait_ge(e.sem, e_done)
                V.reduce_sum(zsum[:, K], zex[:, K], AX.X).then_inc(v.sem, 1)
                dve.wait_ge(v.sem, v.at(n, i + 3))
                V.reciprocal(zrec[:, K], zsum[:, K]).then_inc(v.sem, 1)
                dve.wait_ge(v.sem, v.at(n, i + 4))
                V.scalar_tensor_tensor(out=zw[:, K], in0=zex[:, K], scalar=1.0 / R,
                                       in1=zrec[:, K].unsqueeze(2).to_broadcast([P, nk, NE]),
                                       op0=ALU.mult, op1=ALU.mult).then_inc(v.sem, 1)
                dve.wait_ge(v.sem, v.at(n, i + 5))
                V.tensor_tensor(zg[:, K].rearrange("p k (e r) -> p (k e) r", r=R),
                                zc[:, K, 0:NL].rearrange("p k (e r) -> p k e r", r=R),
                                zw[:, K].unsqueeze(3).to_broadcast([P, nk, NE, R]),
                                ALU.mult).then_inc(v.sem, 1)
                dve.wait_ge(v.sem, v.at(n, i + 6))
                V.tensor_copy(zs[:, K, 0:NL], zg[:, K])
                V.tensor_copy(zs[:, K, 64:64 + NL], zg[:, K]).then_inc(v.sem, 1)
                dve.wait_ge(v.sem, v.at(n, i + 7))
                V.tensor_tensor(zs[:, K, 32:32 + NL], zg[:, K], zs[:, K, 0:NL].bitcast(F32),
                                ALU.subtract).then_inc(v.sem, 1)

            def residual(d, u):
                for j in range(2):
                    dve.wait_ge(wo_ps.sem, wo_ps.at(d, j + 1))
                    if j == 0:
                        dve.wait_ge(xb_ready.sem, xb_ready.at(d))
                    V.scalar_tensor_tensor(out=x1[:, u, 2 * j:2 * j + 2, :],
                                           in0=psX[:, j, :].rearrange("p (k e) -> p k e", k=2),
                                           scalar=gate[:, 0:1], in1=x1[:, u, 2 * j:2 * j + 2, :],
                                           op0=ALU.mult, op1=ALU.add).then_inc(x1_s.sem, 1)

            def xT_split(c):
                dve.wait_ge(xT_ps.sem, xT_ps.at(c))
                V.tensor_copy(xT_hi[:, 1, :], psF[:, 1, :]).then_inc(xT_hi_v.sem, 1)
                for f, hi_s in enumerate((xT_hi_a, xT_hi_v)):
                    dve.wait_ge(hi_s.sem, hi_s.at(c))
                    V.tensor_tensor(xT_lo[:, f, :], psF[:, f, :], xT_hi[:, f, :].bitcast(F32),
                                    ALU.subtract).then_inc(xT_lo_s.sem, 1)

            def x2T_low(d):
                for f in range(FT):
                    dve.wait_ge(x2T_hi_s.sem, x2T_hi_s.at(d, f + 1))
                    V.tensor_tensor(xT_lo[:, f, :], psX[:, 2 + f, :], xT_hi[:, f, :].bitcast(F32),
                                    ALU.subtract).then_inc(x2T_lo_s.sem, 1)

            def q_bias(c):
                for j in range(2):
                    dve.wait_ge(q_ps.sem, q_ps.at(c, j + 1))
                    V.tensor_tensor(q_ev[:, 2 * j:2 * j + 2, :], psX[:, j, :].rearrange("p (k e) -> p k e", k=2),
                                    bq_b.unsqueeze(1).to_broadcast([P, 2, E]), ALU.add).then_inc(q_evac.sem, 1)

            def q_sine(c, u):
                dve.wait_ge(q_evac.sem, q_evac.at(c))
                for k in range(TT):
                    V.tensor_tensor(q_rs[:, k, :].rearrange("p (h s d) -> p h s d", s=2, d=D // 2),
                                    q_ev[:, k, :].rearrange("p (h s d) -> p h s d", s=2, d=D // 2)[:, :, ::-1, :],
                                    sin_q[:, u, k, :].rearrange("p (s d) -> p s d", s=2).unsqueeze(1)
                                    .to_broadcast([P, H, 2, D // 2]), ALU.mult).then_inc(q_sin.sem, 1)

            def q_sum(c):
                dve.wait_ge(q_cos.sem, q_cos.at(c))
                dve.wait_ge(q_sin.sem, q_sin.at(c))
                V.tensor_tensor(q_rc, q_rc, q_rs, ALU.add).then_inc(q_rot.sem, 1)

            def values_bias(b):
                dve.wait_ge(v_ps.sem, v_ps.at(b))
                V.tensor_tensor(v_sb[:, :, 0:D], psF[:, 2, 0:E].rearrange("p (h d) -> p h d", d=D),
                                bv_b.rearrange("p (h d) -> p h d", d=D), ALU.add).then_inc(v_evac.sem, 1)
                for j in range(4):
                    q = slice(32 * j, 32 * j + SR)
                    V.tensor_tensor(vr_sb[q, :, 32 * j:32 * j + D],
                                    psF[q, 2, E:2 * E].rearrange("p (g j d) -> p g j d", j=4, d=D)[:, :, j, :],
                                    bv_b[q, :].rearrange("p (g j d) -> p g j d", j=4, d=D)[:, :, j, :],
                                    ALU.add).then_inc(v_evac.sem, 1)

            def q_low(c):
                dve.wait_ge(q_hi.sem, q_hi.at(c))
                V.tensor_tensor(qs[:, :, :, 32:64].rearrange("p k g r -> p (k g) r"),
                                q_rc.rearrange("p k (g r) -> p (k g) r", r=32),
                                qs[:, :, :, 0:32].rearrange("p k g r -> p (k g) r").bitcast(F32),
                                ALU.subtract).then_inc(q_lo.sem, 1)

            def rotate_keys(b):
                dve.wait_ge(k_ps.sem, k_ps.at(b))
                V.tensor_tensor(k_ev[:, 0, :], psF[:, 2, 0:E], bk_b, ALU.add).then_inc(k_evac.sem, 1)
                V.tensor_tensor(k_ev[0:SR, 1, :], psF[0:SR, 2, E:2 * E], bk_b[0:SR, :], ALU.add).then_inc(k_evac.sem, 1)
                dve.wait_ge(k_evac.sem, k_evac.at(b))
                V.tensor_tensor(k_rc.rearrange("p a (h d) -> p a h d", d=D), k_ev.rearrange("p a (h d) -> p a h d", d=D),
                                cos_k.unsqueeze(2).to_broadcast([P, 2, H, D]), ALU.mult).then_inc(k_rot.sem, 1)
                for a in range(2):
                    V.tensor_tensor(k_rs[:, a, :].rearrange("p (h s d) -> p h s d", s=2, d=D // 2),
                                    k_ev[:, a, :].rearrange("p (h s d) -> p h s d", s=2, d=D // 2)[:, :, ::-1, :],
                                    sin_k[:, a, :].rearrange("p (s d) -> p s d", s=2).unsqueeze(1)
                                    .to_broadcast([P, H, 2, D // 2]), ALU.mult).then_inc(k_rot.sem, 1)
                dve.wait_ge(k_rot.sem, k_rot.at(b, 3))
                V.tensor_tensor(k_rc, k_rc, k_rs, ALU.add).then_inc(k_rot.sem, 1)
                dve.wait_ge(k_rot.sem, k_rot.at(b, 4))
                kf = k_rc.rearrange("p a (g r) -> p (a g) r", r=32)
                kd = ks[:, :, :, :].rearrange("p a g r -> p (a g) r")
                V.tensor_copy(kd[:, :, 0:64].rearrange("p a (t r) -> p a t r", t=2),
                              kf.unsqueeze(2).to_broadcast([P, 2 * NG, 2, 32])).then_inc(k_split.sem, 1)
                dve.wait_ge(k_split.sem, k_split.at(b, 1))
                V.tensor_tensor(kd[:, :, 64:96], kf, kd[:, :, 0:32].bitcast(F32), ALU.subtract).then_inc(k_split.sem, 1)

            def key_operands(b):
                dve.wait_ge(km_ps.sem, km_ps.at(b, 1))
                for hh in range(2):
                    V.tensor_scalar(km[:, 0:4, hh, 0:P], psX[0:KA, 2, :].rearrange("p (g s) -> p g s", g=4),
                                    mask[0:KA, hh:hh + 1], None, ALU.mult).then_inc(km_v.sem, 1)
                dve.wait_ge(km_a.sem, km_a.at(b))
                rest = psO[0:KA, 0:NG * 32].rearrange("p (g s) -> p g s", g=NG)[:, :, 0:SR]
                for hh in range(2):
                    V.tensor_scalar(km[:, :, hh, P:S], rest, mask[0:KA, hh:hh + 1], None, ALU.mult).then_inc(km_v.sem, 1)

            def q_transposed(c, g):
                dve.wait_ge(qT_ps.sem, qT_ps.at(c, g + 1))
                V.tensor_copy(qT[0:KS, g, :], psX[0:KS, g % 4, :]).then_inc(qT_v.sem, 1)

            def h_low(d, m):
                dve.wait_ge(w1_hi_s.sem, w1_hi_s.at(d, m + 1))
                V.scalar_tensor_tensor(out=h_lo[:, m, :], in0=psF[:, (m + 1) % 3, :], scalar=0.0,
                                       in1=h_hi[:, m, :].bitcast(F32), op0=ALU.max,
                                       op1=ALU.subtract).then_inc(w1_lo_s.sem, 1)

            def reduce_max(c, i):
                half, k, j = i // 8, i % 8 // 2, i % 2
                dve.wait_ge(max_ps.sem, max_ps.at(c, i + 1))
                V.tensor_reduce(max_t[:, k, half, :].rearrange("p (h g) -> p g h", h=2)[:, 2 * j:2 * j + 2, :],
                                psX[:, 2 * j:2 * j + 2, 0:2 * S].rearrange("p g (h s) -> p g h s", h=2),
                                AX.X, ALU.max).then_inc(max_red.sem, 1)

            def copy_z2(d, k):
                dve.wait_ge(w2_ps.sem, w2_ps.at(d, k + 1))
                V.tensor_copy(zc[:, k, 0:ZC], psF[:, F_OF_K[k], E:W2N]).then_inc(g2_c.sem, 1)

            def gates2(d, pr):
                dve.wait_ge(g2_c.sem, g2_c.at(d, 2 * pr + 2))
                K = slice(2 * pr, 2 * pr + 2)
                gates_shift(g2_v, d, 8 * pr, K)
                gates_weigh(g2_v, g2_e, d, 8 * pr, K, g2_e.at(d, pr + 1))

            def finish(d, u, k):
                dve.wait_ge(y_ps.sem, y_ps.at(d, k + 1))
                V.scalar_tensor_tensor(out=x1[:, u, k, :], in0=psF[:, F_OF_K[k], 0:E], scalar=gate[:, 1:2],
                                       in1=x1[:, u, k, :], op0=ALU.mult, op1=ALU.add).then_inc(y_out.sem, 1)

            def head_blocks(c, g):
                dve.wait_ge(pv_ps.sem, pv_ps.at(c, g + 1))
                V.transpose(heads_t[:, g, :, :].rearrange("p c r -> p (c r)"), pv_bank(g)).then_inc(pv_t.sem, 1)

            def head_norm(c, f2):
                G2 = slice(2 * f2, 2 * f2 + 2)
                hv = heads_t[:, G2, :, :].rearrange("p g c r -> p (g c) r")
                dve.wait_ge(pv_t.sem, pv_t.at(c, 2 * f2 + 2))
                V.reciprocal(den[:, G2, :].rearrange("p g c -> p (g c)"), hv[:, :, DSEL]).then_inc(den_inv.sem, 1)
                dve.wait_ge(den_inv.sem, den_inv.at(c, f2 + 1))
                V.tensor_tensor(hv[:, :, 0:D], hv[:, :, 0:D],
                                den[:, G2, :].rearrange("p g c -> p (g c)").unsqueeze(2).to_broadcast([P, 32, D]),
                                ALU.mult).then_inc(o_norm.sem, 1)

            def head_back(c, f2):
                G2 = slice(2 * f2, 2 * f2 + 2)
                hv = heads_t[:, G2, :, :].rearrange("p g c r -> p (g c) r")
                nv = ns[:, G2, :, :].rearrange("p g c r -> p (g c) r")
                dve.wait_ge(o_hi.sem, o_hi.at(c, f2 + 1))
                V.tensor_tensor(nv[:, :, D:32], hv[:, :, 0:D], nv[:, :, 0:D].bitcast(F32),
                                ALU.subtract).then_inc(o_lo.sem, 1)
                dve.wait_ge(o_lo.sem, o_lo.at(c, f2 + 1))
                V.transpose(heads_t[:, G2, :, :].rearrange("p g c r -> p g (c r)"),
                            ns[:, G2, :, :].rearrange("p g c r -> p g (c r)").bitcast(F32)).then_inc(o_back.sem, 1)

            def gates1_shift(d):
                dve.wait_ge(z1_ps.sem, z1_ps.at(d))
                V.transpose(zc[:, :, :].rearrange("p k z -> p (k z)"), psF[:, 1, 0:P]).then_inc(g1_v.sem, 1)
                dve.wait_ge(g1_v.sem, g1_v.at(d, 1))
                gates_shift(g1_v, d, 1, slice(0, TT))

            def gates1_weigh(d):
                gates_weigh(g1_v, g1_e, d, 1, slice(0, TT), g1_e.at(d))

            def ln2_stats(d, u):
                dve.wait_ge(x1_s.sem, x1_s.at(d))
                statistics(1, x1[:, u], d, ln2_stat, ln2_agg)

            def step(b, u, first=False, second=False, last=False):
                c = 2 * b + u
                d, e = c - 1, c - 2
                full = not first and not second
                if first:
                    q_bias(c)
                else:
                    head_blocks(d, 3)
                    head_norm(d, 1)
                    head_back(d, 1)
                if first:
                    rotate_keys(b)
                q_sine(c, u)
                q_sum(c)
                if u == 0:
                    values_bias(b)
                    key_operands(b)
                if full:
                    copy_z2(e, 0)
                    copy_z2(e, 1)
                    gates2(e, 0)
                if not first:
                    residual(d, 1 - u)
                    ln2_stats(d, 1 - u)
                if full:
                    finish(e, u, 0)
                    finish(e, u, 1)
                q_low(c)
                if full:
                    copy_z2(e, 2)
                if not last and not first:
                    ln1_stats(c + 1)
                if full:
                    copy_z2(e, 3)
                    gates2(e, 1)
                if not first:
                    x2T_low(d)
                q_transposed(c, 1)
                if not first:
                    gates1_shift(d)
                q_transposed(c, 3)
                if not first:
                    gates1_weigh(d)
                if full:
                    finish(e, u, 2)
                q_transposed(c, 5)
                if full:
                    finish(e, u, 3)
                q_transposed(c, 7)
                for i in range(16):
                    reduce_max(c, i)
                    if first and i == 5:
                        ln1_stats(c + 1)
                    if not first:
                        if i % 2:
                            h_low(d, i // 2)
                dve.wait_ge(maxT_ps.sem, maxT_ps.at(c))
                V.tensor_scalar(max_f[:, 1, :], psO[0:H // 2, :], -1.0, None, ALU.mult).then_inc(maxT_s[1].sem, 1)
                if not last:
                    xT_split(c + 1)
                if first:
                    dve.wait_ge(w_lo["w2a"].sem, 1)
                head_blocks(c, 0)
                head_blocks(c, 1)
                head_norm(c, 0)
                if u == 1 and not last:
                    rotate_keys(b + 1)
                head_blocks(c, 2)
                head_back(c, 0)
                if not last:
                    q_bias(c + 1)

            dve.wait_ge(const_p.sem, 5)
            V.tensor_copy(ident_r[:, :], ident_0).then_inc(const_v.sem, 1)
            ln1_stats(0)
            V.memset(ks[:, :, :, KS:KA].bitcast(F32), 1.0).then_inc(const_v.sem, 1)
            V.memset(kr[:, :, :].bitcast(F32), 0.0).then_inc(const_v.sem, 1)
            V.memset(v_sb[:, :, :], 0.0).then_inc(const_v.sem, 1)
            V.memset(vr_sb[:, :, :], 0.0).then_inc(const_v.sem, 1)
            dve.wait_ge(w_hi["wq"].sem, 1)
            V.tensor_tensor(**low_args("wq")).then_inc(w_lo["wq"].sem, 1)
            xT_split(0)
            dve.wait_ge(const_v.sem, 5)
            V.memset(v_sb[:, :, DSEL:DSEL + 1], 1.0)
            for j in range(4):
                ins = V.memset(vr_sb[32 * j:32 * j + SR, :, 32 * j + DSEL:32 * j + DSEL + 1], 1.0)
            ins.then_inc(const_v.sem, 1)
            dve.wait_ge(gate_ready.sem, 1)
            V.tensor_scalar(bo_b, bo_b, gate[:, 0:1], None, ALU.mult).then_inc(gbo_ready.sem, 1)
            step(0, 0, first=True)
            step(0, 1, second=True)
            with dve.Fori(1, B - 1) as b:
                step(b, 0)
                step(b, 1)
            step(B - 1, 0)
            step(B - 1, 1, last=True)
            d, e = LAST, LAST - 1
            head_blocks(d, 3)
            head_norm(d, 1)
            head_back(d, 1)
            copy_z2(e, 0)
            copy_z2(e, 1)
            gates2(e, 0)
            residual(d, 1)
            ln2_stats(d, 1)
            copy_z2(e, 2)
            finish(e, 0, 0)
            finish(e, 0, 1)
            copy_z2(e, 3)
            gates2(e, 1)
            x2T_low(d)
            finish(e, 0, 2)
            finish(e, 0, 3)
            gates1_shift(d)
            gates1_weigh(d)
            for m in range(HT):
                h_low(d, m)
            copy_z2(d, 0)
            copy_z2(d, 1)
            gates2(d, 0)
            copy_z2(d, 2)
            finish(d, 1, 0)
            finish(d, 1, 1)
            copy_z2(d, 3)
            gates2(d, 1)
            finish(d, 1, 2)
            finish(d, 1, 3)

        @block.tensor
        def _(pe):
            mm = nc.tensor.matmul
            ident = ident_r[:, :].bitcast(F32)

            def tokens(k):
                return slice(P * k, P * k + P)

            def transpose_x(c, banks, src_s, ps):
                pe.wait_ge(src_s.sem, src_s.at(c))
                for f in range(FT):
                    for k in range(TT):
                        ins = nc.tensor.transpose(banks[:, f, tokens(k)], xn[:, k, P * f:P * f + P], ident)
                    ins.then_inc(ps.sem, 1)

            def ctx_transposed(b, src):
                pe.wait_ge(ctx_loaded.sem, ctx_loaded.at(b))
                if src is ctx_sb:
                    pe.wait_ge(w1_lo_s.sem, w1_lo_s.at(2 * b - 2))
                for f in range(FT):
                    nc.tensor.transpose(psF[:, 2, S * f:S * f + P], src[:, 0, P * f:P * f + P], ident)
                    ins = nc.tensor.transpose(psF[:, 2, S * f + P:S * f + S], src[0:SR, 1, P * f:P * f + P],
                                              ident[0:SR, 0:SR])
                ins.then_inc(ctxT_ps.sem, 1)

            def project_q(c, first):
                pe.wait_ge(xT_hi_a.sem, xT_hi_a.at(c))
                pe.wait_ge(xT_hi_v.sem, xT_hi_v.at(c))
                pe.wait_ge(xT_lo_s.sem, xT_lo_s.at(c))
                if first:
                    pe.wait_ge(w_lo["wq"].sem, 1)
                for k in range(TT):
                    o_ps = psX[:, k // 2, E * (k % 2):E * (k % 2) + E]
                    n = 0
                    for a, w in ((xT_hi, wq_hi), (xT_lo, wq_hi), (xT_hi, wq_lo)):
                        for f in range(FT):
                            ins = mm(o_ps, a[:, f, tokens(k)], w[:, f, :], start=n == 0, stop=n == 5)
                            n += 1
                    if k % 2:
                        ins.then_inc(q_ps.sem, 1)

            def project_out(d, c, second):
                if c is not None:
                    pe.wait_ge(q_evac.sem, q_evac.at(c))
                if second:
                    pe.wait_ge(w_lo["wo"].sem, 1)
                pe.wait_ge(oT_s.sem, oT_s.at(d))
                for k in range(TT):
                    o_ps = psX[:, k // 2, E * (k % 2):E * (k % 2) + E]
                    n = 0
                    for w in (wo_hi, wo_lo):
                        for g in range(NQ):
                            ins = mm(o_ps, oT[:, g, tokens(k)], w[:, g, :], start=n == 0, stop=n == 7)
                            n += 1
                    if k % 2:
                        ins.then_inc(wo_ps.sem, 1)

            def project_k(b):
                pe.wait_ge(ctxT_s.sem, ctxT_s.at(b))
                for o, n, rows in ((0, P, slice(0, P)), (E, SR, slice(P, S))):
                    for f in range(FT):
                        ins = mm(psF[0:n, 2, o:o + E], ctxT[:, f, rows], wkv_sb[:, f, 0:E], start=f == 0, stop=f == FT - 1)
                ins.then_inc(k_ps.sem, 1)

            def project_v(b):
                pe.wait_ge(k_evac.sem, k_evac.at(b))
                for f in range(FT):
                    mm(psF[:, 2, 0:E], ctxT[:, f, 0:P], wkv_sb[:, f, E:2 * E], start=f == 0, stop=f == FT - 1)
                for f in range(FT):
                    for j in range(4):
                        ins = mm(psF[32 * j:32 * j + SR, 2, E:2 * E], ctxT[:, f, P:S], wkv_sb[:, f, E:2 * E],
                                 start=f == 0, stop=f == FT - 1)
                ins.then_inc(v_ps.sem, 1)

            def router1(d, second=False):
                if not second:
                    pe.wait_ge(y_out.sem, y_out.at(d - 1, 2))
                pe.wait_ge(x2T_hi_s.sem, x2T_hi_s.at(d))
                pe.wait_ge(x2T_lo_s.sem, x2T_lo_s.at(d))
                if second:
                    pe.wait_ge(a1_loaded.sem, 16)
                    for n in ("w1", "w2a", "w2b", "lora1", "lora2"):
                        pe.wait_ge(w_lo[n].sem, 1)
                    pe.wait_ge(pv_t.sem, pv_t.at(d))
                n = 0
                for a in (xT_hi, xT_lo):
                    for f in range(FT):
                        for k in range(TT):
                            ins = mm(psF[32 * k:32 * k + 32, 1, 0:P], a1_sb[:, f, :], a[:, f, tokens(k)].bitcast(F32),
                                     start=n == 0, stop=n == 3)
                        n += 1
                ins.then_inc(z1_ps.sem, 1)

            def lora1_operand(d):
                pe.wait_ge(g1_v.sem, g1_v.at(d))
                o_ps = psO[0:LR, :].rearrange("r (j k p) -> r k j p", j=4, k=TT)
                for k in range(TT):
                    ins = nc.tensor.transpose(o_ps[:, k].bitcast(F32R), zs[:, k, :], ident_r[:, :])
                ins.then_inc(z1T_ps.sem, 1)

            def hidden_main(d, m, second=False, parts=(0, 1)):
                if parts[0] == 0:
                    if m >= 3:
                        pe.wait_ge(w1_lo_s.sem, w1_lo_s.at(d, m - 2))
                    elif m == 0:
                        pe.wait_ge(g1_v.sem, g1_v.at(d, 1))
                    elif not second:
                        pe.wait_ge(y_out.sem, y_out.at(d - 1, m + 2))
                ops = [(a, w, f) for a, w in ((xT_hi, w1_hi), (xT_lo, w1_hi), (xT_hi, w1_lo)) for f in range(FT)]
                for n in range(3 * parts[0], 3 * parts[-1] + 3):
                    a, w, f = ops[n]
                    mm(psF[:, (m + 1) % 3, :], w[:, f, P * m:P * m + P], a[:, f, :], start=n == 0, stop=False)

            def hidden_lora(d, m):
                if m == 0:
                    pe.wait_ge(z1T_s.sem, z1T_s.at(d))
                mm(psF[:, (m + 1) % 3, :], lora_sb[:, P * m:P * m + P], zT[:, :], start=False, stop=True).then_inc(w1_ps.sem, 1)

            def key_transposes(b):
                pe.wait_ge(k_split.sem, k_split.at(b))
                for g in range(NG):
                    ins = nc.tensor.transpose(psX[0:KA, 2 + g // 4, tokens(g % 4)].bitcast(F32R), ks[:, 0, g, :], ident_r[:, :])
                    if g % 4 == 3:
                        ins.then_inc(km_ps.sem, 1)
                for g in range(NG):
                    ins = nc.tensor.transpose(psO[0:KA, 32 * g:32 * g + SR].bitcast(F32R), ks[0:SR, 1, g, :],
                                              ident_r[0:SR, 0:SR])
                ins.then_inc(km_ps.sem, 1)

            def q_transposes(c, g, first):
                if g == 0:
                    pe.wait_ge(q_lo.sem, q_lo.at(c))
                    pe.wait_ge(q_hi2.sem, q_hi2.at(c))
                elif g == 2 and not first:
                    pe.wait_ge(x2T_hi_s.sem, x2T_hi_s.at(c - 1))
                    pe.wait_ge(x2T_lo_s.sem, x2T_lo_s.at(c - 1))
                elif g >= 4 and g % 2 == 0:
                    pe.wait_ge(qT_a.sem, qT_a.at(c, g // 2 - 1))
                elif g >= 4:
                    pe.wait_ge(qT_v.sem, qT_v.at(c, g // 2 - 1))
                for k in range(TT):
                    ins = nc.tensor.transpose(psX[0:KS, g % 4, tokens(k)].bitcast(F32R), qs[:, k, g, :], ident_r[:, :])
                ins.then_inc(qT_ps.sem, 1)

            def max_scores(c, i):
                half, k, j = i // 8, i % 8 // 2, i % 2
                if i < 2:
                    n = 3 if i == 0 else 4
                    pe.wait_ge(qT_a.sem, qT_a.at(c, n))
                    pe.wait_ge(qT_v.sem, qT_v.at(c, n))
                else:
                    pe.wait_ge(max_red.sem, max_red.at(c, i - 1))
                for g in range(4 * half + 2 * j, 4 * half + 2 * j + 2):
                    ins = mm(psX[:, g % 4, 0:2 * S], qT[0:KS, g, tokens(k)],
                             km[0:KS, g, :, :].rearrange("p h s -> p (h s)"), start=True, stop=True)
                ins.then_inc(max_ps.sem, 1)

            def out_tile(d, k, m0=0, m1=HT):
                if k == 0:
                    pe.wait_ge(w1_hi_s.sem, w1_hi_s.at(d))
                    pe.wait_ge(w1_lo_s.sem, w1_lo_s.at(d))
                if k == 3:
                    pe.wait_ge(y_out.sem, y_out.at(d, 1))
                for m in range(m0, m1):
                    for i, (a, w) in enumerate(((h_hi, w2_hi), (h_lo, w2_hi), (h_hi, w2_lo))):
                        ins = mm(psF[:, F_OF_K[k], 0:W2N], a[:, m, tokens(k)], w[:, m, :],
                                 start=m == 0 and i == 0, stop=m == HT - 1 and i == 2)
                if m1 == HT:
                    ins.then_inc(w2_ps.sem, 1)

            def lora2_operand(d, pr):
                pe.wait_ge(g2_v.sem, g2_v.at(d, 8 * pr + 8))
                if pr == 1:
                    pe.wait_ge(z2T_s.sem, z2T_s.at(d, 1))
                for j in range(2):
                    ins = nc.tensor.transpose(psO[0:LR, tokens(j)].bitcast(F32R), zs[:, 2 * pr + j, :], ident_r[:, :])
                ins.then_inc(z2T_ps.sem, 1)

            def out_lora(d, pr):
                pe.wait_ge(z2T_s.sem, z2T_s.at(d, pr + 1))
                for k in (2 * pr, 2 * pr + 1):
                    mm(psF[:, F_OF_K[k], 0:E], zT[:, tokens(k)], lora_sb[:, HID:HID + E], start=False, stop=True,
                       skip_group_check=True).then_inc(y_ps.sem, 1)

            def max_transposed(c, half, first):
                pe.wait_ge(max_red.sem, max_red.at(c, 8 * half + 8))
                if half:
                    pe.wait_ge(maxT_s[0].sem, maxT_s[0].at(c))
                elif not first:
                    pe.wait_ge(z1T_s.sem, z1T_s.at(c - 1))
                for k in range(TT):
                    ins = nc.tensor.transpose(psO[0:H // 2, tokens(k)].bitcast(F32R), max_t[:, k, half, :], ident_r[:, :])
                ins.then_inc(maxT_ps.sem, 1)

            def scores(c, i):
                if i < 2:
                    pe.wait_ge(max_red.sem, max_red.at(c, 15 + i))
                else:
                    pe.wait_ge(sc_exp.sem, sc_exp.at(c, i - 1))
                if i % 5 == 0:
                    pe.wait_ge(max_rows[i // 5].sem, max_rows[i // 5].at(c))
                kind, n = SCORE_STEPS[i]
                for j in range(2):
                    o_ps = psX[:, 2 * (i % 2) + j, :]
                    if kind == "rest":
                        g = 2 * (n + j)
                        mm(o_ps, kr[:, g, :], qT[:, g, :], start=True, stop=False)
                        ins = mm(o_ps, kr[:, g + 1, :], qT[:, g + 1, :], start=False, stop=True)
                    else:
                        ins = mm(o_ps, km[:, n // 2, j, 0:P], qT[:, n // 2, :], start=True, stop=True)
                ins.then_inc(sc_ps.sem, 1)

            def values(c, g, first, last):
                pe.wait_ge(sc_exp.sem, sc_exp.at(c, PV_AFTER[g]))
                if g == 0:
                    pe.wait_ge(maxT_s[1].sem, maxT_s[1].at(c))
                    if first:
                        pe.wait_ge(const_v.sem, 6)
                if g == 2:
                    pe.wait_ge(pv_t.sem, pv_t.at(c, 1))
                if g % 2 and not last:
                    pe.wait_ge(xT_lo_s.sem, xT_lo_s.at(c + 1, g // 2 + 1))
                mm(pv_bank(g), vr_sb[:, g, :], probs_r[:, g, :], start=True, stop=False)
                for j in range(4):
                    h = 4 * g + j
                    ins = mm(pv_bank(g)[32 * j:32 * j + 32, :], v_sb[:, h, :], probs[:, h % 8, :], start=False, stop=True)
                ins.then_inc(pv_ps.sem, 1)

            def step(b, u, first=False, second=False, last=False):
                c = 2 * b + u
                d, e = c - 1, c - 2
                full = not first and not second
                if first:
                    project_q(c, first)
                    pe.wait_ge(wkv_loaded.sem, 16)
                    project_k(b)
                if u == 0:
                    if not first:
                        pe.wait_ge(pv_t.sem, pv_t.at(d, 3))
                    key_transposes(b)
                    project_v(b)
                if full:
                    pe.wait_ge(pv_t.sem, pv_t.at(d, 3))
                    out_tile(e, 0)
                    pe.wait_ge(pv_t.sem, pv_t.at(d))
                    out_tile(e, 1)
                if not first:
                    project_out(d, c, second)
                if u == 0:
                    pe.wait_ge(v_evac.sem, v_evac.at(b))
                    pe.wait_ge(km_v.sem, km_v.at(b))
                    pe.wait_ge(km_a.sem, km_a.at(b))
                if full:
                    lora2_operand(e, 0)
                    out_tile(e, 2, 0, HT // 2)
                    out_lora(e, 0)
                    out_tile(e, 2, HT // 2, HT)
                    out_tile(e, 3)
                if not first:
                    transpose_x(d, psX[:, 2:4, :], ln2_out, x2T_ps)
                    pe.wait_ge(x1_s.sem, x1_s.at(d))
                else:
                    pe.wait_ge(q_evac.sem, q_evac.at(c))
                for g in range(2):
                    q_transposes(c, g, first)
                if full:
                    lora2_operand(e, 1)
                if not first:
                    router1(d, second)
                if full:
                    out_lora(e, 1)
                for g in range(2, NG):
                    q_transposes(c, g, first)
                    if not first and g in (3, 5):
                        hidden_main(d, 0, second, (g // 2 - 1,))
                if not first:
                    lora1_operand(d)
                for i in range(16):
                    max_scores(c, i)
                    if i == 9:
                        max_transposed(c, 0, first)
                    if not first and i < 13:
                        m = i // 2 + 1
                        hidden_main(d, m, second, (i % 2,))
                        if i == 0:
                            hidden_lora(d, 0)
                        if i % 2:
                            hidden_lora(d, m)
                if not first:
                    hidden_main(d, 7, parts=(1,))
                    hidden_lora(d, 7)
                for i in range(10):
                    scores(c, i)
                    if i == 0:
                        max_transposed(c, 1, first)
                    if i == 1 and not last:
                        if not first:
                            pe.wait_ge(w1_lo_s.sem, w1_lo_s.at(d, 7))
                        transpose_x(c + 1, psF, ln1_out, xT_ps)
                    if i == 3 and u == 1 and not last:
                        ctx_transposed(b + 1, ctx_sb)
                    if i == 6 and u == 1 and not last:
                        project_k(b + 1)
                    if i in PV_SLOT:
                        values(c, PV_SLOT[i], first, last)
                if not last:
                    pe.wait_ge(sc_exp.sem, sc_exp.at(c, 9))
                    project_q(c + 1, False)
                values(c, 3, first, last)

            pe.wait_ge(const_v.sem, 1)
            transpose_x(0, psF, ln1_out, xT_ps)
            ctx_transposed(0, ctx_0)
            step(0, 0, first=True)
            step(0, 1, second=True)
            with pe.Fori(1, B - 1) as b:
                step(b, 0)
                step(b, 1)
            step(B - 1, 0)
            step(B - 1, 1, last=True)
            d, e = LAST, LAST - 1
            pe.wait_ge(pv_t.sem, pv_t.at(d, 3))
            out_tile(e, 0)
            pe.wait_ge(pv_t.sem, pv_t.at(d))
            out_tile(e, 1)
            project_out(d, None, False)
            lora2_operand(e, 0)
            out_tile(e, 2)
            out_lora(e, 0)
            out_tile(e, 3)
            transpose_x(d, psX[:, 2:4, :], ln2_out, x2T_ps)
            lora2_operand(e, 1)
            router1(d)
            out_lora(e, 1)
            hidden_main(d, 0)
            hidden_main(d, 1)
            lora1_operand(d)
            hidden_lora(d, 0)
            hidden_lora(d, 1)
            for m in range(2, HT):
                hidden_main(d, m)
                hidden_lora(d, m)
            for k in range(TT):
                out_tile(d, k)
                if k == 2:
                    lora2_operand(d, 0)
                    out_lora(d, 0)
            lora2_operand(d, 1)
            out_lora(d, 1)


SCORE_STEPS = [("rest", 0), ("main", 0), ("main", 2), ("main", 4), ("main", 6),
               ("rest", 2), ("main", 8), ("main", 10), ("main", 12), ("main", 14)]
PV_AFTER = [3, 5, 8, 10]
PV_SLOT = {3: 0, 5: 1, 8: 2}
LAST = B * UB - 1
F_OF_K = [0, 1, 2, 0]


def position_tables():
    f = np.float32
    base = (np.arange(0, D, 2, dtype=f) + f(0.4 * D)) / f(1.4 * D)
    inv = (f(1.0) / f(10000.0) ** (np.arange(D // 2, dtype=f) / f(D // 2))).astype(f)

    def cs(pos, down):
        pos = pos.astype(f)
        scale = (base[None, :] ** (pos[:, None] / f(E))).astype(f)
        if down:
            scale = (f(1.0) / scale).astype(f)
        ang = pos[:, None] * inv[None, :]
        c, s = np.cos(ang).astype(f) * scale, np.sin(ang).astype(f) * scale
        return np.concatenate([c, c], 1), np.concatenate([-s, s], 1)

    u, p, k = np.meshgrid(np.arange(UB), np.arange(P), np.arange(TT), indexing="ij")
    pos = (CH * u + TT * p + k).transpose(1, 0, 2).reshape(-1)
    cq, sq = (t.reshape(P, -1) * f(D ** -0.5) for t in cs(pos, False))
    pos = (np.arange(P)[:, None] + P * np.arange(2)[None, :]).reshape(-1)
    ck, sk = (t.reshape(P, -1) for t in cs(pos, True))
    r = np.arange(P)
    head = np.where(r < KS, (r % 32) // D, r - KS)
    mask = np.stack([(head == 0), (head == 1)], 1).astype(f)
    return np.concatenate([cq, sq, ck, sk], 1).astype(f), mask


def kernel(**inputs):
    import numpy as _np
    import concourse.bacc as _bacc
    from concourse.bass_utils import run_bass_kernel_spmd as _run

    i = {n: _np.asarray(a) for n, a in inputs.items()}
    perm = _np.arange(E).reshape(H, D // 2, 2).transpose(0, 2, 1).reshape(-1)
    wq = i["L0_xattn_Wq"].T[:, perm].reshape(FT, P, E).transpose(1, 0, 2).reshape(P, -1)
    wkv = _np.concatenate([i["L0_xattn_Wk"].T[:, perm], i["L0_xattn_Wv"].T], 1)
    wo = i["L0_xattn_Wo"].T.reshape(NQ, 4, 1, D, E)
    wo = _np.broadcast_to(wo, (NQ, 4, 2, D, E)).reshape(NQ, P, E).transpose(1, 0, 2).reshape(P, -1)
    w1 = i["L0_ffn_W1"].reshape(FT, P, HID).transpose(1, 0, 2).reshape(P, -1)

    def lora_router(a, r):
        n = a.shape[1]
        return _np.concatenate([a.transpose(1, 0, 2).reshape(n, NL), r, _np.zeros((n, 1), r.dtype)], 1)

    a1 = lora_router(i["L0_ffn_A1"], i["L0_ffn_R1"])
    a1 = _np.concatenate([a1, _np.zeros((E, 32 - ZC), a1.dtype)], 1).reshape(FT, P, 32).transpose(1, 0, 2).reshape(P, -1)
    w2 = _np.concatenate([i["L0_ffn_W2"], lora_router(i["L0_ffn_A2"], i["L0_ffn_R2"])], 1)
    w2 = w2.reshape(HT, P, W2N).transpose(1, 0, 2).reshape(P, -1)
    lora = _np.zeros((LR, HID + E), _np.float32)
    lo = _np.concatenate([i["L0_ffn_B1"].reshape(NL, HID), i["L0_ffn_B2"].reshape(NL, E)], 1)
    bias = _np.concatenate([i["L0_ffn_b1"], i["L0_ffn_b2"]])
    for r in (0, 32, 64):
        lora[r:r + NL] = lo
    for r in (0, 64):
        lora[r + NL] = bias
    pos, mask = position_tables()
    rows = _np.concatenate([i["L0_xattn_bq"][perm], i["L0_xattn_bk"][perm], i["L0_xattn_bv"], i["L0_xattn_bo"],
                            i["g_xattn"], i["g_ffn"]])
    tables = _np.concatenate([pos, _np.broadcast_to(rows, (P, rows.size)), mask], 1)

    arrays = {"x": i["x"], "ctx": i["ctx_1024"], "wq": wq, "wkv": wkv, "wo": wo, "w1": w1, "w2": w2, "a1": a1,
              "lora": lora, "tables": tables}
    arrays = {f"in_{n}_dram": _np.ascontiguousarray(a) for n, a in arrays.items()}
    nc = _bacc.Bacc("TRN2", target_bir_lowering=False, num_devices=1)
    args = [nc.dram_tensor(n, a.shape, mybir.dt.from_np(a.dtype), kind="ExternalInput").ap()
            for n, a in arrays.items()]
    args.append(nc.dram_tensor("out_0_dram", (B, T, E), F32, kind="ExternalOutput").ap())
    build(nc, *args)
    r = _run(nc, [arrays], core_ids=[0])
    return r.results[0]["out_0_dram"]
```
